# Optimizing a Trainium2 kernel written in Bass

```python
import numpy as np
import jax
import jax.numpy as jnp

def _softmax(x, axis=-1):
    return jax.nn.softmax(x, axis=axis)

def _gelu(x):
    return jax.nn.gelu(x, approximate=True)

def _silu(x):
    return jax.nn.silu(x)

def _sigmoid(x):
    return jax.nn.sigmoid(x)

def _layernorm(x, axis=-1, eps=1e-05):
    m = jnp.mean(x, axis=axis, keepdims=True)
    v = jnp.var(x, axis=axis, keepdims=True)
    return (x - m) / jnp.sqrt(v + eps)

def _scatter_add(tgt, idx, src, axis=0):
    return tgt.at[idx].add(src)

def _segment_sum(src, seg, n):
    return jax.ops.segment_sum(src, seg, n)
kernel_name = 'mk_gnn_preln_d2_gnn_r8_2edf58'

def setup_inputs(seed: int=0):
    np.random.seed(seed)
    _w = jnp.asarray

    def _rec_inputs():
        import jax
        import jax.numpy as jnp
        _gk = jax.random.key(seed)
        x = -0.0005121 + 1.001 * jax.random.normal(jax.random.fold_in(_gk, 1), (12500, 32), jnp.float32)
        src = jax.random.randint(jax.random.fold_in(_gk, 2), (400000,), 0, 12500, jnp.int32)
        dst = jnp.minimum((12500 * jax.random.uniform(jax.random.fold_in(_gk, 3), (400000,)) ** 2.0).astype(jnp.int32), 99999)
        _o = jnp.argsort(dst, stable=True)
        src = src[_o]
        dst = dst[_o]
        edge_attr_3 = 0.000844983 + 0.999762 * jax.random.normal(jax.random.fold_in(_gk, 11), (400000, 3), jnp.float32)
        edge_weight = jax.random.uniform(jax.random.fold_in(_gk, 13), (400000,), jnp.float32, 0.0, 1)
        return (x, src, dst, edge_attr_3, edge_weight)
    x, src, dst, edge_attr_3, edge_weight = _rec_inputs()

    def _L0_gnn_setup():
        import jax, jax.numpy as jnp
        import numpy as np
        N_NODES = 12500
        N_EDGES = 400000
        D_IN = 32
        N_HEADS = 4
        D_HEAD = 8
        key = jax.random.key(seed)
        k1, k2, k3, k4, k5, k6, k7 = jax.random.split(key, 7)
        scale = 1.0 / np.sqrt(D_IN)
        x = jax.random.normal(k1, (N_NODES, D_IN), dtype=jnp.float32)
        Wq = jax.random.normal(k2, (D_IN, N_HEADS * D_HEAD), dtype=jnp.float32) * scale
        Wk = jax.random.normal(k3, (D_IN, N_HEADS * D_HEAD), dtype=jnp.float32) * scale
        Wv = jax.random.normal(k4, (D_IN, N_HEADS * D_HEAD), dtype=jnp.float32) * scale
        Wo = jax.random.normal(k5, (N_HEADS * D_HEAD, D_IN), dtype=jnp.float32) * scale
        src = jax.random.randint(k6, (N_EDGES,), 0, N_NODES)
        dst = jax.random.randint(k7, (N_EDGES,), 0, N_NODES)
        edge_index = jnp.stack([src, dst], axis=0).astype(jnp.int64)
        return {'x': x, 'Wq': Wq, 'Wk': Wk, 'Wv': Wv, 'Wo': Wo, 'edge_index': edge_index}
    _L0_gnn_all = _L0_gnn_setup()
    _L0_gnn_in = {k: v for k, v in _L0_gnn_all.items() if k in ('Wq', 'Wk', 'Wv', 'Wo')}
    del _L0_gnn_all

    def _L1_gnn_setup():
        import jax, jax.numpy as jnp
        import numpy as np
        from math import factorial, pi, sqrt
        MUL = 8
        RS = [(MUL, 0), (MUL, 1)]
        N_NODES = 2500
        N_EDGES = 80000
        FEAT_DIM = sum((m * (2 * l + 1) for m, l in RS))
        R_DIM = sum((mo * mi * (2 * min(lo, li) + 1) for mo, lo in RS for mi, li in RS))
        HIDDEN = 64

        def _cg(j1, j2, j3, m1, m2, m3):
            if m1 + m2 != m3:
                return 0.0
            f = factorial
            pre = sqrt((2 * j3 + 1) * f(j3 + j1 - j2) * f(j3 - j1 + j2) * f(j1 + j2 - j3) / f(j1 + j2 + j3 + 1))
            pre *= sqrt(f(j3 + m3) * f(j3 - m3) * f(j1 - m1) * f(j1 + m1) * f(j2 - m2) * f(j2 + m2))
            kmin = max(0, j2 - j3 - m1, j1 - j3 + m2)
            kmax = min(j1 + j2 - j3, j1 - m1, j2 + m2)
            s = 0.0
            for k in range(kmin, kmax + 1):
                s += (-1) ** k / (f(k) * f(j1 + j2 - j3 - k) * f(j1 - m1 - k) * f(j2 + m2 - k) * f(j3 - j2 + m1 + k) * f(j3 - j1 - m2 + k))
            return pre * s

        def _w3j_complex(l1, l2, l3):
            w = np.zeros((2 * l1 + 1, 2 * l2 + 1, 2 * l3 + 1))
            for m1 in range(-l1, l1 + 1):
                for m2 in range(-l2, l2 + 1):
                    m3 = -(m1 + m2)
                    if abs(m3) <= l3:
                        w[m1 + l1, m2 + l2, m3 + l3] = (-1) ** (l1 - l2 - m3) / sqrt(2 * l3 + 1) * _cg(l1, l2, l3, m1, m2, -m3)
            return w

        def _A(l):
            A = np.zeros((2 * l + 1, 2 * l + 1), dtype=complex)
            A[l, l] = 1.0
            for m in range(1, l + 1):
                A[l + m, l + m] = (-1) ** m / sqrt(2)
                A[l + m, l - m] = 1.0 / sqrt(2)
                A[l - m, l - m] = 1j / sqrt(2)
                A[l - m, l + m] = -1j * (-1) ** m / sqrt(2)
            return A

        def real_w3j(l1, l2, l3):
            wc = _w3j_complex(l1, l2, l3).astype(complex)
            wr = np.einsum('abc,ma,nb,oc->mno', wc, _A(l1).conj(), _A(l2).conj(), _A(l3).conj())
            i = int(np.argmax(np.abs(wr)))
            ph = wr.flat[i] / abs(wr.flat[i])
            wr = wr / ph
            assert np.abs(wr.imag).max() < 1e-10
            return np.real(wr).astype(np.float32)
        _W3J = {}
        for _mo, _lo in RS:
            for _mi, _li in RS:
                for _lf in range(abs(_lo - _li), _lo + _li + 1):
                    if (_lo, _lf, _li) not in _W3J:
                        _W3J[_lo, _lf, _li] = jnp.asarray(real_w3j(_lo, _lf, _li))
        _NORM = []
        for _mo, _lo in RS:
            _num = sum((mi * (2 * min(_lo, li) + 1) for mi, li in RS))
            _NORM.append(sqrt(4.0 * pi) * sqrt(2.0 * _lo + 1.0) / sqrt(_num))
        _F_OFFS = [0] + list(np.cumsum([mi * (2 * li + 1) for mi, li in RS]))

        def spherical_harmonics(rel_vec):
            r = rel_vec / jnp.linalg.norm(rel_vec, axis=-1, keepdims=True)
            x, y, z = (r[:, 0], r[:, 1], r[:, 2])
            y0 = jnp.full_like(x, 0.5 / sqrt(pi))[:, None]
            c1 = sqrt(3.0 / (4.0 * pi))
            y1 = c1 * jnp.stack([y, z, x], axis=-1)
            c2a = 0.5 * sqrt(15.0 / pi)
            c2b = 0.25 * sqrt(5.0 / pi)
            c2c = 0.25 * sqrt(15.0 / pi)
            y2 = jnp.stack([c2a * x * y, c2a * y * z, c2b * (3.0 * z * z - 1.0), c2a * x * z, c2c * (x * x - y * y)], axis=-1)
            return jnp.concatenate([y0, y1, y2], axis=-1)
        key = jax.random.key(seed)
        ks = jax.random.split(key, 6)
        features = jax.random.normal(ks[0], (N_NODES, FEAT_DIM), dtype=jnp.float32)
        abs_distances = jax.random.uniform(ks[1], (N_EDGES,), dtype=jnp.float32, minval=0.1, maxval=1.0)
        rel_vec = jax.random.normal(ks[2], (N_EDGES, 3), dtype=jnp.float32)
        edge_index = jax.random.randint(ks[3], (2, N_EDGES), 0, N_NODES, dtype=jnp.int32)
        w1 = jax.random.normal(ks[4], (1, HIDDEN), dtype=jnp.float32)
        b1 = jnp.zeros((HIDDEN,), jnp.float32)
        w2 = jax.random.normal(ks[5], (HIDDEN, R_DIM), dtype=jnp.float32) / sqrt(HIDDEN)
        b2 = jnp.zeros((R_DIM,), jnp.float32)
        return {'features': features, 'abs_distances': abs_distances, 'rel_vec': rel_vec, 'edge_index': edge_index, 'w1': w1, 'b1': b1, 'w2': w2, 'b2': b2}
    _L1_gnn_all = _L1_gnn_setup()
    _L1_gnn_in = {k: v for k, v in _L1_gnn_all.items() if k in ('w1', 'b1', 'w2', 'b2')}
    del _L1_gnn_all
    return {'x': x, 'src': src, 'dst': dst, 'edge_attr_3': edge_attr_3, 'edge_weight': edge_weight, 'L0_gnn_Wq': _L0_gnn_in['Wq'], 'L0_gnn_Wk': _L0_gnn_in['Wk'], 'L0_gnn_Wv': _L0_gnn_in['Wv'], 'L0_gnn_Wo': _L0_gnn_in['Wo'], 'L1_gnn_w1': _L1_gnn_in['w1'], 'L1_gnn_b1': _L1_gnn_in['b1'], 'L1_gnn_w2': _L1_gnn_in['w2'], 'L1_gnn_b2': _L1_gnn_in['b2']}

def reference(x, src, dst, edge_attr_3, edge_weight, L0_gnn_Wq, L0_gnn_Wk, L0_gnn_Wv, L0_gnn_Wo, L1_gnn_w1, L1_gnn_b1, L1_gnn_w2, L1_gnn_b2):
    import jax
    import jax.numpy as jnp

    def _L0_gnn_ref(x, Wq, Wk, Wv, Wo, edge_index):
        import jax, jax.numpy as jnp
        import numpy as np
        N_NODES = 12500
        N_EDGES = 400000
        D_IN = 32
        N_HEADS = 4
        D_HEAD = 8
        N = x.shape[0]
        src, dst = (edge_index[0], edge_index[1])
        q = (x @ Wq).reshape(N, N_HEADS, D_HEAD)
        k = (x @ Wk).reshape(N, N_HEADS, D_HEAD)
        v = (x @ Wv).reshape(N, N_HEADS, D_HEAD)
        inv_sqrt_d = jnp.asarray(1.0 / np.sqrt(D_HEAD), dtype=x.dtype)
        scores = jnp.einsum('ehd,ehd->eh', q[dst], k[src]) * inv_sqrt_d
        m = jax.ops.segment_max(scores, dst, num_segments=N)
        m = jnp.where(jnp.isfinite(m), m, jnp.zeros_like(m))
        e = jnp.exp(scores - m[dst])
        denom = jax.ops.segment_sum(e, dst, num_segments=N)
        msg = jax.ops.segment_sum(e[:, :, None] * v[src], dst, num_segments=N)
        attn_out = msg / jnp.maximum(denom, 1e-16)[:, :, None]
        out = attn_out.reshape(N, N_HEADS * D_HEAD) @ Wo
        return x + out

    def _L1_gnn_ref(features, abs_distances, rel_vec, edge_index, w1, b1, w2, b2):
        import jax, jax.numpy as jnp
        import numpy as np
        from math import factorial, pi, sqrt
        MUL = 8
        RS = [(MUL, 0), (MUL, 1)]
        N_NODES = 2500
        N_EDGES = 80000
        FEAT_DIM = sum((m * (2 * l + 1) for m, l in RS))
        R_DIM = sum((mo * mi * (2 * min(lo, li) + 1) for mo, lo in RS for mi, li in RS))
        HIDDEN = 64

        def _cg(j1, j2, j3, m1, m2, m3):
            if m1 + m2 != m3:
                return 0.0
            f = factorial
            pre = sqrt((2 * j3 + 1) * f(j3 + j1 - j2) * f(j3 - j1 + j2) * f(j1 + j2 - j3) / f(j1 + j2 + j3 + 1))
            pre *= sqrt(f(j3 + m3) * f(j3 - m3) * f(j1 - m1) * f(j1 + m1) * f(j2 - m2) * f(j2 + m2))
            kmin = max(0, j2 - j3 - m1, j1 - j3 + m2)
            kmax = min(j1 + j2 - j3, j1 - m1, j2 + m2)
            s = 0.0
            for k in range(kmin, kmax + 1):
                s += (-1) ** k / (f(k) * f(j1 + j2 - j3 - k) * f(j1 - m1 - k) * f(j2 + m2 - k) * f(j3 - j2 + m1 + k) * f(j3 - j1 - m2 + k))
            return pre * s

        def _w3j_complex(l1, l2, l3):
            w = np.zeros((2 * l1 + 1, 2 * l2 + 1, 2 * l3 + 1))
            for m1 in range(-l1, l1 + 1):
                for m2 in range(-l2, l2 + 1):
                    m3 = -(m1 + m2)
                    if abs(m3) <= l3:
                        w[m1 + l1, m2 + l2, m3 + l3] = (-1) ** (l1 - l2 - m3) / sqrt(2 * l3 + 1) * _cg(l1, l2, l3, m1, m2, -m3)
            return w

        def _A(l):
            A = np.zeros((2 * l + 1, 2 * l + 1), dtype=complex)
            A[l, l] = 1.0
            for m in range(1, l + 1):
                A[l + m, l + m] = (-1) ** m / sqrt(2)
                A[l + m, l - m] = 1.0 / sqrt(2)
                A[l - m, l - m] = 1j / sqrt(2)
                A[l - m, l + m] = -1j * (-1) ** m / sqrt(2)
            return A

        def real_w3j(l1, l2, l3):
            wc = _w3j_complex(l1, l2, l3).astype(complex)
            wr = np.einsum('abc,ma,nb,oc->mno', wc, _A(l1).conj(), _A(l2).conj(), _A(l3).conj())
            i = int(np.argmax(np.abs(wr)))
            ph = wr.flat[i] / abs(wr.flat[i])
            wr = wr / ph
            assert np.abs(wr.imag).max() < 1e-10
            return np.real(wr).astype(np.float32)
        _W3J = {}
        for _mo, _lo in RS:
            for _mi, _li in RS:
                for _lf in range(abs(_lo - _li), _lo + _li + 1):
                    if (_lo, _lf, _li) not in _W3J:
                        _W3J[_lo, _lf, _li] = jnp.asarray(real_w3j(_lo, _lf, _li))
        _NORM = []
        for _mo, _lo in RS:
            _num = sum((mi * (2 * min(_lo, li) + 1) for mi, li in RS))
            _NORM.append(sqrt(4.0 * pi) * sqrt(2.0 * _lo + 1.0) / sqrt(_num))
        _F_OFFS = [0] + list(np.cumsum([mi * (2 * li + 1) for mi, li in RS]))

        def spherical_harmonics(rel_vec):
            r = rel_vec / jnp.linalg.norm(rel_vec, axis=-1, keepdims=True)
            x, y, z = (r[:, 0], r[:, 1], r[:, 2])
            y0 = jnp.full_like(x, 0.5 / sqrt(pi))[:, None]
            c1 = sqrt(3.0 / (4.0 * pi))
            y1 = c1 * jnp.stack([y, z, x], axis=-1)
            c2a = 0.5 * sqrt(15.0 / pi)
            c2b = 0.25 * sqrt(5.0 / pi)
            c2c = 0.25 * sqrt(15.0 / pi)
            y2 = jnp.stack([c2a * x * y, c2a * y * z, c2b * (3.0 * z * z - 1.0), c2a * x * z, c2c * (x * x - y * y)], axis=-1)
            return jnp.concatenate([y0, y1, y2], axis=-1)
        src, dst = (edge_index[0], edge_index[1])
        R = jax.nn.relu(abs_distances[:, None] @ w1 + b1) @ w2 + b2
        Y = spherical_harmonics(rel_vec)
        Fj = features[src]
        E = Fj.shape[0]
        msg_blocks = []
        r_off = 0
        for i, (mo, lo) in enumerate(RS):
            acc = jnp.zeros((E, mo, 2 * lo + 1), dtype=features.dtype)
            for j, (mi, li) in enumerate(RS):
                n_lf = 2 * min(lo, li) + 1
                sz = mo * mi * n_lf
                Rb = R[:, r_off:r_off + sz].reshape(E, mo, mi, n_lf)
                r_off += sz
                Fb = Fj[:, _F_OFFS[j]:_F_OFFS[j + 1]].reshape(E, mi, 2 * li + 1)
                for k, lf in enumerate(range(abs(lo - li), lo + li + 1)):
                    C = _W3J[lo, lf, li]
                    Yf = Y[:, lf * lf:(lf + 1) * (lf + 1)]
                    acc = acc + _NORM[i] * jnp.einsum('euv,ef,evi,ofi->euo', Rb[..., k], Yf, Fb, C)
            msg_blocks.append(acc.reshape(E, -1))
        msg = jnp.concatenate(msg_blocks, axis=-1)
        out = jnp.zeros((features.shape[0], msg.shape[1]), dtype=features.dtype)
        out = out.at[dst].add(msg)
        return out
    edge_index = jnp.stack([src, dst])
    h = jnp.maximum(_layernorm(x, axis=-1), 0.0)
    x = x + _L0_gnn_ref(h, L0_gnn_Wq, L0_gnn_Wk, L0_gnn_Wv, L0_gnn_Wo, edge_index)
    h = jnp.maximum(_layernorm(x, axis=-1), 0.0)
    x = x + _L1_gnn_ref(h, edge_weight, edge_attr_3, edge_index, L1_gnn_w1, L1_gnn_b1, L1_gnn_w2, L1_gnn_b2)
    return x

_drawn_inputs = setup_inputs


def setup_inputs(seed=0):
    import zlib

    import numpy as np

    out = dict(_drawn_inputs(seed))
    spreads = {'L1_gnn_b1': (0.0, 0.1), 'L1_gnn_b2': (0.0, 0.1)}
    factors = {'L0_gnn_Wq': 3.253, 'L0_gnn_Wk': 3.443}
    for name, (base, spread) in spreads.items():
        noise = np.random.default_rng([zlib.crc32(name.encode()), seed]).standard_normal(out[name].shape)
        drawn = base * np.exp(spread * noise) if base else spread * noise
        out[name] = jnp.asarray(drawn.astype(out[name].dtype))
    for name, factor in factors.items():
        out[name] = (out[name] * factor).astype(out[name].dtype)
    return out
```

```python
from contextlib import ExitStack
from math import pi, sqrt

import concourse.bass as bass
from concourse import mybir

FP32 = mybir.dt.float32
BF16 = mybir.dt.bfloat16
I32 = mybir.dt.int32
U32 = mybir.dt.uint32
ALU = mybir.AluOpType
ACT = mybir.ActivationFunctionType
AX = mybir.AxisListType

P = 128
NODES, EDGES, D = 12500, 400000, 32
HEADS, DH = 4, 8
BLOCKS = 98
NODES_PAD = P * BLOCKS
GROUP = 4
BLOCKS_UP = 100
BATCH = 5
TURNS = BLOCKS_UP // (GROUP * BATCH)

T = 54
SLOTS = 3132
CHUNKS = SLOTS // T
PAIRS = CHUNKS // 2
EDGES_PAD = P * SLOTS
TRI = 3
HALF = T // 2
GPC = T // TRI

ROWW = 128
SP_, SC_ = 116, 27
BB = BLOCKS + 1
PARTS = 3

STATE = 40
HC = DH + 1
SUMS = HEADS * HC
HID = 64
VU = 8
JC = 16
COLS = 40
J_PE = 9
BIG = 1.0e30
FAR = float(1 << 22)

C0 = 0.5 / sqrt(pi)
C1 = sqrt(3.0 / (4.0 * pi))
C2 = sqrt(3.0 / (8.0 * pi))
N0 = sqrt(4.0 * pi) / sqrt(16.0)
N1 = sqrt(4.0 * pi) * sqrt(3.0) / sqrt(32.0)

assert CHUNKS * T == SLOTS and 2 * PAIRS == CHUNKS and GPC * TRI == T and SP_ * SC_ * ROWW == EDGES_PAD


def spread(ap, n):
    return ap.rearrange("p (a o) -> p a o", o=1).to_broadcast([ap.shape[0], ap.shape[1], n])


def spread_front(ap, n):
    return ap.rearrange("p (o a) -> p o a", o=1).to_broadcast([ap.shape[0], n, ap.shape[1]])


def chain(engine, done, base=0):
    count = [0]

    def step(instruction):
        count[0] += 1
        instruction.then_inc(done, 1)
        engine.wait_ge(done, base + count[0])
    step.count = count
    return step


def pairs(engine, body):
    with engine.Fori(0, PAIRS - 1) as i:
        body(i, False)
    body(PAIRS - 1, True)


def build_identity(pool, step, ident):
    step(pool.memset(ident[:, :], 0.0))
    step(pool.affine_select(out=ident[:, :], in_=ident[:, :], compare_op=ALU.not_equal, fill=1.0,
                            base=0, pattern=[[-1, P]], channel_multiplier=1))


def normalise(nc, vec, step, squares, x, h, mean, var, root_asked, root_done, asked):
    step(nc.vector.tensor_reduce(mean[:, :], x, axis=AX.X, op=ALU.add))
    step(nc.vector.tensor_scalar(mean[:, :], mean[:, :], 1.0 / D, None, ALU.mult))
    step(nc.vector.tensor_tensor(h, x, spread(mean[:, :], D), ALU.subtract))
    step(nc.vector.tensor_tensor(squares, h, h, ALU.mult))
    step(nc.vector.tensor_reduce(var[:, :], squares, axis=AX.X, op=ALU.add))
    step(nc.vector.tensor_scalar(var[:, :], var[:, :], 1.0 / D, 1e-5, ALU.mult, ALU.add))
    vec.sem_inc(root_asked, 1)
    vec.wait_ge(root_done, asked)
    step(nc.vector.reciprocal(var[:, :], var[:, :]))
    step(nc.vector.scalar_tensor_tensor(out=h, in0=h, scalar=0.0, in1=spread(var[:, :], D),
                                        op0=ALU.max, op1=ALU.mult))


def prologue(nc, a, k):
    with ExitStack() as ctx:
        sb = lambda name, shape, dt=FP32: ctx.enter_context(nc.sbuf_tensor(name, shape, dt))
        pb = lambda name, shape, dt=FP32: ctx.enter_context(nc.psum_tensor(name, shape, dt))
        sem = lambda name: ctx.enter_context(nc.semaphore(name))
        xs = sb("xs", [P, BLOCKS, D])
        hs = sb("hs", [P, BLOCKS_UP, D])
        scratch = sb("scratch", [P, BLOCKS, D])
        zeros = scratch
        mean, var = sb("mean", [P, BLOCKS]), sb("var", [P, BLOCKS])
        wqkv = sb("wqkv", [P, GROUP, 3 * D])
        stage = sb("stage", [P, BATCH, P])
        hT = sb("hT", [P, BATCH, P])
        kv = sb("kv", [P, BLOCKS_UP, 2 * D])
        q = sb("q", [P, BLOCKS_UP, D])
        samp_i, samp = sb("samp_i", [SP_, SC_], I32), sb("samp", [SP_, SC_])
        starts_i, starts = sb("starts_i", [SP_, P + 1], I32), sb("starts", [SP_, P + 1])
        lows_i, lows = sb("lows_i", [SP_, BB], I32), sb("lows", [SP_, BB])
        above = sb("above", [SP_, SC_, P + 1], BF16)
        here = sb("here", [SP_, SC_, P], BF16)
        less = sb("less", [SP_, SC_, BB], BF16)
        ones = sb("ones", [SP_, BB], BF16)
        part = sb("part", [SP_, SC_])
        nid_i, nid = sb("nid_i", [P, BB], I32), sb("nid", [P, BB])
        row, row_i = sb("row", [P, BB]), sb("row_i", [P, BB], I32)
        drow = sb("drow", [P, BB, ROWW], I32)
        below = sb("below", [P, BB // PARTS, ROWW])
        ptr = sb("ptr", [P, BB])
        some = sb("some", [P, BLOCKS])
        first_at, first_i = sb("first_at", [P, BLOCKS]), sb("first_i", [P, BLOCKS], I32)
        last_at = sb("last_at", [P, BLOCKS])
        pair = sb("pair", [P, BLOCKS, 2])
        mine_i, mine = sb("mine_i", [P, 1], I32), sb("mine", [P, 1])
        edge_i, last_dst, prev_dst = sb("edge_i", [P, 1], I32), sb("last_dst", [P, 1], I32), sb("prev_dst", [P, 1], I32)
        own = sb("own", [P, 2])
        cross = sb("cross", [P, 3])
        ident = k["ident"]
        psT = pb("psT", [P, 2, 512])
        psM = pb("psM", [P, BATCH, 512])
        psC = pb("psC", [P, 512])

        x_loaded, w_loaded, samp_loaded = sem("x_loaded"), sem("w_loaded"), sem("samp_loaded")
        wblk_cleared, zeros_set, q_filled = sem("wblk_cleared"), sem("zeros_set"), sem("q_filled")
        pool_done, vec_done, act_done = sem("pool_done"), sem("vec_done"), sem("act_done")
        consts_ready, root_asked, root_done = sem("consts_ready"), sem("root_asked"), sem("root_done")
        staged, turned, hT_ready, projected, q_out, kv_out = (sem(n) for n in (
            "staged", "turned", "hT_ready", "projected", "q_out", "kv_out"))
        onehots, counted, rows_asked, ends_loaded = (sem(n) for n in ("onehots", "counted", "rows_asked", "ends_loaded"))
        rows_here = [sem(f"rows_here{i}") for i in range(PARTS)]
        first_asked, q_spread, tables, ptr_out, table_asked = (sem(n) for n in (
            "first_asked", "q_spread", "tables", "ptr_out", "table_asked"))
        own_here, qfirst_here, lns = sem("own_here"), sem("qfirst_here"), sem("lns")
        hT_free = sem("hT_free")

        with nc.Block() as block:

            @block.sync
            def _(sp):
                sp.dma_start(samp_i[:, :], a["samples"]).then_inc(samp_loaded, 16)
                sp.dma_start(xs[:, :, :], a["x"].rearrange("(p b) c -> p b c", b=BLOCKS)).then_inc(x_loaded, 16)
                sp.wait_ge(wblk_cleared, 1)
                for j in range(GROUP):
                    for n, w in enumerate(("wq", "wk", "wv")):
                        sp.dma_start(wqkv[j * D:(j + 1) * D, j, n * D:(n + 1) * D], a[w]).then_inc(w_loaded, 16)
                dst = a["dst"].rearrange("(p s) -> p s", s=SLOTS)
                with nc.allow_non_contiguous_dma(reason="one word per partition"):
                    sp.dma_start(mine_i[:, :], dst[:, 0:1]).then_inc(ends_loaded, 16)
                    sp.dma_start(last_dst[:, :], dst[:, SLOTS - 1:SLOTS]).then_inc(ends_loaded, 16)
                    sp.dma_start(prev_dst[:, :], a["dst_ext"][0:EDGES_PAD].rearrange("(p s) -> p s", s=SLOTS)[:, 0:1]).then_inc(ends_loaded, 16)
                sp.wait_ge(q_out, TURNS)
                sp.wait_ge(kv_out, TURNS)
                sp.dma_start(a["kv"].rearrange("(p b) c -> p b c", b=BLOCKS), kv[:, 0:BLOCKS, :]).then_inc(tables, 16)
                sp.dma_start(a["q"].rearrange("(p b) c -> p b c", b=BLOCKS), q[:, 0:BLOCKS, :]).then_inc(tables, 16)
                sp.wait_ge(table_asked, 1)
                sp.dma_start(a["ptr"].rearrange("(p b) c -> p b c", b=BLOCKS), pair[:, :, :]).then_inc(ptr_out, 16)
                sp.wait_ge(tables, 32)
                sp.wait_ge(ptr_out, 16)

            @block.gpsimd
            def _(pool):
                step = chain(pool, pool_done)
                step(nc.gpsimd.memset(wqkv[:, :, :], 0.0))
                pool.sem_inc(wblk_cleared, 1)
                build_identity(nc.gpsimd, step, ident)
                nc.gpsimd.iota(starts_i[:, :], pattern=[[BLOCKS, P + 1]], base=0, channel_multiplier=0).then_inc(consts_ready, 1)
                nc.gpsimd.iota(lows_i[:, :], pattern=[[1, BB]], base=0, channel_multiplier=0).then_inc(consts_ready, 1)
                nc.gpsimd.iota(nid_i[:, :], pattern=[[1, BB]], base=0, channel_multiplier=BLOCKS).then_inc(consts_ready, 1)
                nc.gpsimd.iota(edge_i[:, :], pattern=[[0, 1]], base=0, channel_multiplier=SLOTS).then_inc(consts_ready, 1)
                nc.gpsimd.memset(ones[:, :], 1.0).then_inc(consts_ready, 1)
                pool.wait_ge(rows_asked, 1)
                for b in range(BB):
                    nc.gpsimd.indirect_dma_start(
                        drow[:, b, :], None, a["dst_rows"],
                        bass.IndirectOffsetOnAxis(ap=row_i[:, b:b + 1].bitcast(U32), axis=0),
                    ).then_inc(rows_here[b // (BB // PARTS)], 16)
                pool.wait_ge(first_asked, 1)
                pool.wait_ge(q_filled, 16 * D)
                pool.wait_ge(q_out, TURNS)
                for b in range(BLOCKS):
                    nc.gpsimd.indirect_dma_start(
                        a["qexp"], bass.IndirectOffsetOnAxis(ap=first_i[:, b:b + 1].bitcast(U32), axis=0),
                        q[:, b, :], None, bounds_check=EDGES_PAD - 1, oob_is_err=False).then_inc(q_spread, 16)
                pool.wait_ge(ends_loaded, 48)
                pool.wait_ge(ptr_out, 16)
                pool.wait_ge(tables, 32)
                mine_at = bass.IndirectOffsetOnAxis(ap=mine_i[:, :].bitcast(U32), axis=0)
                nc.gpsimd.indirect_dma_start(own[:, :], None, a["ptr"], mine_at).then_inc(own_here, 16)
                nc.gpsimd.indirect_dma_start(k["q_first"][:, :], None, a["q"], mine_at).then_inc(qfirst_here, 16)
                pool.wait_ge(q_spread, 16 * BLOCKS)
                pool.wait_ge(qfirst_here, 16)

            @block.scalar
            def _(act):
                step = chain(act, act_done)
                act.wait_ge(zeros_set, 1)
                rows = a["qexp"][0:EDGES_PAD, :].rearrange("(p s) c -> p (s c)", s=SLOTS)
                for j in range(D):
                    act.dma_start(rows[:, j * SLOTS:(j + 1) * SLOTS],
                                  zeros[:, :, :].rearrange("p b c -> p (b c)")[:, 0:SLOTS]).then_inc(q_filled, 16)
                act.wait_ge(root_asked, 1)
                nc.scalar.activation(var[:, :], var[:, :], ACT.Sqrt).then_inc(root_done, 1)
                with act.Fori(0, TURNS) as i:
                    act.wait_ge(turned, i + 1)
                    nc.scalar.activation(hT[:, :, :].rearrange("p g n -> p (g n)"),
                                         psT[:, :, :].rearrange("p a n -> p (a n)")[:, 0:BATCH * P],
                                         ACT.Copy).then_inc(hT_ready, 1)
                    act.wait_ge(projected, i + 1)
                    nc.scalar.activation(
                        q[:, bass.ds(i * (BATCH * GROUP), BATCH * GROUP), :].rearrange("p (g j) c -> p g j c", j=GROUP),
                        psM[:, :, 0:GROUP * 3 * D].rearrange("p g (j c) -> p g j c", j=GROUP)[:, :, :, 0:D],
                        ACT.Copy, scale=1.0 / sqrt(DH)).then_inc(q_out, 1)

            @block.tensor
            def _(pe):
                pe.wait_ge(onehots, 1)
                for s in range(SC_):
                    nc.tensor.matmul(psC[:, 0:BB], above[:, s, 0:P], ones[:, :], start=(s == 0), stop=False)
                    last = nc.tensor.matmul(psC[:, 0:BB], here[:, s, :], less[:, s, :], start=False, stop=(s == SC_ - 1))
                last.then_inc(counted, 1)
                pe.wait_ge(w_loaded, 16 * GROUP * 3)
                pe.wait_ge(pool_done, 3)
                with pe.Fori(0, TURNS) as i:
                    pe.wait_ge(staged, i + 1)
                    for g in range(BATCH):
                        last = nc.tensor.transpose(psT[:, (g * P) // 512, (g * P) % 512:(g * P) % 512 + P],
                                                   stage[:, g, :], ident[:, :])
                    last.then_inc(turned, 1)
                    pe.wait_ge(hT_ready, i + 1)
                    for g in range(BATCH):
                        last = nc.tensor.matmul(psM[:, g, 0:GROUP * 3 * D], hT[:, g, :],
                                                wqkv[:, :, :].rearrange("p j c -> p (j c)"), start=True, stop=True)
                    last.then_inc(projected, 1)

            @block.vector
            def _(vec):
                step = chain(vec, vec_done)
                v = nc.vector
                step(v.memset(zeros[:, :, :], 0.0))
                vec.sem_inc(zeros_set, 1)
                step(v.memset(hs[:, BLOCKS:BLOCKS_UP, :], 0.0))
                vec.wait_ge(samp_loaded, 16)
                vec.wait_ge(consts_ready, 5)
                step(v.tensor_copy(samp[:, :], samp_i[:, :]))
                step(v.tensor_copy(starts[:, :], starts_i[:, :]))
                step(v.tensor_copy(lows[:, :], lows_i[:, :]))
                step(v.tensor_copy(nid[:, :], nid_i[:, :]))
                step(v.tensor_tensor(above[:, :, :], spread_front(starts[:, :], SC_), spread(samp[:, :], P + 1), ALU.is_gt))
                step(v.tensor_reduce(part[:, :], above[:, :, :], axis=AX.X, op=ALU.add))
                step(v.tensor_tensor(here[:, :, :], above[:, :, 1:P + 1], above[:, :, 0:P], ALU.subtract))
                step(v.tensor_scalar(part[:, :], part[:, :], float(BLOCKS), -float(BLOCKS * P), ALU.mult, ALU.add))
                step(v.tensor_tensor(part[:, :], samp[:, :], part[:, :], ALU.add))
                step(v.tensor_tensor(less[:, :, :], spread_front(lows[:, :], SC_), spread(part[:, :], BB), ALU.is_gt))
                vec.sem_inc(onehots, 1)
                vec.wait_ge(counted, 1)
                step(v.tensor_scalar(row[:, :], psC[:, 0:BB], -1.0, 0.0, ALU.add, ALU.max))
                step(v.tensor_copy(row_i[:, :], row[:, :]))
                vec.sem_inc(rows_asked, 1)
                vec.wait_ge(x_loaded, 16)
                vec.wait_ge(q_filled, 16 * D)
                normalise(nc, vec, step, scratch[:, :, :], xs[:, :, :], hs[:, 0:BLOCKS, :], mean, var, root_asked, root_done, 1)
                step(v.tensor_tensor(k["res"][:, :, :], xs[:, :, :], hs[:, 0:BLOCKS, :], ALU.add))
                with vec.Fori(0, TURNS) as i:
                    v.tensor_copy(stage[:, :, :].rearrange("p g n -> p (g n)"),
                                  hs[:, bass.ds(i * (BATCH * GROUP), BATCH * GROUP), :].rearrange("p b c -> p (b c)")
                                  ).then_inc(staged, 1)
                    vec.wait_ge(q_out, i + 1)
                    v.tensor_copy(
                        kv[:, bass.ds(i * (BATCH * GROUP), BATCH * GROUP), :].rearrange("p (g j) c -> p g j c", j=GROUP),
                        psM[:, :, 0:GROUP * 3 * D].rearrange("p g (j c) -> p g j c", j=GROUP)[:, :, :, D:3 * D]
                    ).then_inc(kv_out, 1)
                    vec.wait_ge(kv_out, i + 1)
                w = BB // PARTS
                for g in range(PARTS):
                    vec.wait_ge(rows_here[g], 16 * w)
                    at = slice(g * w, (g + 1) * w)
                    step(v.tensor_tensor(below[:, :, :], drow[:, at, :], spread(nid[:, at], ROWW), ALU.is_lt))
                    step(v.tensor_reduce(ptr[:, at], below[:, :, :], axis=AX.X, op=ALU.add))
                step(v.scalar_tensor_tensor(out=ptr[:, :], in0=row[:, :], scalar=float(ROWW), in1=ptr[:, :], op0=ALU.mult, op1=ALU.add))
                lo, hi = ptr[:, 0:BLOCKS], ptr[:, 1:BB]
                step(v.tensor_tensor(some[:, :], hi, lo, ALU.is_gt))
                step(v.tensor_scalar(first_at[:, :], some[:, :], -FAR, FAR, ALU.mult, ALU.add))
                step(v.tensor_tensor(first_at[:, :], first_at[:, :], lo, ALU.add))
                step(v.tensor_copy(first_i[:, :], first_at[:, :]))
                vec.sem_inc(first_asked, 1)
                step(v.tensor_scalar(last_at[:, :], hi, -1.0 - EDGES_PAD, None, ALU.add))
                step(v.tensor_tensor(last_at[:, :], last_at[:, :], some[:, :], ALU.mult))
                step(v.tensor_scalar(last_at[:, :], last_at[:, :], float(EDGES_PAD), None, ALU.add))
                step(v.tensor_copy(k["last_i"][:, :], last_at[:, :]))
                step(v.tensor_copy(pair[:, :, 0], lo))
                step(v.tensor_copy(pair[:, :, 1], hi))
                vec.sem_inc(table_asked, 1)
                vec.wait_ge(ends_loaded, 48)
                step(v.tensor_tensor(k["whole"][:, :], last_dst[:, :], prev_dst[:, :], ALU.is_equal))
                vec.wait_ge(own_here, 16)
                step(v.tensor_copy(mine[:, :], edge_i[:, :]))
                step(v.tensor_scalar(cross[:, 2:3], own[:, 1:2], -1.0, None, ALU.add))
                step(v.tensor_copy(k["end_i"][:, :], cross[:, 2:3]))
                step(v.tensor_tensor(cross[:, 0:1], own[:, 0:1], mine[:, :], ALU.is_lt))
                step(v.tensor_scalar(mine[:, :], mine[:, :], float(SLOTS), None, ALU.add))
                step(v.tensor_tensor(cross[:, 1:2], cross[:, 2:3], mine[:, :], ALU.is_lt))
                step(v.tensor_tensor(cross[:, 0:1], cross[:, 0:1], cross[:, 1:2], ALU.mult))
                step(v.tensor_scalar(cross[:, 0:1], cross[:, 0:1], -FAR, FAR, ALU.mult, ALU.add))
                step(v.tensor_tensor(cross[:, 0:1], cross[:, 0:1], cross[:, 2:3], ALU.add))
                step(v.tensor_copy(k["patch_i"][:, :], cross[:, 0:1]))


def attention(nc, a, k):
    with ExitStack() as ctx:
        sb = lambda name, shape, dt=FP32: ctx.enter_context(nc.sbuf_tensor(name, shape, dt))
        sem = lambda name: ctx.enter_context(nc.semaphore(name))
        T1 = T + 1
        src_i = [sb(f"src_i{b}", [P, T], I32) for b in range(2)]
        kv = [sb(f"kv{b}", [P, T, 2 * D]) for b in range(2)]
        dst_i = [sb(f"dst_i{b}", [P, T1], I32) for b in range(2)]
        attr = [sb(f"attr{b}", [P, T, 3]) for b in range(2)]
        qin = [sb(f"qin{b}", [P, T, D]) for b in range(2)]
        same = sb("same", [P, T1])
        pen = sb("pen", [P, T1])
        same_c, pen_c = sb("same_c", [P, D, T1]), sb("pen_c", [P, HEADS, T1])
        qseed, qrun = sb("qseed", [P, D, T1]), sb("qrun", [P, D, T1])
        qk = sb("qk", [P, HEADS, T, DH])
        score = sb("score", [P, HEADS, T1])
        decay = sb("decay", [P, HEADS, T1])
        rel = sb("rel", [P, HEADS, T])
        decay_c = sb("decay_c", [P, SUMS, T1])
        ev, sums = sb("ev", [P, HEADS, HC, T1]), k["sums"]
        peak = k["peak"]
        out = [sb(f"out{b}", [P, T, STATE]) for b in range(2)]
        sq, rn = sb("sq", [P, T, 3]), sb("rn", [P, T])
        zrow = sb("zrow", [2, STATE])

        src_loaded, dst_loaded, attr_loaded, q_loaded, kv_here, stored = (
            [sem(f"{n}{b}") for b in range(2)] for n in ("src_loaded", "dst_loaded", "attr_loaded", "q_loaded", "kv_here", "stored"))
        kv_free, dst_free, attr_free, q_free = (sem(n) for n in ("kv_free", "dst_free", "attr_free", "q_free"))
        flags_ready, spread_ready, q_scanned, exps_asked, exps_ready = (sem(n) for n in (
            "flags_ready", "spread_ready", "q_scanned", "exps_asked", "exps_ready"))
        sums_ready, sums_copied, rn_asked, rn_ready = (sem(n) for n in ("sums_ready", "sums_copied", "rn_asked", "rn_ready"))
        vec_done, zrow_set, chunk_begun = sem("vec_done2"), sem("zrow_set"), sem("chunk_begun")
        edges = lambda name: a[name].rearrange("(p s) -> p s", s=SLOTS)

        with nc.Block() as block:

            @block.sync
            def _(sp):
                base = a["dst_ext"]
                before = base[0:EDGES_PAD].rearrange("(p s) -> p s", s=SLOTS)
                def load_src(b, at):
                    sp.dma_start(src_i[b][:, :], edges("src")[:, bass.ds(at, T)]).then_inc(src_loaded[b], 16)

                load_src(0, 0)
                load_src(1, T)

                def body(i, last):
                    for b in range(2):
                        at = i * (2 * T) + b * T
                        sp.wait_ge(dst_free, i * 2 + b + 1)
                        sp.dma_start(dst_i[b][:, 0:T], before[:, bass.ds(at, T)]).then_inc(dst_loaded[b], 16)
                        sp.dma_start(dst_i[b][:, T:T1], edges("dst")[:, bass.ds(at + (T - 1), 1)], allow_slow_non_contiguous=True).then_inc(dst_loaded[b], 16)
                        sp.wait_ge(attr_free, i * 2 + b + 1)
                        sp.dma_start(attr[b][:, :, :].rearrange("p t c -> p (t c)"),
                                     a["attr"].rearrange("(p s) c -> p (s c)", s=SLOTS)[:, bass.ds(at * 3, 3 * T)]).then_inc(attr_loaded[b], 16)
                        sp.wait_ge(q_free, i * 2 + b + 1)
                        sp.dma_start(qin[b][:, :, :].rearrange("p t c -> p (t c)"),
                                     a["qexp"].rearrange("(p s) c -> p (s c)", s=SLOTS)[:, bass.ds(at * D, D * T)]).then_inc(q_loaded[b], 16)
                        if not last:
                            sp.wait_ge(kv_here[b], i * (16 * T) + 16 * T)
                            load_src(b, i * (2 * T) + (b + 2) * T)
                pairs(sp, body)

            @block.gpsimd
            def _(pool):
                with pool.Fori(0, PAIRS) as i:
                    for b in range(2):
                        pool.wait_ge(src_loaded[b], i * 16 + 16)
                        pool.wait_ge(kv_free, i * 2 + b + 1)
                        pool.sem_inc(chunk_begun, 1)
                        for t in range(T):
                            nc.gpsimd.indirect_dma_start(
                                kv[b][:, t, :], None, a["kv"],
                                bass.IndirectOffsetOnAxis(ap=src_i[b][:, t:t + 1].bitcast(U32), axis=0)).then_inc(kv_here[b], 16)

            @block.scalar
            def _(act):
                act.wait_ge(zrow_set, 1)
                for b in range(2):
                    act.dma_start(a["state"][EDGES_PAD + b:EDGES_PAD + b + 1, :], zrow[b:b + 1, :]).then_inc(stored[b], 16)
                act.sem_inc(q_free, 2)
                with act.Fori(0, PAIRS) as i:
                    for b in range(2):
                        c1 = i * 2 + b + 1
                        act.wait_ge(rn_asked, c1)
                        nc.scalar.activation(rn[:, :], rn[:, :], ACT.Sqrt).then_inc(rn_ready, 1)
                        act.wait_ge(flags_ready, c1)
                        act.wait_ge(q_scanned, c1)
                        nc.scalar.activation(same_c[:, :, :], spread_front(same[:, :], D), ACT.Copy).then_inc(spread_ready, 1)
                        nc.scalar.activation(pen_c[:, :, :], spread_front(pen[:, :], HEADS), ACT.Copy).then_inc(spread_ready, 1)
                        act.wait_ge(q_loaded[b], i * 16 + 16)
                        nc.scalar.activation(qseed[:, :, 1:T1], qin[b][:, :, :].rearrange("p t c -> p c t"), ACT.Copy).then_inc(spread_ready, 1)
                        act.wait_ge(spread_ready, c1 * 3)
                        act.sem_inc(q_free, 1)
                        act.wait_ge(exps_asked, c1)
                        nc.scalar.activation(decay_c[:, :, :].rearrange("p (h c) t -> p h c t", c=HC),
                                             decay[:, :, :].rearrange("p h (o t) -> p h o t", o=1).to_broadcast([P, HEADS, HC, T1]),
                                             ACT.Exp).then_inc(exps_ready, 1)
                        nc.scalar.activation(ev[:, :, DH, 1:T1], rel[:, :, :], ACT.Exp).then_inc(exps_ready, 1)
                        act.wait_ge(sums_ready, c1)
                        act.wait_ge(stored[b], i * 16 + 16)
                        nc.scalar.activation(out[b][:, :, 0:SUMS], sums[:, :, 1:T1].rearrange("p c t -> p t c"), ACT.Copy).then_inc(sums_copied, 1)
                        nc.scalar.activation(out[b][:, :, SUMS:STATE], peak[:, :, 1:T1].rearrange("p c t -> p t c"), ACT.Copy).then_inc(sums_copied, 1)
                        act.wait_ge(sums_copied, c1 * 2 + 2)
                        act.dma_start(a["state"][0:EDGES_PAD, :].rearrange("(p s) c -> p (s c)", s=SLOTS)[:, bass.ds(i * (2 * T * STATE) + b * (T * STATE), T * STATE)],
                                      out[b][:, :, :].rearrange("p t c -> p (t c)")).then_inc(stored[b], 16)
                for b in range(2):
                    act.wait_ge(stored[b], 16 * (PAIRS + 1))

            @block.vector
            def _(vec):
                v = nc.vector
                step = chain(vec, vec_done)
                step(v.memset(zrow[:, :], 0.0))
                vec.sem_inc(zrow_set, 1)
                step(v.tensor_copy(qrun[:, :, T], k["q_first"][:, :]))
                step(v.memset(peak[:, :, T:T1], -BIG))
                step(v.memset(sums[:, :, T:T1], 0.0))
                step(v.memset(same[:, :], 0.0))
                step(v.memset(decay[:, :, :], -BIG))
                for primed, n in ((kv_free, 2), (dst_free, 2), (attr_free, 2), (q_scanned, 1), (sums_copied, 2)):
                    vec.sem_inc(primed, n)
                steps = 20
                base = step.count[0]
                with vec.Fori(0, PAIRS) as i:
                    step = chain(vec, vec_done, base + i * (2 * steps))
                    for b in range(2):
                        c1 = i * 2 + b + 1
                        at = i * (2 * T) + b * T
                        vec.wait_ge(attr_loaded[b], i * 16 + 16)
                        step(v.tensor_tensor(sq[:, :, :], attr[b][:, :, :], attr[b][:, :, :], ALU.mult))
                        step(v.tensor_reduce(rn[:, :], sq[:, :, :], axis=AX.X, op=ALU.add))
                        vec.sem_inc(rn_asked, 1)
                        vec.wait_ge(dst_loaded[b], i * 32 + 32)
                        step(v.tensor_tensor(same[:, 1:T1], dst_i[b][:, 1:T1], dst_i[b][:, 0:T], ALU.is_equal))
                        vec.sem_inc(dst_free, 1)
                        step(v.tensor_scalar(pen[:, :], same[:, :], BIG, -BIG, ALU.mult, ALU.add))
                        vec.sem_inc(flags_ready, 1)
                        step(v.tensor_copy(k["same"][:, bass.ds(at, T)], same[:, 1:T1]))
                        vec.wait_ge(rn_ready, c1)
                        step(v.reciprocal(rn[:, :], rn[:, :]))
                        step(v.tensor_tensor(k["unit"][:, bass.ds(at, T), 0:2], attr[b][:, :, 1:3], spread(rn[:, :], 2), ALU.mult))
                        step(v.tensor_tensor(k["unit"][:, bass.ds(at, T), 2], attr[b][:, :, 0], rn[:, :], ALU.mult))
                        vec.sem_inc(attr_free, 1)
                        step(v.tensor_copy(qseed[:, :, 0], qrun[:, :, T]))
                        vec.wait_ge(spread_ready, c1 * 3)
                        flat = lambda x: x[:, :, :].rearrange("p c t -> p (c t)")
                        step(v.tensor_tensor_scan(flat(qrun), flat(same_c), flat(qseed), 0.0, ALU.mult, ALU.add))
                        vec.wait_ge(kv_here[b], i * (16 * T) + 16 * T)
                        step(v.tensor_tensor(qk[:, :, :, :], qrun[:, :, 1:T1].rearrange("p (h d) t -> p h t d", d=DH),
                                             kv[b][:, :, 0:D].rearrange("p t (h d) -> p h t d", d=DH), ALU.mult))
                        step(v.tensor_reduce(score[:, :, 1:T1], qk[:, :, :, :], axis=AX.X, op=ALU.add))
                        step(v.tensor_copy(score[:, :, 0], peak[:, :, T]))
                        vec.wait_ge(sums_copied, c1 * 2)
                        step(v.tensor_tensor_scan(flat(peak), flat(pen_c), flat(score), -BIG, ALU.add, ALU.max))
                        step(v.tensor_tensor(decay[:, :, 1:T1], peak[:, :, 0:T], pen_c[:, :, 1:T1], ALU.add))
                        step(v.tensor_tensor(decay[:, :, 1:T1], decay[:, :, 1:T1], peak[:, :, 1:T1], ALU.subtract))
                        step(v.tensor_tensor(rel[:, :, :], score[:, :, 1:T1], peak[:, :, 1:T1], ALU.subtract))
                        vec.sem_inc(q_scanned, 1)
                        vec.sem_inc(exps_asked, 1)
                        vec.wait_ge(exps_ready, c1 * 2)
                        step(v.tensor_tensor(ev[:, :, 0:DH, 1:T1], kv[b][:, :, D:2 * D].rearrange("p t (h d) -> p h d t", d=DH),
                                             ev[:, :, DH:HC, 1:T1].to_broadcast([P, HEADS, DH, T]), ALU.mult))
                        vec.sem_inc(kv_free, 1)
                        step(v.tensor_copy(ev[:, :, :, 0], sums[:, :, T].rearrange("p (h c) -> p h c", c=HC)))
                        step(v.tensor_tensor_scan(flat(sums), flat(decay_c), ev[:, :, :, :].rearrange("p h c t -> p (h c t)"), 0.0, ALU.mult, ALU.add))
                        vec.sem_inc(sums_ready, 1)
                    assert step.count[0] == 2 * steps, step.count[0]
                vec.wait_ge(sums_copied, CHUNKS * 2 + 2)


def node_attention(nc, a, k):
    with ExitStack() as ctx:
        sb = lambda name, shape, dt=FP32: ctx.enter_context(nc.sbuf_tensor(name, shape, dt))
        pb = lambda name, shape, dt=FP32: ctx.enter_context(nc.psum_tensor(name, shape, dt))
        sem = lambda name: ctx.enter_context(nc.semaphore(name))
        per_turn = BATCH * GROUP
        blocks_of = lambda i: min(per_turn, BLOCKS - i * per_turn)
        tail = sb("tail", [P, 3, SUMS])
        rows = sb("rows", [SUMS, 3, P])
        peaks, totals = sb("peaks", [SUMS, P + 1]), sb("totals", [SUMS, P + 1])
        shrink, gain = sb("shrink", [SUMS, P]), sb("gain", [SUMS, P])
        carry = sb("carry", [P, 2, SUMS])
        patch = sb("patch", [P, STATE])
        top, ex = sb("top", [P, SUMS]), sb("ex", [P, 2, SUMS])
        mix = sb("mix", [P, 2, SUMS])
        state = sb("state", [P, BLOCKS, STATE])
        rden = sb("rden", [P, per_turn, HEADS])
        stage, hT = sb("stage3", [P, BATCH, P]), sb("hT3", [P, BATCH, P])
        wo = sb("wo", [P, GROUP, D])
        hs = sb("hs3", [P, BLOCKS, D])
        squares = sb("squares3", [P, per_turn, D])
        mean, var = sb("mean3", [P, per_turn]), sb("var3", [P, per_turn])
        ident = k["ident"]
        psA, psB = pb("psA", [P, 3, P]), pb("psB", [P, 2, SUMS])
        psT = pb("psT3", [P, 2, 512])
        psM = pb("psM3", [P, 2, 512])

        wo_loaded, wo_cleared, tail_ready, turned, rows_ready, ex_asked, ex_done, carry_ready, carry_back = (sem(n) for n in (
            "wo_loaded", "wo_cleared", "tail_ready", "turned3", "rows_ready", "ex_asked", "ex_done", "carry_ready", "carry_back"))
        patch_here, patch_ready, patched = sem("patch_here"), sem("patch_ready"), sem("patched")
        states_here = [sem(f"states_here{i}") for i in range(TURNS)]
        staged, stage_turned, hT_ready, projected, root_asked, root_done, h_ready, h_stored = (sem(n) for n in (
            "staged3", "stage_turned3", "hT_ready3", "projected3", "root_asked3", "root_done3", "h_ready3", "h_stored"))
        vec_done, pool_done = sem("vec_done3"), sem("pool_done3")

        with nc.Block() as block:

            @block.sync
            def _(sp):
                sp.wait_ge(wo_cleared, 1)
                for j in range(GROUP):
                    sp.dma_start(wo[j * D:(j + 1) * D, j, :], a["wo"]).then_inc(wo_loaded, 16)
                for i in range(TURNS):
                    sp.wait_ge(h_ready, i + 1)
                    b0 = i * per_turn
                    sp.dma_start(a["h2"].rearrange("(p b) c -> p b c", b=BLOCKS)[:, b0:b0 + blocks_of(i), :],
                                 hs[:, b0:b0 + blocks_of(i), :]).then_inc(h_stored, 16)
                sp.wait_ge(h_stored, 16 * TURNS)

            @block.gpsimd
            def _(pool):
                step = chain(pool, pool_done)
                step(nc.gpsimd.memset(wo[:, :, :], 0.0))
                pool.sem_inc(wo_cleared, 1)
                nc.gpsimd.indirect_dma_start(patch[:, :], None, a["state"], bass.IndirectOffsetOnAxis(
                    ap=k["end_i"][:, :].bitcast(U32), axis=0)).then_inc(patch_here, 16)
                pool.wait_ge(patch_ready, 1)
                nc.gpsimd.indirect_dma_start(a["state"], bass.IndirectOffsetOnAxis(
                    ap=k["patch_i"][:, :].bitcast(U32), axis=0), patch[:, :], None,
                    bounds_check=EDGES_PAD - 1, oob_is_err=False).then_inc(patched, 16)
                pool.wait_ge(patched, 16)
                for b in range(BLOCKS):
                    nc.gpsimd.indirect_dma_start(state[:, b, :], None, a["state"], bass.IndirectOffsetOnAxis(
                        ap=k["last_i"][:, b:b + 1].bitcast(U32), axis=0)).then_inc(states_here[b // per_turn], 16)

            @block.scalar
            def _(act):
                act.wait_ge(ex_asked, 1)
                nc.scalar.activation(shrink[:, :], shrink[:, :], ACT.Exp).then_inc(ex_done, 1)
                nc.scalar.activation(gain[:, :], gain[:, :], ACT.Exp).then_inc(ex_done, 1)
                act.wait_ge(ex_asked, 2)
                nc.scalar.activation(ex[:, :, :], ex[:, :, :], ACT.Exp).then_inc(ex_done, 1)
                for i in range(TURNS):
                    act.wait_ge(stage_turned, i + 1)
                    nc.scalar.activation(hT[:, :, :].rearrange("p g n -> p (g n)"),
                                         psT[:, :, :].rearrange("p a n -> p (a n)")[:, 0:BATCH * P],
                                         ACT.Copy).then_inc(hT_ready, 1)
                    act.wait_ge(root_asked, i + 1)
                    nc.scalar.activation(var[:, :], var[:, :], ACT.Sqrt).then_inc(root_done, 1)

            @block.tensor
            def _(pe):
                pe.wait_ge(tail_ready, 1)
                for n in range(3):
                    last = nc.tensor.transpose(psA[0:SUMS, n, :], tail[:, n, :], ident[:, :])
                last.then_inc(turned, 1)
                pe.wait_ge(carry_ready, 1)
                nc.tensor.transpose(psB[:, 0, :], peaks[:, 0:P], ident[0:SUMS, 0:SUMS])
                nc.tensor.transpose(psB[:, 1, :], totals[:, 0:P], ident[0:SUMS, 0:SUMS]).then_inc(carry_back, 1)
                pe.wait_ge(wo_loaded, 16 * GROUP)
                for i in range(TURNS):
                    pe.wait_ge(staged, i + 1)
                    for g in range(BATCH):
                        last = nc.tensor.transpose(psT[:, g // 4, (g % 4) * P:(g % 4 + 1) * P], stage[:, g, :], ident[:, :])
                    last.then_inc(stage_turned, 1)
                    pe.wait_ge(hT_ready, i + 1)
                    for g in range(BATCH):
                        last = nc.tensor.matmul(psM[:, g // 4, (g % 4) * P:(g % 4 + 1) * P], hT[:, g, :],
                                                wo[:, :, :].rearrange("p j c -> p (j c)"), start=True, stop=True)
                    last.then_inc(projected, 1)

            @block.vector
            def _(vec):
                v = nc.vector
                step = chain(vec, vec_done)
                step(v.tensor_copy(tail[:, 0, :].rearrange("p (h c) -> p h c", c=HC), spread(k["peak"][:, :, T], HC)))
                step(v.tensor_copy(tail[:, 1, :], k["sums"][:, :, T]))
                step(v.tensor_copy(tail[:, 2, :], k["whole"][:, :].to_broadcast([P, SUMS])))
                vec.sem_inc(tail_ready, 1)
                vec.wait_ge(turned, 1)
                step(v.tensor_copy(rows[:, :, :], psA[0:SUMS, :, :]))
                step(v.tensor_scalar(rows[:, 2, :], rows[:, 2, :], BIG, -BIG, ALU.mult, ALU.add))
                step(v.memset(peaks[:, 0:1], -BIG))
                step(v.memset(totals[:, 0:1], 0.0))
                step(v.tensor_tensor_scan(peaks[:, 1:P + 1], rows[:, 2, :], rows[:, 0, :], -BIG, ALU.add, ALU.max))
                step(v.tensor_tensor(shrink[:, :], peaks[:, 0:P], rows[:, 2, :], ALU.add))
                step(v.tensor_tensor(shrink[:, :], shrink[:, :], peaks[:, 1:P + 1], ALU.subtract))
                step(v.tensor_tensor(gain[:, :], rows[:, 0, :], peaks[:, 1:P + 1], ALU.subtract))
                vec.sem_inc(ex_asked, 1)
                vec.wait_ge(ex_done, 2)
                step(v.tensor_tensor(gain[:, :], gain[:, :], rows[:, 1, :], ALU.mult))
                step(v.tensor_tensor_scan(totals[:, 1:P + 1], shrink[:, :], gain[:, :], 0.0, ALU.mult, ALU.add))
                vec.sem_inc(carry_ready, 1)
                vec.wait_ge(carry_back, 1)
                step(v.tensor_copy(carry[:, :, :], psB[:, :, :]))
                vec.wait_ge(patch_here, 16)
                pk = spread(patch[:, SUMS:STATE], HC)
                byhead = lambda x: x.rearrange("p (h c) -> p h c", c=HC)
                step(v.tensor_tensor(byhead(top[:, :]), byhead(carry[:, 0, :]), pk, ALU.max))
                step(v.tensor_tensor(byhead(ex[:, 0, :]), pk, byhead(top[:, :]), ALU.subtract))
                step(v.tensor_tensor(ex[:, 1, :], carry[:, 0, :], top[:, :], ALU.subtract))
                vec.sem_inc(ex_asked, 1)
                vec.wait_ge(ex_done, 3)
                step(v.tensor_tensor(mix[:, 0, :], patch[:, 0:SUMS], ex[:, 0, :], ALU.mult))
                step(v.tensor_tensor(mix[:, 1, :], carry[:, 1, :], ex[:, 1, :], ALU.mult))
                step(v.tensor_tensor(patch[:, 0:SUMS], mix[:, 0, :], mix[:, 1, :], ALU.add))
                vec.sem_inc(patch_ready, 1)
                step(v.memset(stage[:, :, :], 0.0))
                step(v.memset(var[:, :], 1.0))
                for i in range(TURNS):
                    b0, nb = i * per_turn, blocks_of(i)
                    at = slice(b0, b0 + nb)
                    vec.wait_ge(states_here[i], 16 * nb)
                    st = state[:, at, 0:SUMS].rearrange("p b (h c) -> p b h c", c=HC)
                    step(v.tensor_scalar(rden[:, 0:nb, :], st[:, :, :, DH], 1e-16, None, ALU.max))
                    step(v.reciprocal(rden[:, 0:nb, :], rden[:, 0:nb, :]))
                    step(v.tensor_tensor(
                        stage[:, :, :].rearrange("p g (j c) -> p (g j) c", j=GROUP)[:, 0:nb, :].rearrange("p b (h c) -> p b h c", c=DH),
                        st[:, :, :, 0:DH],
                        rden[:, 0:nb, :].rearrange("p b (h o) -> p b h o", o=1).to_broadcast([P, nb, HEADS, DH]), ALU.mult))
                    vec.sem_inc(staged, 1)
                    vec.wait_ge(projected, i + 1)
                    step(v.tensor_tensor(k["res"][:, at, :], k["res"][:, at, :],
                                         psM[:, :, :].rearrange("p a (j c) -> p (a j) c", c=D)[:, 0:nb, :], ALU.add))
                    normalise(nc, vec, step, squares[:, 0:nb, :], k["res"][:, at, :], hs[:, at, :], mean[:, 0:nb], var[:, 0:nb],
                              root_asked, root_done, i + 1)
                    vec.sem_inc(h_ready, 1)


def tensor_product(nc, a, k):
    with ExitStack() as ctx:
        sb = lambda name, shape, dt=FP32: ctx.enter_context(nc.sbuf_tensor(name, shape, dt))
        pb = lambda name, shape, dt=FP32: ctx.enter_context(nc.psum_tensor(name, shape, dt))
        sem = lambda name: ctx.enter_context(nc.semaphore(name))
        T1 = T + 1
        GC = TRI * COLS
        w1, b1 = sb("w1", [HID, 1]), sb("b1", [HID, 1])
        wraw, wrad = sb("wraw", [HID + 1, 384]), sb("wrad", [HID + 1, 384])
        hid = [sb(f"hid{b}", [HID + 1, HALF * P]) for b in range(2)]
        src_i = [sb(f"src4_{b}", [P, T], I32) for b in range(2)]
        feat = [sb(f"feat{b}", [P, T, D]) for b in range(2)]
        ops = [sb(f"ops{b}", [P, T, 4 * JC]) for b in range(2)]
        dots = sb("dots", [P, T, 3 * VU])
        ca, cb = sb("ca", [P, T, VU]), sb("cb", [P, T, VU])
        prod = [sb(f"prod{r}", [P, JC, GC]) for r in range(2)]
        rest = [sb(f"rest{r}", [P, GC]) for r in range(2)]
        red = sb("red", [P, T, COLS])
        seed, same_c, run = sb("seed", [P, D, T1]), sb("same_c4", [P, D, T1]), k["run"]
        out = sb("out4", [P, T, D])
        zrow = sb("zrow4", [1, D])
        ident = k["ident"]
        psR = pb("psR", [P, 2, TRI, 512])
        psS = pb("psS", [P, 2, 512])

        w_loaded, wrad_ready, zrow_set, rows_set = sem("w_loaded4"), sem("wrad_ready"), sem("zrow_set4"), sem("rows_set")
        src_loaded, feat_here, w_here = ([sem(f"{n}{b}") for b in range(2)] for n in ("src_loaded4", "feat_here", "w_here"))
        feat_free, stored = sem("feat_free"), sem("stored4")
        hid_free = [sem(f"hid_free{h}") for h in range(2)]
        hid_ready = [sem(f"hid_ready{h}") for h in range(2)]
        radial_ready, radial_free, prod_ready, rest_ready, sum_ready, sum_free = (sem(n) for n in (
            "radial_ready", "radial_free", "prod_ready", "rest_ready", "sum_ready", "sum_free"))
        ops_copied, ops_free, flags_ready, red_free, scanned, run_copied = (sem(n) for n in (
            "ops_copied", "ops_free", "flags_ready4", "red_free", "scanned", "run_copied"))
        vec_done, chunk_begun = sem("vec_done4"), sem("chunk_begun4")

        with nc.Block() as block:

            @block.sync
            def _(sp):
                sp.dma_start(w1[:, :], a["w1"]).then_inc(w_loaded, 16)
                sp.dma_start(b1[:, :], a["b1"]).then_inc(w_loaded, 16)
                sp.dma_start(wraw[0:HID, :], a["w2"]).then_inc(w_loaded, 16)
                sp.dma_start(wraw[HID:HID + 1, :], a["b2"]).then_inc(w_loaded, 16)
                sources = a["src"].rearrange("(p s) -> p s", s=SLOTS)

                def load_src(b, at):
                    sp.dma_start(src_i[b][:, :], sources[:, bass.ds(at, T)]).then_inc(src_loaded[b], 16)

                def load_w(h, at):
                    sp.dma_start(hid[h][0:HID, :], a["wT"][bass.ds(at, HALF * P)].rearrange("(o n) -> o n", o=1).to_broadcast([HID, HALF * P])
                                 ).then_inc(w_here[h], 16)

                load_src(0, 0)
                load_src(1, T)
                load_w(0, 0)
                load_w(1, HALF * P)

                def body(i, last):
                    for b in range(2):
                        c1 = i * 2 + b + 1
                        if not last:
                            sp.wait_ge(feat_here[b], i * (16 * T) + 16 * T)
                            load_src(b, i * (2 * T) + (b + 2) * T)
                        if not (last and b == 1):
                            for h in range(2):
                                sp.wait_ge(hid_free[h], c1)
                                load_w(h, i * (2 * T * P) + ((b + 1) * T + h * HALF) * P)
                pairs(sp, body)

            @block.gpsimd
            def _(pool):
                with pool.Fori(0, PAIRS) as i:
                    for b in range(2):
                        pool.wait_ge(src_loaded[b], i * 16 + 16)
                        pool.wait_ge(feat_free, i * 2 + b + 1)
                        pool.sem_inc(chunk_begun, 1)
                        for t in range(T):
                            nc.gpsimd.indirect_dma_start(
                                feat[b][:, t, :], None, a["h2"],
                                bass.IndirectOffsetOnAxis(ap=src_i[b][:, t:t + 1].bitcast(U32), axis=0)).then_inc(feat_here[b], 16)

            @block.tensor
            def _(pe):
                def radial(c, g, r):
                    h, g0 = (0, 0) if g * TRI < HALF else (1, HALF // TRI)
                    if g == g0:
                        pe.wait_ge(hid_ready[h], c + 1)
                    pe.wait_ge(radial_free, c * GPC + g + 1)
                    for t in range(TRI):
                        at = ((g - g0) * TRI + t) * P
                        last_mm = nc.tensor.matmul(psR[:, r, t, 0:384], hid[h][:, at:at + P], wrad[:, :], start=True, stop=True)
                    last_mm.then_inc(radial_ready, 1)
                    if (g + 1) * TRI in (HALF, T):
                        pe.wait_ge(radial_ready, c * GPC + g + 1)
                        pe.sem_inc(hid_free[h], 1)

                def sums(c, g, r):
                    pe.wait_ge(sum_free, c * GPC + g + 1)
                    pe.wait_ge(prod_ready, (c * GPC + g) * 4 + 4)
                    for j in range(J_PE):
                        nc.tensor.matmul(psS[:, r, 0:GC], ident[:, :], prod[r][:, j, :], start=(j == 0), stop=False)
                    pe.wait_ge(rest_ready, c * GPC + g + 1)
                    nc.tensor.matmul(psS[:, r, 0:GC], ident[:, :], rest[r][:, :], start=False, stop=True).then_inc(sum_ready, 1)

                pe.wait_ge(wrad_ready, 1)
                radial(0, 0, 0)

                def body(i, last):
                    for b in range(2):
                        for g in range(GPC):
                            if g + 1 < GPC:
                                radial(i * 2 + b, g + 1, (g + 1) % 2)
                            elif not (last and b == 1):
                                radial(i * 2 + b + 1, 0, 0)
                            sums(i * 2 + b, g, g % 2)
                pairs(pe, body)

            @block.scalar
            def _(act):
                act.wait_ge(zrow_set, 1)
                act.dma_start(a["state2"][EDGES_PAD:EDGES_PAD + 1, :], zrow[:, :]).then_inc(stored, 16)
                act.wait_ge(w_loaded, 64)

                def hidden(h, c):
                    act.wait_ge(w_here[h], c * 16 + 16)
                    nc.scalar.activation(hid[h][0:HID, :], hid[h][0:HID, :], ACT.Relu, bias=b1[:, :], scale=w1[:, :]).then_inc(hid_ready[h], 1)

                def operands(b, c):
                    act.wait_ge(feat_here[b], (c - b) * (8 * T) + 16 * T)
                    act.wait_ge(ops_free, c + 1)
                    nc.scalar.activation(ops[b][:, :, 0:VU], feat[b][:, :, 0:VU], ACT.Copy).then_inc(ops_copied, 1)
                    for o in range(3):
                        nc.scalar.activation(ops[b][:, :, JC + JC * o:JC + JC * o + VU],
                                             feat[b][:, :, VU:D].rearrange("p t (v i) -> p t v i", i=3)[:, :, :, o], ACT.Copy).then_inc(ops_copied, 1)

                act.wait_ge(rows_set, 1)
                hidden(0, 0)
                hidden(1, 0)
                operands(0, 0)

                def body(i, last):
                    for b in range(2):
                        c = i * 2 + b
                        for g in range(GPC):
                            if g == 0:
                                act.wait_ge(red_free, c + 1)
                            act.wait_ge(sum_ready, c * GPC + g + 1)
                            nc.scalar.activation(red[:, g * TRI:(g + 1) * TRI, :].rearrange("p t c -> p (t c)"),
                                                 psS[:, g % 2, 0:GC], ACT.Copy).then_inc(sum_free, 1)
                            if g == 2:
                                act.wait_ge(scanned, c + 1)
                                nc.scalar.activation(same_c[:, :, 1:T1],
                                                     spread_front(k["same"][:, bass.ds(i * (2 * T) + b * T, T)], D), ACT.Copy).then_inc(flags_ready, 1)
                            if not (last and b == 1):
                                if g == 4:
                                    operands(1 - b, c + 1)
                                if g == HALF // TRI + 2:
                                    hidden(0, c + 1)
                        if not (last and b == 1):
                            hidden(1, c + 1)
                        act.wait_ge(scanned, c + 2)
                        act.wait_ge(stored, c * 16 + 16)
                        nc.scalar.activation(out[:, :, :], run[:, :, 1:T1].rearrange("p c t -> p t c"), ACT.Copy).then_inc(run_copied, 1)
                        act.wait_ge(run_copied, c + 2)
                        act.dma_start(a["state2"][0:EDGES_PAD, :].rearrange("(p s) c -> p (s c)", s=SLOTS)[:, bass.ds(i * (2 * T * D) + b * (T * D), T * D)],
                                      out[:, :, :].rearrange("p t c -> p (t c)")).then_inc(stored, 16)
                pairs(act, body)
                act.wait_ge(stored, 16 * (CHUNKS + 1))

            @block.vector
            def _(vec):
                v = nc.vector
                step = chain(vec, vec_done)
                step(v.memset(zrow[:, :], 0.0))
                vec.sem_inc(zrow_set, 1)
                for h in range(2):
                    step(v.memset(hid[h][HID:HID + 1, :], 1.0))
                step(v.memset(same_c[:, :, 0:1], 0.0))
                step(v.memset(run[:, :, T:T1], 0.0))
                vec.sem_inc(rows_set, 1)
                for primed, n in ((feat_free, 2), (radial_free, 2), (sum_free, 2), (ops_free, 2),
                                  (red_free, 1), (scanned, 1), (run_copied, 1)):
                    vec.sem_inc(primed, n)
                vec.wait_ge(w_loaded, 64)
                raw = lambda lo, n: wraw[:, lo:lo + n].rearrange("p (u v) -> p u v", u=VU)
                r11 = wraw[:, 192:384].rearrange("p (u v f) -> p u v f", u=VU, f=3)
                new = wrad[:, :].rearrange("p (u j) -> p u j", j=JC)
                for to, frm, coef in (
                        (new[:, 0:VU, 0:VU], raw(0, 64), N0 * C0),
                        (new[:, 0:VU, VU:JC], raw(64, 64), N0 * C1 / sqrt(3.0)),
                        (new[:, VU:2 * VU, 0:VU], raw(128, 64), N1 * C1 / sqrt(3.0)),
                        (new[:, VU:2 * VU, VU:JC], r11[:, :, :, 2], N1 * C2),
                        (new[:, 2 * VU:3 * VU, VU:JC], r11[:, :, :, 1], N1 * C1 / sqrt(6.0)),
                        (new[:, 2 * VU:3 * VU, 0:VU], r11[:, :, :, 2], -N1 * C2 / 3.0)):
                    step(v.tensor_scalar(to, frm, coef, None, ALU.mult))
                across = new[:, 2 * VU:3 * VU, 0:VU]
                step(v.scalar_tensor_tensor(out=across, in0=r11[:, :, :, 0], scalar=N1 * C0 / sqrt(3.0), in1=across, op0=ALU.mult, op1=ALU.add))
                vec.sem_inc(wrad_ready, 1)

                unit_of = lambda at, o: spread(k["unit"][:, bass.ds(at, T), o], VU)

                def dot(step, b, c, at):
                    vec.wait_ge(ops_copied, c * 4 + 4)
                    f1 = feat[b][:, :, VU:D].rearrange("p t (v i) -> p t v i", i=3)
                    step(v.tensor_tensor(dots[:, :, :].rearrange("p t (v i) -> p t v i", i=3), f1,
                                         k["unit"][:, bass.ds(at, T), :].rearrange("p t (o i) -> p t o i", o=1).to_broadcast([P, T, VU, 3]), ALU.mult))
                    vec.sem_inc(feat_free, 1)
                    step(v.tensor_reduce(ops[b][:, :, VU:JC], dots[:, :, :].rearrange("p t (v i) -> p t v i", i=3), axis=AX.X, op=ALU.add))

                def cross(step, b, at, o):
                    f = lambda x: ops[b][:, :, JC + JC * (x % 3):JC + JC * (x % 3) + VU]
                    step(v.tensor_tensor(ca[:, :, :], f(o + 2), unit_of(at, (o + 1) % 3), ALU.mult))
                    step(v.tensor_tensor(cb[:, :, :], f(o + 1), unit_of(at, (o + 2) % 3), ALU.mult))
                    step(v.tensor_tensor(ops[b][:, :, JC + JC * o + VU:2 * JC + JC * o], ca[:, :, :], cb[:, :, :], ALU.subtract))

                def products(b, c, g):
                    r, q = g % 2, c * GPC + g
                    ts = slice(g * TRI, (g + 1) * TRI)
                    vec.wait_ge(radial_ready, q + 1)
                    vec.wait_ge(sum_free, q + 1)
                    to = prod[r][:, :, :].rearrange("p j (t c) -> p t c j", c=COLS)
                    v.tensor_tensor(to[:, :, 0:2 * VU, :], psR[:, r, :, 0:256].rearrange("p t (u j) -> p t u j", j=JC),
                                    ops[b][:, ts, 0:JC].rearrange("p t (o j) -> p t o j", o=1).to_broadcast([P, TRI, 2 * VU, JC]),
                                    ALU.mult).then_inc(prod_ready, 1)
                    for o in range(3):
                        v.tensor_tensor(to[:, :, (2 + o) * VU:(3 + o) * VU, :], psR[:, r, :, 256:384].rearrange("p t (u j) -> p t u j", j=JC),
                                        ops[b][:, ts, JC + JC * o:2 * JC + JC * o].rearrange("p t (z j) -> p t z j", z=1).to_broadcast([P, TRI, VU, JC]),
                                        ALU.mult).then_inc(prod_ready, 1)
                    vec.wait_ge(prod_ready, q * 4 + 4)
                    vec.sem_inc(radial_free, 1)
                    v.tensor_reduce(rest[r][:, :], prod[r][:, J_PE:JC, :].rearrange("p j c -> p c j"), axis=AX.X, op=ALU.add).then_inc(rest_ready, 1)

                def finish(step, c, at):
                    vec.wait_ge(sum_free, c * GPC + GPC + 2)
                    vec.wait_ge(run_copied, c + 1)
                    along = dots[:, :, :].rearrange("p t (o u) -> p t o u", o=3)
                    step(v.tensor_tensor(along, red[:, :, VU:2 * VU].rearrange("p t (o u) -> p t o u", o=1).to_broadcast([P, T, 3, VU]),
                                         k["unit"][:, bass.ds(at, T), :].rearrange("p t (i o) -> p t i o", o=1).to_broadcast([P, T, 3, VU]), ALU.mult))
                    step(v.tensor_tensor(seed[:, VU:D, 1:T1].rearrange("p (u o) t -> p t o u", o=3), along,
                                         red[:, :, 2 * VU:COLS].rearrange("p t (o u) -> p t o u", o=3), ALU.add))
                    step(v.tensor_copy(seed[:, 0:VU, 1:T1].rearrange("p u t -> p t u"), red[:, :, 0:VU]))
                    step(v.tensor_copy(seed[:, :, 0], run[:, :, T]))
                    vec.sem_inc(red_free, 1)
                    vec.wait_ge(flags_ready, c + 1)
                    flat = lambda x: x[:, :, :].rearrange("p c t -> p (c t)")
                    step(v.tensor_tensor_scan(flat(run), flat(same_c), flat(seed), 0.0, ALU.mult, ALU.add))
                    vec.sem_inc(scanned, 1)

                for o in range(3):
                    if o == 0:
                        dot(step, 0, 0, 0)
                    cross(step, 0, 0, o)
                base, steps = step.count[0], 16

                def body(i, last):
                    step = chain(vec, vec_done, base + i * (2 * steps))
                    for b in range(2):
                        c = i * 2 + b
                        at = i * (2 * T) + b * T
                        more = not (last and b == 1)
                        for g in range(GPC):
                            products(b, c, g)
                            if more and g in (12, 13, 14):
                                if g == 12:
                                    vec.wait_ge(ops_copied, c * 4 + 8)
                                cross(step, 1 - b, at + T, g - 12)
                        vec.wait_ge(rest_ready, c * GPC + GPC)
                        vec.sem_inc(ops_free, 1)
                        if more:
                            dot(step, 1 - b, c + 1, at + T)
                        finish(step, c, at)
                    assert last or step.count[0] == 2 * steps, step.count[0]
                pairs(vec, body)
                vec.wait_ge(run_copied, CHUNKS + 1)


def node_sums(nc, a, k):
    with ExitStack() as ctx:
        sb = lambda name, shape, dt=FP32: ctx.enter_context(nc.sbuf_tensor(name, shape, dt))
        pb = lambda name, shape, dt=FP32: ctx.enter_context(nc.psum_tensor(name, shape, dt))
        sem = lambda name: ctx.enter_context(nc.semaphore(name))
        per_turn = BATCH * GROUP
        blocks_of = lambda i: min(per_turn, BLOCKS - i * per_turn)
        tail, rows = sb("tail5", [P, 2, D]), sb("rows5", [D, 2, P])
        totals = sb("totals5", [D, P + 1])
        patch = sb("patch5", [P, D])
        state = sb("state5", [P, BLOCKS, D])
        psA, psB = pb("psA5", [P, 2, P]), pb("psB5", [P, D])
        tail_ready, turned, carry_ready, carry_back, patch_here, patch_ready, patched, x_ready, x_stored, vec_done = (
            sem(n) for n in ("tail_ready5", "turned5", "carry_ready5", "carry_back5", "patch_here5", "patch_ready5",
                             "patched5", "x_ready", "x_stored", "vec_done5"))
        sums_here = [sem(f"sums_here{i}") for i in range(TURNS)]

        with nc.Block() as block:

            @block.sync
            def _(sp):
                for i in range(TURNS):
                    sp.wait_ge(x_ready, i + 1)
                    b0 = i * per_turn
                    sp.dma_start(a["out"].rearrange("(p b) c -> p b c", b=BLOCKS)[:, b0:b0 + blocks_of(i), :],
                                 state[:, b0:b0 + blocks_of(i), :]).then_inc(x_stored, 16)
                sp.wait_ge(x_stored, 16 * TURNS)

            @block.gpsimd
            def _(pool):
                nc.gpsimd.indirect_dma_start(patch[:, :], None, a["state2"], bass.IndirectOffsetOnAxis(
                    ap=k["end_i"][:, :].bitcast(U32), axis=0)).then_inc(patch_here, 16)
                pool.wait_ge(patch_ready, 1)
                nc.gpsimd.indirect_dma_start(a["state2"], bass.IndirectOffsetOnAxis(
                    ap=k["patch_i"][:, :].bitcast(U32), axis=0), patch[:, :], None,
                    bounds_check=EDGES_PAD - 1, oob_is_err=False).then_inc(patched, 16)
                pool.wait_ge(patched, 16)
                for b in range(BLOCKS):
                    nc.gpsimd.indirect_dma_start(state[:, b, :], None, a["state2"], bass.IndirectOffsetOnAxis(
                        ap=k["last_i"][:, b:b + 1].bitcast(U32), axis=0)).then_inc(sums_here[b // per_turn], 16)

            @block.tensor
            def _(pe):
                pe.wait_ge(tail_ready, 1)
                nc.tensor.transpose(psA[0:D, 0, :], tail[:, 0, :], k["ident"][:, :])
                nc.tensor.transpose(psA[0:D, 1, :], tail[:, 1, :], k["ident"][:, :]).then_inc(turned, 1)
                pe.wait_ge(carry_ready, 1)
                nc.tensor.transpose(psB[:, :], totals[:, 0:P], k["ident"][0:D, 0:D]).then_inc(carry_back, 1)

            @block.vector
            def _(vec):
                v = nc.vector
                step = chain(vec, vec_done)
                step(v.tensor_copy(tail[:, 0, :], k["run"][:, :, T]))
                step(v.tensor_copy(tail[:, 1, :], k["whole"][:, :].to_broadcast([P, D])))
                vec.sem_inc(tail_ready, 1)
                vec.wait_ge(turned, 1)
                step(v.tensor_copy(rows[:, :, :], psA[0:D, :, :]))
                step(v.memset(totals[:, 0:1], 0.0))
                step(v.tensor_tensor_scan(totals[:, 1:P + 1], rows[:, 1, :], rows[:, 0, :], 0.0, ALU.mult, ALU.add))
                vec.sem_inc(carry_ready, 1)
                vec.wait_ge(carry_back, 1)
                vec.wait_ge(patch_here, 16)
                step(v.tensor_tensor(patch[:, :], patch[:, :], psB[:, :], ALU.add))
                vec.sem_inc(patch_ready, 1)
                for i in range(TURNS):
                    b0, nb = i * per_turn, blocks_of(i)
                    at = slice(b0, b0 + nb)
                    vec.wait_ge(sums_here[i], 16 * nb)
                    step(v.tensor_tensor(state[:, at, :], state[:, at, :], k["res"][:, at, :], ALU.add))
                    vec.sem_inc(x_ready, 1)


def gnn_kernel(nc, a):
    with ExitStack() as ctx:
        sb = lambda name, shape, dt=FP32: ctx.enter_context(nc.sbuf_tensor(name, shape, dt))
        k = {
            "ident": sb("ident", [P, P]),
            "res": sb("res", [P, BLOCKS, D]),
            "q_first": sb("q_first", [P, D]),
            "last_i": sb("last_i", [P, BLOCKS], I32),
            "whole": sb("whole", [P, 1]),
            "end_i": sb("end_i", [P, 1], I32),
            "patch_i": sb("patch_i", [P, 1], I32),
        }
        prologue(nc, a, k)
        k["same"] = sb("same_all", [P, SLOTS])
        k["unit"] = sb("unit", [P, SLOTS, 3])
        with ExitStack() as states:
            k["peak"] = states.enter_context(nc.sbuf_tensor("peak", [P, HEADS, T + 1], FP32))
            k["sums"] = states.enter_context(nc.sbuf_tensor("sums", [P, SUMS, T + 1], FP32))
            attention(nc, a, k)
            node_attention(nc, a, k)
        k["run"] = sb("run", [P, D, T + 1])
        tensor_product(nc, a, k)
        node_sums(nc, a, k)


def kernel(x, src, dst, edge_attr_3, edge_weight, L0_gnn_Wq, L0_gnn_Wk, L0_gnn_Wv, L0_gnn_Wo,
           L1_gnn_w1, L1_gnn_b1, L1_gnn_w2, L1_gnn_b2):
    import numpy as np
    import concourse.bacc as bacc
    from concourse.bass_utils import run_bass_kernel_spmd

    def padded(array, rows, value=0):
        array = np.asarray(array)
        fill = np.full((rows - array.shape[0],) + array.shape[1:], value, array.dtype)
        return np.ascontiguousarray(np.concatenate([array, fill]))

    dst_pad = padded(dst, EDGES_PAD, NODES)
    weights = padded(edge_weight, EDGES_PAD).reshape(P, SLOTS)
    arrays = {
        "x": padded(x, NODES_PAD),
        "src": padded(src, EDGES_PAD),
        "dst": dst_pad,
        "dst_ext": np.concatenate([np.full(1, -1, dst_pad.dtype), dst_pad]),
        "dst_rows": dst_pad.reshape(-1, ROWW),
        "samples": np.ascontiguousarray(dst_pad[::ROWW].reshape(SP_, SC_)),
        "attr": padded(edge_attr_3, EDGES_PAD, 1),
        "wT": np.ascontiguousarray(weights.T).reshape(-1),
        "wq": np.asarray(L0_gnn_Wq), "wk": np.asarray(L0_gnn_Wk), "wv": np.asarray(L0_gnn_Wv), "wo": np.asarray(L0_gnn_Wo),
        "w1": np.asarray(L1_gnn_w1).reshape(HID, 1), "b1": np.asarray(L1_gnn_b1).reshape(HID, 1),
        "w2": np.asarray(L1_gnn_w2), "b2": np.asarray(L1_gnn_b2).reshape(1, -1),
    }
    nc = bacc.Bacc("TRN2", target_bir_lowering=False, num_devices=1)
    a = {n: nc.dram_tensor(f"in_{n}", v.shape, mybir.dt.from_np(v.dtype), kind="ExternalInput").ap() for n, v in arrays.items()}
    for name, shape in (("kv", (NODES_PAD, 2 * D)), ("q", (NODES_PAD, D)), ("qexp", (EDGES_PAD, D)), ("ptr", (NODES_PAD, 2)),
                        ("state", (EDGES_PAD + 2, STATE)), ("h2", (NODES_PAD, D)), ("state2", (EDGES_PAD + 1, D))):
        a[name] = nc.dram_tensor(f"scratch_{name}", shape, FP32, kind="Internal").ap()
    a["out"] = nc.dram_tensor("out_x", (NODES_PAD, D), FP32, kind="ExternalOutput").ap()
    gnn_kernel(nc, a)
    result = run_bass_kernel_spmd(nc, [{f"in_{n}": v for n, v in arrays.items()}], core_ids=[0])
    return result.results[0]["out_x"][:NODES]
```

```python
from contextlib import ExitStack
from math import pi, sqrt

import concourse.bass as bass
from concourse import mybir

FP32 = mybir.dt.float32
BF16 = mybir.dt.bfloat16
I32 = mybir.dt.int32
U32 = mybir.dt.uint32
ALU = mybir.AluOpType
ACT = mybir.ActivationFunctionType
AX = mybir.AxisListType

P = 128
NODES, EDGES, D = 12500, 400000, 32
HEADS, DH = 4, 8
BLOCKS = 98
NODES_PAD = P * BLOCKS
GROUP = 4
BLOCKS_UP = 100
BATCH = 5
TURNS = BLOCKS_UP // (GROUP * BATCH)

T = 54
SLOTS = 3132
CHUNKS = SLOTS // T
PAIRS = CHUNKS // 2
EDGES_PAD = P * SLOTS
TRI = 3
SIX = 2 * TRI
HALF = T // 2
GPC = T // TRI
SPC = T // SIX

ROWW = 128
SP_, SC_ = 116, 27
BB = BLOCKS + 1
PARTS = 3

STATE = 40
HC = DH + 1
SUMS = HEADS * HC
HID = 64
VU = 8
JC = 16
COLS = 32
FOLD = 7
BIG = 1.0e30
FAR = float(1 << 22)

C0 = 0.5 / sqrt(pi)
C1 = sqrt(3.0 / (4.0 * pi))
C2 = sqrt(3.0 / (8.0 * pi))
N0 = sqrt(4.0 * pi) / sqrt(16.0)
N1 = sqrt(4.0 * pi) * sqrt(3.0) / sqrt(32.0)

assert CHUNKS * T == SLOTS and 2 * PAIRS == CHUNKS and GPC * TRI == T and SP_ * SC_ * ROWW == EDGES_PAD


def spread(ap, n):
    return ap.rearrange("p (a o) -> p a o", o=1).to_broadcast([ap.shape[0], ap.shape[1], n])


def spread_front(ap, n):
    return ap.rearrange("p (o a) -> p o a", o=1).to_broadcast([ap.shape[0], n, ap.shape[1]])


def chain(engine, done, base=0):
    count = [0]

    def settle():
        engine.wait_ge(done, base + count[0])

    def step(instruction, hold=True):
        count[0] += 1
        instruction.then_inc(done, 1)
        if hold:
            settle()
    step.count, step.settle = count, settle
    return step


def pairs(engine, body):
    with engine.Fori(0, PAIRS - 1) as i:
        body(i, False)
    body(PAIRS - 1, True)


def pairs_apart(engine, body):
    body(0, True, False)
    with engine.Fori(1, PAIRS - 1) as i:
        body(i, False, False)
    body(PAIRS - 1, False, True)


def build_identity(pool, step, ident):
    step(pool.memset(ident[:, :], 0.0))
    step(pool.affine_select(out=ident[:, :], in_=ident[:, :], compare_op=ALU.not_equal, fill=1.0,
                            base=0, pattern=[[-1, P]], channel_multiplier=1))


def normalise(nc, vec, step, squares, x, h, mean, var, root_asked, root_done, asked):
    step(nc.vector.tensor_reduce(mean[:, :], x, axis=AX.X, op=ALU.add))
    step(nc.vector.tensor_scalar(mean[:, :], mean[:, :], 1.0 / D, None, ALU.mult))
    step(nc.vector.tensor_tensor(h, x, spread(mean[:, :], D), ALU.subtract))
    step(nc.vector.tensor_tensor(squares, h, h, ALU.mult))
    step(nc.vector.tensor_reduce(var[:, :], squares, axis=AX.X, op=ALU.add))
    step(nc.vector.tensor_scalar(var[:, :], var[:, :], 1.0 / D, 1e-5, ALU.mult, ALU.add))
    vec.sem_inc(root_asked, 1)
    vec.wait_ge(root_done, asked)
    step(nc.vector.reciprocal(var[:, :], var[:, :]))
    step(nc.vector.scalar_tensor_tensor(out=h, in0=h, scalar=0.0, in1=spread(var[:, :], D),
                                        op0=ALU.max, op1=ALU.mult))


def prologue(nc, a, k):
    with ExitStack() as ctx:
        sb = lambda name, shape, dt=FP32: ctx.enter_context(nc.sbuf_tensor(name, shape, dt))
        pb = lambda name, shape, dt=FP32: ctx.enter_context(nc.psum_tensor(name, shape, dt))
        sem = lambda name: ctx.enter_context(nc.semaphore(name))
        xs = sb("xs", [P, BLOCKS, D])
        hs = sb("hs", [P, BLOCKS_UP, D])
        scratch = sb("scratch", [P, BLOCKS, D])
        zeros = sb("zeros", [P, SLOTS])
        mean, var = sb("mean", [P, BLOCKS]), sb("var", [P, BLOCKS])
        wqkv = sb("wqkv", [P, GROUP, 3 * D])
        stage = sb("stage", [P, BATCH, P])
        hT = sb("hT", [P, BATCH, P])
        kv = sb("kv", [P, BLOCKS_UP, 2 * D])
        q = sb("q", [P, BLOCKS_UP, D])
        samp_i, samp = sb("samp_i", [SP_, SC_], I32), sb("samp", [SP_, SC_])
        starts_i, starts = sb("starts_i", [SP_, P + 1], I32), sb("starts", [SP_, P + 1])
        lows_i, lows = sb("lows_i", [SP_, BB], I32), sb("lows", [SP_, BB])
        above = sb("above", [SP_, SC_, P + 1], BF16)
        here = sb("here", [SP_, SC_, P], BF16)
        less = sb("less", [SP_, SC_, BB], BF16)
        ones = sb("ones", [SP_, BB], BF16)
        part = sb("part", [SP_, SC_])
        nid_i, nid = sb("nid_i", [P, BB], I32), sb("nid", [P, BB])
        row, row_i = sb("row", [P, BB]), sb("row_i", [P, BB], I32)
        drow = sb("drow", [P, BB, ROWW], I32)
        below = sb("below", [P, BB // PARTS, ROWW], BF16)
        ptr = sb("ptr", [P, BB])
        some = sb("some", [P, BLOCKS])
        first_at, first_i = sb("first_at", [P, BLOCKS]), sb("first_i", [P, BLOCKS], I32)
        last_at = sb("last_at", [P, BLOCKS])
        pair = sb("pair", [P, BLOCKS, 2])
        mine_i, mine = sb("mine_i", [P, 1], I32), sb("mine", [P, 1])
        edge_i, last_dst, prev_dst = sb("edge_i", [P, 1], I32), sb("last_dst", [P, 1], I32), sb("prev_dst", [P, 1], I32)
        own = sb("own", [P, 2])
        cross = sb("cross", [P, 3])
        ident = k["ident"]
        psT = pb("psT", [P, 2, 512])
        psM = pb("psM", [P, BATCH, 512])
        psC = pb("psC", [P, 512])

        x_loaded, w_loaded, samp_loaded = sem("x_loaded"), sem("w_loaded"), sem("samp_loaded")
        wblk_cleared, zeros_set, q_filled = sem("wblk_cleared"), sem("zeros_set"), sem("q_filled")
        pool_done, vec_done, act_done = sem("pool_done"), sem("vec_done"), sem("act_done")
        consts_ready, root_asked, root_done = sem("consts_ready"), sem("root_asked"), sem("root_done")
        staged, turned, hT_ready, projected, q_out, kv_out = (sem(n) for n in (
            "staged", "turned", "hT_ready", "projected", "q_out", "kv_out"))
        onehots, counted, rows_asked, ends_loaded = (sem(n) for n in ("onehots", "counted", "rows_asked", "ends_loaded"))
        rows_here = [sem(f"rows_here{i}") for i in range(PARTS)]
        first_asked, q_spread, tables, ptr_out, table_asked = (sem(n) for n in (
            "first_asked", "q_spread", "tables", "ptr_out", "table_asked"))
        own_here, qfirst_here, lns = sem("own_here"), sem("qfirst_here"), sem("lns")
        hT_free = sem("hT_free")

        with nc.Block() as block:

            @block.sync
            def _(sp):
                sp.dma_start(samp_i[:, :], a["samples"]).then_inc(samp_loaded, 16)
                sp.dma_start(xs[:, :, :], a["x"].rearrange("(p b) c -> p b c", b=BLOCKS)).then_inc(x_loaded, 16)
                sp.wait_ge(wblk_cleared, 1)
                for j in range(GROUP):
                    for n, w in enumerate(("wq", "wk", "wv")):
                        sp.dma_start(wqkv[j * D:(j + 1) * D, j, n * D:(n + 1) * D], a[w]).then_inc(w_loaded, 16)
                dst = a["dst"].rearrange("(p s) -> p s", s=SLOTS)
                with nc.allow_non_contiguous_dma(reason="one word per partition"):
                    sp.dma_start(mine_i[:, :], dst[:, 0:1]).then_inc(ends_loaded, 16)
                    sp.dma_start(last_dst[:, :], dst[:, SLOTS - 1:SLOTS]).then_inc(ends_loaded, 16)
                    sp.dma_start(prev_dst[:, :], a["dst_ext"][0:EDGES_PAD].rearrange("(p s) -> p s", s=SLOTS)[:, 0:1]).then_inc(ends_loaded, 16)
                sp.wait_ge(q_out, TURNS)
                sp.wait_ge(kv_out, TURNS)
                sp.dma_start(a["kv"].rearrange("(p b) c -> p b c", b=BLOCKS), kv[:, 0:BLOCKS, :]).then_inc(tables, 16)
                sp.dma_start(a["q"].rearrange("(p b) c -> p b c", b=BLOCKS), q[:, 0:BLOCKS, :]).then_inc(tables, 16)
                sp.wait_ge(table_asked, 1)
                sp.dma_start(a["ptr"].rearrange("(p b) c -> p b c", b=BLOCKS), pair[:, :, :]).then_inc(ptr_out, 16)
                sp.wait_ge(tables, 32)
                sp.wait_ge(ptr_out, 16)

            @block.gpsimd
            def _(pool):
                step = chain(pool, pool_done)
                step(nc.gpsimd.memset(wqkv[:, :, :], 0.0))
                pool.sem_inc(wblk_cleared, 1)
                build_identity(nc.gpsimd, step, ident)
                nc.gpsimd.iota(starts_i[:, :], pattern=[[BLOCKS, P + 1]], base=0, channel_multiplier=0).then_inc(consts_ready, 1)
                nc.gpsimd.iota(lows_i[:, :], pattern=[[1, BB]], base=0, channel_multiplier=0).then_inc(consts_ready, 1)
                nc.gpsimd.iota(nid_i[:, :], pattern=[[1, BB]], base=0, channel_multiplier=BLOCKS).then_inc(consts_ready, 1)
                nc.gpsimd.iota(edge_i[:, :], pattern=[[0, 1]], base=0, channel_multiplier=SLOTS).then_inc(consts_ready, 1)
                nc.gpsimd.memset(ones[:, :], 1.0).then_inc(consts_ready, 1)
                pool.wait_ge(rows_asked, 1)
                for b in range(BB):
                    nc.gpsimd.indirect_dma_start(
                        drow[:, b, :], None, a["dst_rows"],
                        bass.IndirectOffsetOnAxis(ap=row_i[:, b:b + 1].bitcast(U32), axis=0),
                    ).then_inc(rows_here[b // (BB // PARTS)], 16)
                pool.wait_ge(first_asked, 1)
                pool.wait_ge(q_filled, 16 * D)
                pool.wait_ge(q_out, TURNS)
                for b in range(BLOCKS):
                    nc.gpsimd.indirect_dma_start(
                        a["qexp"], bass.IndirectOffsetOnAxis(ap=first_i[:, b:b + 1].bitcast(U32), axis=0),
                        q[:, b, :], None, bounds_check=EDGES_PAD - 1, oob_is_err=False).then_inc(q_spread, 16)
                pool.wait_ge(ends_loaded, 48)
                pool.wait_ge(ptr_out, 16)
                pool.wait_ge(tables, 32)
                mine_at = bass.IndirectOffsetOnAxis(ap=mine_i[:, :].bitcast(U32), axis=0)
                nc.gpsimd.indirect_dma_start(own[:, :], None, a["ptr"], mine_at).then_inc(own_here, 16)
                nc.gpsimd.indirect_dma_start(k["q_first"][:, :], None, a["q"], mine_at).then_inc(qfirst_here, 16)
                pool.wait_ge(q_spread, 16 * BLOCKS)
                pool.wait_ge(qfirst_here, 16)

            @block.scalar
            def _(act):
                step = chain(act, act_done)
                act.wait_ge(zeros_set, 1)
                rows = a["qexp"][0:EDGES_PAD, :].rearrange("(p s) c -> p (s c)", s=SLOTS)
                for j in range(D):
                    act.dma_start(rows[:, j * SLOTS:(j + 1) * SLOTS], zeros[:, :]).then_inc(q_filled, 16)
                act.wait_ge(root_asked, 1)
                nc.scalar.activation(var[:, :], var[:, :], ACT.Sqrt).then_inc(root_done, 1)
                with act.Fori(0, TURNS) as i:
                    act.wait_ge(turned, i + 1)
                    nc.scalar.activation(hT[:, :, :].rearrange("p g n -> p (g n)"),
                                         psT[:, :, :].rearrange("p a n -> p (a n)")[:, 0:BATCH * P],
                                         ACT.Copy).then_inc(hT_ready, 1)
                    act.wait_ge(projected, i + 1)
                    nc.scalar.activation(
                        q[:, bass.ds(i * (BATCH * GROUP), BATCH * GROUP), :].rearrange("p (g j) c -> p g j c", j=GROUP),
                        psM[:, :, 0:GROUP * 3 * D].rearrange("p g (j c) -> p g j c", j=GROUP)[:, :, :, 0:D],
                        ACT.Copy, scale=1.0 / sqrt(DH)).then_inc(q_out, 1)

            @block.tensor
            def _(pe):
                pe.wait_ge(onehots, 1)
                for s in range(SC_):
                    nc.tensor.matmul(psC[:, 0:BB], above[:, s, 0:P], ones[:, :], start=(s == 0), stop=False)
                    last = nc.tensor.matmul(psC[:, 0:BB], here[:, s, :], less[:, s, :], start=False, stop=(s == SC_ - 1))
                last.then_inc(counted, 1)
                pe.wait_ge(w_loaded, 16 * GROUP * 3)
                pe.wait_ge(pool_done, 3)
                with pe.Fori(0, TURNS) as i:
                    pe.wait_ge(staged, i + 1)
                    for g in range(BATCH):
                        last = nc.tensor.transpose(psT[:, (g * P) // 512, (g * P) % 512:(g * P) % 512 + P],
                                                   stage[:, g, :], ident[:, :])
                    last.then_inc(turned, 1)
                    pe.wait_ge(hT_ready, i + 1)
                    for g in range(BATCH):
                        last = nc.tensor.matmul(psM[:, g, 0:GROUP * 3 * D], hT[:, g, :],
                                                wqkv[:, :, :].rearrange("p j c -> p (j c)"), start=True, stop=True)
                    last.then_inc(projected, 1)

            @block.vector
            def _(vec):
                step = chain(vec, vec_done)
                v = nc.vector
                step(v.memset(zeros[:, :], 0.0))
                vec.sem_inc(zeros_set, 1)
                step(v.memset(hs[:, BLOCKS:BLOCKS_UP, :], 0.0))
                vec.wait_ge(samp_loaded, 16)
                vec.wait_ge(consts_ready, 5)
                step(v.tensor_copy(samp[:, :], samp_i[:, :]))
                step(v.tensor_copy(starts[:, :], starts_i[:, :]))
                step(v.tensor_copy(lows[:, :], lows_i[:, :]))
                step(v.tensor_copy(nid[:, :], nid_i[:, :]))
                step(v.tensor_tensor(above[:, :, :], spread_front(starts[:, :], SC_), spread(samp[:, :], P + 1), ALU.is_gt))
                step(v.tensor_reduce(part[:, :], above[:, :, :], axis=AX.X, op=ALU.add))
                step(v.tensor_tensor(here[:, :, :], above[:, :, 1:P + 1], above[:, :, 0:P], ALU.subtract))
                step(v.tensor_scalar(part[:, :], part[:, :], float(BLOCKS), -float(BLOCKS * P), ALU.mult, ALU.add))
                step(v.tensor_tensor(part[:, :], samp[:, :], part[:, :], ALU.add))
                step(v.tensor_tensor(less[:, :, :], spread_front(lows[:, :], SC_), spread(part[:, :], BB), ALU.is_gt))
                vec.sem_inc(onehots, 1)
                vec.wait_ge(counted, 1)
                step(v.tensor_scalar(row[:, :], psC[:, 0:BB], -1.0, 0.0, ALU.add, ALU.max))
                step(v.tensor_copy(row_i[:, :], row[:, :]))
                vec.sem_inc(rows_asked, 1)
                vec.wait_ge(x_loaded, 16)
                normalise(nc, vec, step, scratch[:, :, :], xs[:, :, :], hs[:, 0:BLOCKS, :], mean, var, root_asked, root_done, 1)
                step(v.tensor_tensor(k["res"][:, :, :], xs[:, :, :], hs[:, 0:BLOCKS, :], ALU.add))
                with vec.Fori(0, TURNS) as i:
                    v.tensor_copy(stage[:, :, :].rearrange("p g n -> p (g n)"),
                                  hs[:, bass.ds(i * (BATCH * GROUP), BATCH * GROUP), :].rearrange("p b c -> p (b c)")
                                  ).then_inc(staged, 1)
                    vec.wait_ge(q_out, i + 1)
                    v.tensor_copy(
                        kv[:, bass.ds(i * (BATCH * GROUP), BATCH * GROUP), :].rearrange("p (g j) c -> p g j c", j=GROUP),
                        psM[:, :, 0:GROUP * 3 * D].rearrange("p g (j c) -> p g j c", j=GROUP)[:, :, :, D:3 * D]
                    ).then_inc(kv_out, 1)
                    vec.wait_ge(kv_out, i + 1)
                w = BB // PARTS
                for g in range(PARTS):
                    vec.wait_ge(rows_here[g], 16 * w)
                    at = slice(g * w, (g + 1) * w)
                    step(v.tensor_tensor(below[:, :, :], drow[:, at, :], spread(nid[:, at], ROWW), ALU.is_lt))
                    step(v.tensor_reduce(ptr[:, at], below[:, :, :], axis=AX.X, op=ALU.add))
                step(v.scalar_tensor_tensor(out=ptr[:, :], in0=row[:, :], scalar=float(ROWW), in1=ptr[:, :], op0=ALU.mult, op1=ALU.add))
                lo, hi = ptr[:, 0:BLOCKS], ptr[:, 1:BB]
                step(v.tensor_tensor(some[:, :], hi, lo, ALU.is_gt))
                step(v.tensor_scalar(first_at[:, :], some[:, :], -FAR, FAR, ALU.mult, ALU.add))
                step(v.tensor_tensor(first_at[:, :], first_at[:, :], lo, ALU.add))
                step(v.tensor_copy(first_i[:, :], first_at[:, :]))
                vec.sem_inc(first_asked, 1)
                step(v.tensor_scalar(last_at[:, :], hi, -1.0 - EDGES_PAD, None, ALU.add))
                step(v.tensor_tensor(last_at[:, :], last_at[:, :], some[:, :], ALU.mult))
                step(v.tensor_scalar(last_at[:, :], last_at[:, :], float(EDGES_PAD), None, ALU.add))
                step(v.tensor_copy(k["last_i"][:, :], last_at[:, :]))
                step(v.tensor_copy(pair[:, :, 0], lo))
                step(v.tensor_copy(pair[:, :, 1], hi))
                vec.sem_inc(table_asked, 1)
                vec.wait_ge(ends_loaded, 48)
                step(v.tensor_tensor(k["whole"][:, :], last_dst[:, :], prev_dst[:, :], ALU.is_equal))
                vec.wait_ge(own_here, 16)
                step(v.tensor_copy(mine[:, :], edge_i[:, :]))
                step(v.tensor_scalar(cross[:, 2:3], own[:, 1:2], -1.0, None, ALU.add))
                step(v.tensor_copy(k["end_i"][:, :], cross[:, 2:3]))
                step(v.tensor_tensor(cross[:, 0:1], own[:, 0:1], mine[:, :], ALU.is_lt))
                step(v.tensor_scalar(mine[:, :], mine[:, :], float(SLOTS), None, ALU.add))
                step(v.tensor_tensor(cross[:, 1:2], cross[:, 2:3], mine[:, :], ALU.is_lt))
                step(v.tensor_tensor(cross[:, 0:1], cross[:, 0:1], cross[:, 1:2], ALU.mult))
                step(v.tensor_scalar(cross[:, 0:1], cross[:, 0:1], -FAR, FAR, ALU.mult, ALU.add))
                step(v.tensor_tensor(cross[:, 0:1], cross[:, 0:1], cross[:, 2:3], ALU.add))
                step(v.tensor_copy(k["patch_i"][:, :], cross[:, 0:1]))


def attention(nc, a, k):
    with ExitStack() as ctx:
        sb = lambda name, shape, dt=FP32: ctx.enter_context(nc.sbuf_tensor(name, shape, dt))
        sem = lambda name: ctx.enter_context(nc.semaphore(name))
        T1 = T + 1
        src_i = [sb(f"src_i{b}", [P, T], I32) for b in range(2)]
        kv = [sb(f"kv{b}", [P, T, 2 * D]) for b in range(2)]
        dst_i = [sb(f"dst_i{b}", [P, T1], I32) for b in range(2)]
        attr = [sb(f"attr{b}", [P, T, 3]) for b in range(2)]
        qin = [sb(f"qin{b}", [P, T, D]) for b in range(2)]
        same = sb("same", [P, T1])
        pen = sb("pen", [P, T1])
        same_c, pen_c = sb("same_c", [P, D, T1]), sb("pen_c", [P, HEADS, T1])
        qseed, qrun = sb("qseed", [P, D, T1]), sb("qrun", [P, D, T1])
        qk = sb("qk", [P, HEADS, T, DH])
        score = sb("score", [P, HEADS, T1])
        decay = sb("decay", [P, HEADS, T1])
        rel = sb("rel", [P, HEADS, T])
        decay_c = sb("decay_c", [P, SUMS, T1])
        ev, sums = sb("ev", [P, HEADS, HC, T1]), k["sums"]
        peak = k["peak"]
        out = [sb(f"out{b}", [P, T, STATE]) for b in range(2)]
        sq, rn = sb("sq", [P, T, 3]), sb("rn", [P, T])
        frame = [sb(f"frame_out{b}", [P, T, 9]) for b in range(2)]
        sgn, inv, xy = sb("sgn", [P, T]), sb("inv", [P, T]), sb("xy", [P, T])
        zrow = sb("zrow", [2, STATE])

        src_loaded, dst_loaded, attr_loaded, q_loaded, kv_here, stored = (
            [sem(f"{n}{b}") for b in range(2)] for n in ("src_loaded", "dst_loaded", "attr_loaded", "q_loaded", "kv_here", "stored"))
        kv_free, dst_free, attr_free, q_free = (sem(n) for n in ("kv_free", "dst_free", "attr_free", "q_free"))
        flags_ready, spread_ready, q_scanned, exps_asked, exps_ready = (sem(n) for n in (
            "flags_ready", "spread_ready", "q_scanned", "exps_asked", "exps_ready"))
        sums_ready, sums_copied, rn_asked, rn_ready = (sem(n) for n in ("sums_ready", "sums_copied", "rn_asked", "rn_ready"))
        frame_ready, frame_free = sem("frame_ready"), sem("frame_free")
        frame_stored = [sem(f"frame_stored{b}") for b in range(2)]
        vec_done, zrow_set, chunk_begun = sem("vec_done2"), sem("zrow_set"), sem("chunk_begun")
        edges = lambda name: a[name].rearrange("(p s) -> p s", s=SLOTS)

        with nc.Block() as block:

            @block.sync
            def _(sp):
                base = a["dst_ext"]
                before = base[0:EDGES_PAD].rearrange("(p s) -> p s", s=SLOTS)
                def load_src(b, at):
                    sp.dma_start(src_i[b][:, :], edges("src")[:, bass.ds(at, T)]).then_inc(src_loaded[b], 16)

                load_src(0, 0)
                load_src(1, T)

                def body(i, last):
                    for b in range(2):
                        at = i * (2 * T) + b * T
                        sp.wait_ge(dst_free, i * 2 + b + 1)
                        sp.dma_start(dst_i[b][:, 0:T], before[:, bass.ds(at, T)]).then_inc(dst_loaded[b], 16)
                        sp.dma_start(dst_i[b][:, T:T1], edges("dst")[:, bass.ds(at + (T - 1), 1)], allow_slow_non_contiguous=True).then_inc(dst_loaded[b], 16)
                        sp.wait_ge(attr_free, i * 2 + b + 1)
                        sp.dma_start(attr[b][:, :, :].rearrange("p t c -> p (t c)"),
                                     a["attr"].rearrange("(p s) c -> p (s c)", s=SLOTS)[:, bass.ds(at * 3, 3 * T)]).then_inc(attr_loaded[b], 16)
                        sp.wait_ge(q_free, i * 2 + b + 1)
                        sp.dma_start(qin[b][:, :, :].rearrange("p t c -> p (t c)"),
                                     a["qexp"].rearrange("(p s) c -> p (s c)", s=SLOTS)[:, bass.ds(at * D, D * T)]).then_inc(q_loaded[b], 16)
                        sp.wait_ge(frame_ready, i * 2 + b + 1)
                        sp.dma_start(a["frame"].rearrange("(p s) c -> p (s c)", s=SLOTS)[:, bass.ds(at * 9, 9 * T)],
                                     frame[b][:, :, :].rearrange("p t c -> p (t c)")).then_inc(frame_stored[b], 16)
                        sp.wait_ge(frame_stored[b], i * 16 + 16)
                        sp.sem_inc(frame_free, 1)
                        if not last:
                            sp.wait_ge(kv_here[b], i * (16 * T) + 16 * T)
                            load_src(b, i * (2 * T) + (b + 2) * T)
                pairs(sp, body)

            @block.gpsimd
            def _(pool):
                with pool.Fori(0, PAIRS) as i:
                    for b in range(2):
                        pool.wait_ge(src_loaded[b], i * 16 + 16)
                        pool.wait_ge(kv_free, i * 2 + b + 1)
                        pool.sem_inc(chunk_begun, 1)
                        for t in range(T):
                            nc.gpsimd.indirect_dma_start(
                                kv[b][:, t, :], None, a["kv"],
                                bass.IndirectOffsetOnAxis(ap=src_i[b][:, t:t + 1].bitcast(U32), axis=0)).then_inc(kv_here[b], 16)

            @block.scalar
            def _(act):
                act.wait_ge(zrow_set, 1)
                for b in range(2):
                    act.dma_start(a["state"][EDGES_PAD + b:EDGES_PAD + b + 1, :], zrow[b:b + 1, :]).then_inc(stored[b], 16)
                act.sem_inc(q_free, 2)
                with act.Fori(0, PAIRS) as i:
                    for b in range(2):
                        c1 = i * 2 + b + 1
                        act.wait_ge(rn_asked, c1)
                        nc.scalar.activation(rn[:, :], rn[:, :], ACT.Sqrt).then_inc(rn_ready, 1)
                        act.wait_ge(flags_ready, c1)
                        act.wait_ge(q_scanned, c1)
                        nc.scalar.activation(same_c[:, :, :], spread_front(same[:, :], D), ACT.Copy).then_inc(spread_ready, 1)
                        nc.scalar.activation(pen_c[:, :, :], spread_front(pen[:, :], HEADS), ACT.Copy).then_inc(spread_ready, 1)
                        act.wait_ge(q_loaded[b], i * 16 + 16)
                        nc.scalar.activation(qseed[:, :, 1:T1], qin[b][:, :, :].rearrange("p t c -> p c t"), ACT.Copy).then_inc(spread_ready, 1)
                        act.wait_ge(spread_ready, c1 * 3)
                        act.sem_inc(q_free, 1)
                        act.wait_ge(exps_asked, c1)
                        nc.scalar.activation(decay_c[:, :, :].rearrange("p (h c) t -> p h c t", c=HC),
                                             decay[:, :, :].rearrange("p h (o t) -> p h o t", o=1).to_broadcast([P, HEADS, HC, T1]),
                                             ACT.Exp).then_inc(exps_ready, 1)
                        nc.scalar.activation(ev[:, :, DH, 1:T1], rel[:, :, :], ACT.Exp).then_inc(exps_ready, 1)
                        act.wait_ge(sums_ready, c1)
                        act.wait_ge(stored[b], i * 16 + 16)
                        nc.scalar.activation(out[b][:, :, 0:SUMS], sums[:, :, 1:T1].rearrange("p c t -> p t c"), ACT.Copy).then_inc(sums_copied, 1)
                        nc.scalar.activation(out[b][:, :, SUMS:STATE], peak[:, :, 1:T1].rearrange("p c t -> p t c"), ACT.Copy).then_inc(sums_copied, 1)
                        act.wait_ge(sums_copied, c1 * 2 + 2)
                        act.dma_start(a["state"][0:EDGES_PAD, :].rearrange("(p s) c -> p (s c)", s=SLOTS)[:, bass.ds(i * (2 * T * STATE) + b * (T * STATE), T * STATE)],
                                      out[b][:, :, :].rearrange("p t c -> p (t c)")).then_inc(stored[b], 16)
                for b in range(2):
                    act.wait_ge(stored[b], 16 * (PAIRS + 1))

            @block.vector
            def _(vec):
                v = nc.vector
                step = chain(vec, vec_done)
                step(v.memset(zrow[:, :], 0.0))
                vec.sem_inc(zrow_set, 1)
                step(v.tensor_copy(qrun[:, :, T], k["q_first"][:, :]))
                step(v.memset(peak[:, :, T:T1], -BIG))
                step(v.memset(sums[:, :, T:T1], 0.0))
                step(v.memset(same[:, :], 0.0))
                step(v.memset(decay[:, :, :], -BIG))
                for primed, n in ((kv_free, 2), (dst_free, 2), (attr_free, 2), (frame_free, 2), (q_scanned, 1), (sums_copied, 2)):
                    vec.sem_inc(primed, n)
                steps = 34
                base = step.count[0]
                with vec.Fori(0, PAIRS) as i:
                    step = chain(vec, vec_done, base + i * (2 * steps))
                    for b in range(2):
                        c1 = i * 2 + b + 1
                        at = i * (2 * T) + b * T
                        vec.wait_ge(attr_loaded[b], i * 16 + 16)
                        step(v.tensor_tensor(sq[:, :, :], attr[b][:, :, :], attr[b][:, :, :], ALU.mult))
                        step(v.tensor_reduce(rn[:, :], sq[:, :, :], axis=AX.X, op=ALU.add))
                        vec.sem_inc(rn_asked, 1)
                        vec.wait_ge(dst_loaded[b], i * 32 + 32)
                        step(v.tensor_tensor(same[:, 1:T1], dst_i[b][:, 1:T1], dst_i[b][:, 0:T], ALU.is_equal))
                        vec.sem_inc(dst_free, 1)
                        step(v.tensor_scalar(pen[:, :], same[:, :], BIG, -BIG, ALU.mult, ALU.add))
                        vec.sem_inc(flags_ready, 1)
                        step(v.tensor_copy(k["same"][:, bass.ds(at, T)], same[:, 1:T1]))
                        vec.wait_ge(rn_ready, c1)
                        step(v.reciprocal(rn[:, :], rn[:, :]))
                        vec.wait_ge(frame_free, c1)
                        fr = frame[b]
                        nx, ny, nz = fr[:, :, 0], fr[:, :, 1], fr[:, :, 2]
                        step(v.tensor_tensor(fr[:, :, 0:2], attr[b][:, :, 1:3], spread(rn[:, :], 2), ALU.mult))
                        step(v.tensor_tensor(nz, attr[b][:, :, 0], rn[:, :], ALU.mult))
                        vec.sem_inc(attr_free, 1)
                        step(v.tensor_scalar(sgn[:, :], nz, 0.0, 2.0, ALU.is_ge, ALU.mult))
                        step(v.tensor_scalar(sgn[:, :], sgn[:, :], -1.0, None, ALU.add))
                        step(v.tensor_tensor(inv[:, :], sgn[:, :], nz, ALU.add))
                        step(v.reciprocal(inv[:, :], inv[:, :]))
                        step(v.scalar_tensor_tensor(out=xy[:, :], in0=ny, scalar=-1.0, in1=inv[:, :], op0=ALU.mult, op1=ALU.mult))
                        step(v.tensor_tensor(fr[:, :, 6], xy[:, :], nx, ALU.mult))
                        step(v.tensor_tensor(xy[:, :], xy[:, :], ny, ALU.mult))
                        step(v.tensor_tensor(fr[:, :, 7], xy[:, :], sgn[:, :], ALU.add))
                        step(v.tensor_scalar(fr[:, :, 8], ny, -1.0, None, ALU.mult))
                        step(v.scalar_tensor_tensor(out=fr[:, :, 5], in0=nx, scalar=-1.0, in1=sgn[:, :], op0=ALU.mult, op1=ALU.mult))
                        step(v.tensor_tensor(fr[:, :, 4], fr[:, :, 6], sgn[:, :], ALU.mult))
                        step(v.tensor_tensor(xy[:, :], nx, inv[:, :], ALU.mult))
                        step(v.tensor_tensor(xy[:, :], xy[:, :], fr[:, :, 5], ALU.mult))
                        step(v.tensor_scalar(fr[:, :, 3], xy[:, :], 1.0, None, ALU.add))
                        vec.sem_inc(frame_ready, 1)
                        step(v.tensor_copy(qseed[:, :, 0], qrun[:, :, T]))
                        vec.wait_ge(spread_ready, c1 * 3)
                        flat = lambda x: x[:, :, :].rearrange("p c t -> p (c t)")
                        step(v.tensor_tensor_scan(flat(qrun), flat(same_c), flat(qseed), 0.0, ALU.mult, ALU.add))
                        vec.wait_ge(kv_here[b], i * (16 * T) + 16 * T)
                        step(v.tensor_tensor(qk[:, :, :, :], qrun[:, :, 1:T1].rearrange("p (h d) t -> p h t d", d=DH),
                                             kv[b][:, :, 0:D].rearrange("p t (h d) -> p h t d", d=DH), ALU.mult))
                        step(v.tensor_reduce(score[:, :, 1:T1], qk[:, :, :, :], axis=AX.X, op=ALU.add))
                        step(v.tensor_copy(score[:, :, 0], peak[:, :, T]))
                        vec.wait_ge(sums_copied, c1 * 2)
                        step(v.tensor_tensor_scan(flat(peak), flat(pen_c), flat(score), -BIG, ALU.add, ALU.max))
                        step(v.tensor_tensor(decay[:, :, 1:T1], peak[:, :, 0:T], pen_c[:, :, 1:T1], ALU.add))
                        step(v.tensor_tensor(decay[:, :, 1:T1], decay[:, :, 1:T1], peak[:, :, 1:T1], ALU.subtract))
                        step(v.tensor_tensor(rel[:, :, :], score[:, :, 1:T1], peak[:, :, 1:T1], ALU.subtract))
                        vec.sem_inc(q_scanned, 1)
                        vec.sem_inc(exps_asked, 1)
                        vec.wait_ge(exps_ready, c1 * 2)
                        step(v.tensor_tensor(ev[:, :, 0:DH, 1:T1], kv[b][:, :, D:2 * D].rearrange("p t (h d) -> p h d t", d=DH),
                                             ev[:, :, DH:HC, 1:T1].to_broadcast([P, HEADS, DH, T]), ALU.mult))
                        vec.sem_inc(kv_free, 1)
                        step(v.tensor_copy(ev[:, :, :, 0], sums[:, :, T].rearrange("p (h c) -> p h c", c=HC)))
                        step(v.tensor_tensor_scan(flat(sums), flat(decay_c), ev[:, :, :, :].rearrange("p h c t -> p (h c t)"), 0.0, ALU.mult, ALU.add))
                        vec.sem_inc(sums_ready, 1)
                    assert step.count[0] == 2 * steps, step.count[0]
                vec.wait_ge(sums_copied, CHUNKS * 2 + 2)


def node_attention(nc, a, k):
    with ExitStack() as ctx:
        sb = lambda name, shape, dt=FP32: ctx.enter_context(nc.sbuf_tensor(name, shape, dt))
        pb = lambda name, shape, dt=FP32: ctx.enter_context(nc.psum_tensor(name, shape, dt))
        sem = lambda name: ctx.enter_context(nc.semaphore(name))
        per_turn = BATCH * GROUP
        blocks_of = lambda i: min(per_turn, BLOCKS - i * per_turn)
        tail = sb("tail", [P, 3, SUMS])
        rows = sb("rows", [SUMS, 3, P])
        peaks, totals = sb("peaks", [SUMS, P + 1]), sb("totals", [SUMS, P + 1])
        shrink, gain = sb("shrink", [SUMS, P]), sb("gain", [SUMS, P])
        carry = sb("carry", [P, 2, SUMS])
        patch = sb("patch", [P, STATE])
        top, ex = sb("top", [P, SUMS]), sb("ex", [P, 2, SUMS])
        mix = sb("mix", [P, 2, SUMS])
        state = sb("state", [P, BLOCKS, STATE])
        rden = sb("rden", [P, per_turn, HEADS])
        stage, hT = sb("stage3", [P, BATCH, P]), sb("hT3", [P, BATCH, P])
        wo = sb("wo", [P, GROUP, D])
        hs = sb("hs3", [P, BLOCKS, D])
        squares = sb("squares3", [P, per_turn, D])
        mean, var = sb("mean3", [P, per_turn]), sb("var3", [P, per_turn])
        ident = k["ident"]
        psA, psB = pb("psA", [P, 3, P]), pb("psB", [P, 2, SUMS])
        psT = pb("psT3", [P, 2, 512])
        psM = pb("psM3", [P, 2, 512])

        wo_loaded, wo_cleared, tail_ready, turned, rows_ready, ex_asked, ex_done, carry_ready, carry_back = (sem(n) for n in (
            "wo_loaded", "wo_cleared", "tail_ready", "turned3", "rows_ready", "ex_asked", "ex_done", "carry_ready", "carry_back"))
        patch_here, patch_ready, patched = sem("patch_here"), sem("patch_ready"), sem("patched")
        states_here = [sem(f"states_here{i}") for i in range(TURNS)]
        staged, stage_turned, hT_ready, projected, root_asked, root_done, h_ready, h_stored = (sem(n) for n in (
            "staged3", "stage_turned3", "hT_ready3", "projected3", "root_asked3", "root_done3", "h_ready3", "h_stored"))
        vec_done, pool_done = sem("vec_done3"), sem("pool_done3")

        with nc.Block() as block:

            @block.sync
            def _(sp):
                sp.wait_ge(wo_cleared, 1)
                for j in range(GROUP):
                    sp.dma_start(wo[j * D:(j + 1) * D, j, :], a["wo"]).then_inc(wo_loaded, 16)
                for i in range(TURNS):
                    sp.wait_ge(h_ready, i + 1)
                    b0 = i * per_turn
                    sp.dma_start(a["h2"].rearrange("(p b) c -> p b c", b=BLOCKS)[:, b0:b0 + blocks_of(i), :],
                                 hs[:, b0:b0 + blocks_of(i), :]).then_inc(h_stored, 16)
                sp.wait_ge(h_stored, 16 * TURNS)

            @block.gpsimd
            def _(pool):
                step = chain(pool, pool_done)
                step(nc.gpsimd.memset(wo[:, :, :], 0.0))
                pool.sem_inc(wo_cleared, 1)
                nc.gpsimd.indirect_dma_start(patch[:, :], None, a["state"], bass.IndirectOffsetOnAxis(
                    ap=k["end_i"][:, :].bitcast(U32), axis=0)).then_inc(patch_here, 16)
                pool.wait_ge(patch_ready, 1)
                nc.gpsimd.indirect_dma_start(a["state"], bass.IndirectOffsetOnAxis(
                    ap=k["patch_i"][:, :].bitcast(U32), axis=0), patch[:, :], None,
                    bounds_check=EDGES_PAD - 1, oob_is_err=False).then_inc(patched, 16)
                pool.wait_ge(patched, 16)
                for b in range(BLOCKS):
                    nc.gpsimd.indirect_dma_start(state[:, b, :], None, a["state"], bass.IndirectOffsetOnAxis(
                        ap=k["last_i"][:, b:b + 1].bitcast(U32), axis=0)).then_inc(states_here[b // per_turn], 16)

            @block.scalar
            def _(act):
                act.wait_ge(ex_asked, 1)
                nc.scalar.activation(shrink[:, :], shrink[:, :], ACT.Exp).then_inc(ex_done, 1)
                nc.scalar.activation(gain[:, :], gain[:, :], ACT.Exp).then_inc(ex_done, 1)
                act.wait_ge(ex_asked, 2)
                nc.scalar.activation(ex[:, :, :], ex[:, :, :], ACT.Exp).then_inc(ex_done, 1)
                for i in range(TURNS):
                    act.wait_ge(stage_turned, i + 1)
                    nc.scalar.activation(hT[:, :, :].rearrange("p g n -> p (g n)"),
                                         psT[:, :, :].rearrange("p a n -> p (a n)")[:, 0:BATCH * P],
                                         ACT.Copy).then_inc(hT_ready, 1)
                    act.wait_ge(root_asked, i + 1)
                    nc.scalar.activation(var[:, :], var[:, :], ACT.Sqrt).then_inc(root_done, 1)

            @block.tensor
            def _(pe):
                pe.wait_ge(tail_ready, 1)
                for n in range(3):
                    last = nc.tensor.transpose(psA[0:SUMS, n, :], tail[:, n, :], ident[:, :])
                last.then_inc(turned, 1)
                pe.wait_ge(carry_ready, 1)
                nc.tensor.transpose(psB[:, 0, :], peaks[:, 0:P], ident[0:SUMS, 0:SUMS])
                nc.tensor.transpose(psB[:, 1, :], totals[:, 0:P], ident[0:SUMS, 0:SUMS]).then_inc(carry_back, 1)
                pe.wait_ge(wo_loaded, 16 * GROUP)
                for i in range(TURNS):
                    pe.wait_ge(staged, i + 1)
                    for g in range(BATCH):
                        last = nc.tensor.transpose(psT[:, g // 4, (g % 4) * P:(g % 4 + 1) * P], stage[:, g, :], ident[:, :])
                    last.then_inc(stage_turned, 1)
                    pe.wait_ge(hT_ready, i + 1)
                    for g in range(BATCH):
                        last = nc.tensor.matmul(psM[:, g // 4, (g % 4) * P:(g % 4 + 1) * P], hT[:, g, :],
                                                wo[:, :, :].rearrange("p j c -> p (j c)"), start=True, stop=True)
                    last.then_inc(projected, 1)

            @block.vector
            def _(vec):
                v = nc.vector
                step = chain(vec, vec_done)
                step(v.tensor_copy(tail[:, 0, :].rearrange("p (h c) -> p h c", c=HC), spread(k["peak"][:, :, T], HC)))
                step(v.tensor_copy(tail[:, 1, :], k["sums"][:, :, T]))
                step(v.tensor_copy(tail[:, 2, :], k["whole"][:, :].to_broadcast([P, SUMS])))
                vec.sem_inc(tail_ready, 1)
                vec.wait_ge(turned, 1)
                step(v.tensor_copy(rows[:, :, :], psA[0:SUMS, :, :]))
                step(v.tensor_scalar(rows[:, 2, :], rows[:, 2, :], BIG, -BIG, ALU.mult, ALU.add))
                step(v.memset(peaks[:, 0:1], -BIG))
                step(v.memset(totals[:, 0:1], 0.0))
                step(v.tensor_tensor_scan(peaks[:, 1:P + 1], rows[:, 2, :], rows[:, 0, :], -BIG, ALU.add, ALU.max))
                step(v.tensor_tensor(shrink[:, :], peaks[:, 0:P], rows[:, 2, :], ALU.add))
                step(v.tensor_tensor(shrink[:, :], shrink[:, :], peaks[:, 1:P + 1], ALU.subtract))
                step(v.tensor_tensor(gain[:, :], rows[:, 0, :], peaks[:, 1:P + 1], ALU.subtract))
                vec.sem_inc(ex_asked, 1)
                vec.wait_ge(ex_done, 2)
                step(v.tensor_tensor(gain[:, :], gain[:, :], rows[:, 1, :], ALU.mult))
                step(v.tensor_tensor_scan(totals[:, 1:P + 1], shrink[:, :], gain[:, :], 0.0, ALU.mult, ALU.add))
                vec.sem_inc(carry_ready, 1)
                vec.wait_ge(carry_back, 1)
                step(v.tensor_copy(carry[:, :, :], psB[:, :, :]))
                vec.wait_ge(patch_here, 16)
                pk = spread(patch[:, SUMS:STATE], HC)
                byhead = lambda x: x.rearrange("p (h c) -> p h c", c=HC)
                step(v.tensor_tensor(byhead(top[:, :]), byhead(carry[:, 0, :]), pk, ALU.max))
                step(v.tensor_tensor(byhead(ex[:, 0, :]), pk, byhead(top[:, :]), ALU.subtract))
                step(v.tensor_tensor(ex[:, 1, :], carry[:, 0, :], top[:, :], ALU.subtract))
                vec.sem_inc(ex_asked, 1)
                vec.wait_ge(ex_done, 3)
                step(v.tensor_tensor(mix[:, 0, :], patch[:, 0:SUMS], ex[:, 0, :], ALU.mult))
                step(v.tensor_tensor(mix[:, 1, :], carry[:, 1, :], ex[:, 1, :], ALU.mult))
                step(v.tensor_tensor(patch[:, 0:SUMS], mix[:, 0, :], mix[:, 1, :], ALU.add))
                vec.sem_inc(patch_ready, 1)
                step(v.memset(stage[:, :, :], 0.0))
                step(v.memset(var[:, :], 1.0))
                for i in range(TURNS):
                    b0, nb = i * per_turn, blocks_of(i)
                    at = slice(b0, b0 + nb)
                    vec.wait_ge(states_here[i], 16 * nb)
                    st = state[:, at, 0:SUMS].rearrange("p b (h c) -> p b h c", c=HC)
                    step(v.tensor_scalar(rden[:, 0:nb, :], st[:, :, :, DH], 1e-16, None, ALU.max))
                    step(v.reciprocal(rden[:, 0:nb, :], rden[:, 0:nb, :]))
                    step(v.tensor_tensor(
                        stage[:, :, :].rearrange("p g (j c) -> p (g j) c", j=GROUP)[:, 0:nb, :].rearrange("p b (h c) -> p b h c", c=DH),
                        st[:, :, :, 0:DH],
                        rden[:, 0:nb, :].rearrange("p b (h o) -> p b h o", o=1).to_broadcast([P, nb, HEADS, DH]), ALU.mult))
                    vec.sem_inc(staged, 1)
                    vec.wait_ge(projected, i + 1)
                    step(v.tensor_tensor(k["res"][:, at, :], k["res"][:, at, :],
                                         psM[:, :, :].rearrange("p a (j c) -> p (a j) c", c=D)[:, 0:nb, :], ALU.add))
                    normalise(nc, vec, step, squares[:, 0:nb, :], k["res"][:, at, :], hs[:, at, :], mean[:, 0:nb], var[:, 0:nb],
                              root_asked, root_done, i + 1)
                    vec.sem_inc(h_ready, 1)


def tensor_product(nc, a, k):
    with ExitStack() as ctx:
        sb = lambda name, shape, dt=FP32: ctx.enter_context(nc.sbuf_tensor(name, shape, dt))
        pb = lambda name, shape, dt=FP32: ctx.enter_context(nc.psum_tensor(name, shape, dt))
        sem = lambda name: ctx.enter_context(nc.semaphore(name))
        T1 = T + 1
        GC = SIX * COLS
        w1, b1 = sb("w1", [HID, 1]), sb("b1", [HID, 1])
        wraw, wrad = sb("wraw", [HID + 1, 384]), sb("wrad", [HID + 1, 384])
        hid = [sb(f"hid{b}", [HID + 1, HALF * P]) for b in range(2)]
        src_i = [sb(f"src4_{b}", [P, T], I32) for b in range(2)]
        feat = [sb(f"feat{b}", [P, T, D]) for b in range(2)]
        frame = [sb(f"frame{b}", [P, T, 9]) for b in range(2)]
        ops = [sb(f"ops{b}", [P, T, 3 * JC]) for b in range(2)]
        parts = sb("parts", [P, T, 3, 3 * VU])
        prod = [sb(f"prod{r}", [P, JC, GC]) for r in range(2)]
        red = [sb(f"red{b}", [P, T, COLS]) for b in range(2)]
        seed, same_c, run = sb("seed", [P, D, T1]), sb("same_c4", [P, D, T1]), k["run"]
        out = sb("out4", [P, T, D])
        zrow = sb("zrow4", [1, D])
        ident = k["ident"]
        psR = pb("psR", [P, 2, TRI, 512])
        psS = pb("psS", [P, 2, 512])

        w_loaded, wrad_ready, zrow_set, rows_set = sem("w_loaded4"), sem("wrad_ready"), sem("zrow_set4"), sem("rows_set")
        src_loaded, feat_here, w_here, frame_here = ([sem(f"{n}{b}") for b in range(2)] for n in (
            "src_loaded4", "feat_here", "w_here", "frame_here"))
        feat_free, frame_free, stored = sem("feat_free"), sem("frame_free4"), sem("stored4")
        hid_free = [sem(f"hid_free{h}") for h in range(2)]
        hid_ready = [sem(f"hid_ready{h}") for h in range(2)]
        radial_ready, prod_done, prod_ready, sum_ready, sum_free = (sem(n) for n in (
            "radial_ready", "prod_done", "prod_ready", "sum_ready", "sum_free"))
        ops_copied, turned_ready, turned_copied, ops_free, flags_ready, red_free, scanned, run_copied = (sem(n) for n in (
            "ops_copied", "turned_ready", "turned_copied", "ops_free", "flags_ready4", "red_free", "scanned", "run_copied"))
        seeded, vec_done, chunk_begun = sem("seeded"), sem("vec_done4"), sem("chunk_begun4")

        with nc.Block() as block:

            @block.sync
            def _(sp):
                sp.dma_start(w1[:, :], a["w1"]).then_inc(w_loaded, 16)
                sp.dma_start(b1[:, :], a["b1"]).then_inc(w_loaded, 16)
                sp.dma_start(wraw[0:HID, :], a["w2"]).then_inc(w_loaded, 16)
                sp.dma_start(wraw[HID:HID + 1, :], a["b2"]).then_inc(w_loaded, 16)
                sources = a["src"].rearrange("(p s) -> p s", s=SLOTS)
                frames = a["frame"].rearrange("(p s) c -> p (s c)", s=SLOTS)

                def load_src(b, at):
                    sp.dma_start(src_i[b][:, :], sources[:, bass.ds(at, T)]).then_inc(src_loaded[b], 16)

                def load_frame(b, at):
                    sp.dma_start(frame[b][:, :, :].rearrange("p t c -> p (t c)"), frames[:, bass.ds(at * 9, 9 * T)]).then_inc(frame_here[b], 16)

                def load_w(h, at):
                    sp.dma_start(hid[h][0:HID, :], a["wT"][bass.ds(at, HALF * P)].rearrange("(o n) -> o n", o=1).to_broadcast([HID, HALF * P])
                                 ).then_inc(w_here[h], 16)

                load_src(0, 0)
                load_src(1, T)
                load_w(0, 0)
                load_w(1, HALF * P)
                load_frame(0, 0)
                load_frame(1, T)

                def body(i, last):
                    for b in range(2):
                        c1 = i * 2 + b + 1
                        if not last:
                            sp.wait_ge(feat_here[b], i * (16 * T) + 16 * T)
                            load_src(b, i * (2 * T) + (b + 2) * T)
                        if not (last and b == 1):
                            for h in range(2):
                                sp.wait_ge(hid_free[h], c1)
                                load_w(h, i * (2 * T * P) + ((b + 1) * T + h * HALF) * P)
                        if not last:
                            sp.wait_ge(frame_free, c1)
                            load_frame(b, i * (2 * T) + (b + 2) * T)
                pairs(sp, body)

            @block.gpsimd
            def _(pool):
                with pool.Fori(0, PAIRS) as i:
                    for b in range(2):
                        pool.wait_ge(src_loaded[b], i * 16 + 16)
                        pool.wait_ge(feat_free, i * 2 + b + 1)
                        pool.sem_inc(chunk_begun, 1)
                        for t in range(T):
                            nc.gpsimd.indirect_dma_start(
                                feat[b][:, t, :], None, a["h2"],
                                bass.IndirectOffsetOnAxis(ap=src_i[b][:, t:t + 1].bitcast(U32), axis=0)).then_inc(feat_here[b], 16)

            @block.tensor
            def _(pe):
                def radial(c, g):
                    h, g0 = (0, 0) if g * TRI < HALF else (1, HALF // TRI)
                    if g == g0:
                        pe.wait_ge(hid_ready[h], c + 1)
                    pe.wait_ge(prod_done, 3 * (c * GPC + g) + 3)
                    for t in range(TRI):
                        at = ((g - g0) * TRI + t) * P
                        last_mm = nc.tensor.matmul(psR[:, g % 2, t, 0:384], hid[h][:, at:at + P], wrad[:, :], start=True, stop=True)
                    last_mm.then_inc(radial_ready, 1)
                    if (g + 1) * TRI in (HALF, T):
                        pe.wait_ge(radial_ready, c * GPC + g + 1)
                        pe.sem_inc(hid_free[h], 1)

                def sums(c, b, s):
                    r, q = (b * SPC + s) % 2, c * SPC + s
                    pe.wait_ge(sum_free, q + 1)
                    pe.wait_ge(prod_done, q * 6 + 12)
                    order = [j for j in range(FOLD, JC) if not JC // 2 <= j < JC // 2 + FOLD]
                    for n, j in enumerate(order):
                        nc.tensor.matmul(psS[:, r, 0:GC], ident[:, :], prod[r][:, j, :], start=(n == 0), stop=False)
                    pe.wait_ge(prod_ready, q + 1)
                    for j in range(FOLD):
                        last_mm = nc.tensor.matmul(psS[:, r, 0:GC], ident[:, :], prod[r][:, j, :], start=False, stop=(j == FOLD - 1))
                    last_mm.then_inc(sum_ready, 1)

                pe.wait_ge(wrad_ready, 1)
                radial(0, 0)
                radial(0, 1)

                def body(i, last):
                    for b in range(2):
                        for s in range(SPC):
                            for g in (2 * s + 2, 2 * s + 3):
                                if g < GPC:
                                    radial(i * 2 + b, g)
                                elif not (last and b == 1):
                                    radial(i * 2 + b + 1, g - GPC)
                            sums(i * 2 + b, b, s)
                pairs(pe, body)

            @block.scalar
            def _(act):
                act.wait_ge(zrow_set, 1)
                act.dma_start(a["state2"][EDGES_PAD:EDGES_PAD + 1, :], zrow[:, :]).then_inc(stored, 16)
                act.wait_ge(w_loaded, 64)

                def hidden(h, c):
                    act.wait_ge(w_here[h], c * 16 + 16)
                    nc.scalar.activation(hid[h][0:HID, :], hid[h][0:HID, :], ACT.Relu, bias=b1[:, :], scale=w1[:, :]).then_inc(hid_ready[h], 1)

                def scalars(b, c):
                    act.wait_ge(feat_here[b], (c - b) * (8 * T) + 16 * T)
                    act.wait_ge(ops_free, c + 1)
                    nc.scalar.activation(ops[b][:, :, 0:VU], feat[b][:, :, 0:VU], ACT.Copy).then_inc(ops_copied, 1)

                def turned(b, c):
                    act.wait_ge(turned_ready, c + 1)
                    nc.scalar.activation(ops[b][:, :, JC:JC + VU], ops[b][:, :, 2 * JC + VU:3 * JC], ACT.Copy, scale=-1.0).then_inc(turned_copied, 1)
                    nc.scalar.activation(ops[b][:, :, 2 * JC:2 * JC + VU], ops[b][:, :, JC + VU:2 * JC], ACT.Copy).then_inc(turned_copied, 1)

                def seed_scalars(b, c):
                    act.wait_ge(sum_free, c * SPC + SPC + 2)
                    act.wait_ge(scanned, c * 2 + 1)
                    nc.scalar.activation(seed[:, 0:VU, 1:T1], red[b][:, :, 0:VU].rearrange("p t u -> p u t"), ACT.Copy).then_inc(seeded, 1)

                def flags(c, at):
                    act.wait_ge(scanned, c * 2 + 1)
                    nc.scalar.activation(same_c[:, :, 1:T1], spread_front(k["same"][:, bass.ds(at, T)], D), ACT.Copy).then_inc(flags_ready, 1)

                def store(c, at):
                    act.wait_ge(scanned, c * 2 + 3)
                    act.wait_ge(stored, c * 16 + 16)
                    nc.scalar.activation(out[:, :, :], run[:, :, 1:T1].rearrange("p c t -> p t c"), ACT.Copy).then_inc(run_copied, 1)
                    act.wait_ge(run_copied, c + 2)
                    act.dma_start(a["state2"][0:EDGES_PAD, :].rearrange("(p s) c -> p (s c)", s=SLOTS)[:, bass.ds(at * D, T * D)],
                                  out[:, :, :].rearrange("p t c -> p (t c)")).then_inc(stored, 16)

                act.wait_ge(rows_set, 1)
                hidden(0, 0)
                hidden(1, 0)
                scalars(0, 0)
                turned(0, 0)

                def body(i, first, last):
                    for b in range(2):
                        c = i * 2 + b
                        at = i * (2 * T) + b * T
                        more = not (last and b == 1)
                        for s in range(SPC):
                            if s == 0:
                                act.wait_ge(red_free, c + 1)
                            act.wait_ge(sum_ready, c * SPC + s + 1)
                            nc.scalar.activation(red[b][:, s * SIX:(s + 1) * SIX, :].rearrange("p t c -> p (t c)"),
                                                 psS[:, (b * SPC + s) % 2, 0:GC], ACT.Copy).then_inc(sum_free, 1)
                            if s == 0 and not (first and b == 0):
                                seed_scalars(1 - b, c - 1)
                            if s == 1 and more:
                                scalars(1 - b, c + 1)
                            if s == 5 and not (first and b == 0):
                                store(c - 1, at - T)
                            if s == 5:
                                flags(c, at)
                                if more:
                                    hidden(0, c + 1)
                            if s == 7 and more:
                                turned(1 - b, c + 1)
                        if more:
                            hidden(1, c + 1)
                pairs_apart(act, body)
                seed_scalars(1, CHUNKS - 1)
                store(CHUNKS - 1, SLOTS - T)
                act.wait_ge(stored, 16 * (CHUNKS + 1))

            @block.vector
            def _(vec):
                v = nc.vector
                step = chain(vec, vec_done)
                step(v.memset(zrow[:, :], 0.0))
                vec.sem_inc(zrow_set, 1)
                for h in range(2):
                    step(v.memset(hid[h][HID:HID + 1, :], 1.0))
                step(v.memset(same_c[:, :, 0:1], 0.0))
                step(v.memset(run[:, :, T:T1], 0.0))
                vec.sem_inc(rows_set, 1)
                for primed, n in ((feat_free, 2), (prod_done, 6), (sum_free, 2), (ops_free, 2),
                                  (red_free, 2), (scanned, 1), (run_copied, 1)):
                    vec.sem_inc(primed, n)
                vec.wait_ge(w_loaded, 64)
                raw = lambda lo, n: wraw[:, lo:lo + n].rearrange("p (u v) -> p u v", u=VU)
                r11 = wraw[:, 192:384].rearrange("p (u v f) -> p u v f", u=VU, f=3)
                new = wrad[:, :].rearrange("p (u j) -> p u j", j=JC)
                along, across = new[:, VU:2 * VU, VU:JC], new[:, 2 * VU:3 * VU, VU:JC]
                for to, frm, coef in (
                        (new[:, 0:VU, 0:VU], raw(0, 64), N0 * C0),
                        (new[:, 0:VU, VU:JC], raw(64, 64), N0 * C1 / sqrt(3.0)),
                        (new[:, VU:2 * VU, 0:VU], raw(128, 64), N1 * C1 / sqrt(3.0)),
                        (new[:, 2 * VU:3 * VU, 0:VU], r11[:, :, :, 1], N1 * C1 / sqrt(6.0)),
                        (along, r11[:, :, :, 2], N1 * C2 * 2.0 / 3.0),
                        (across, r11[:, :, :, 2], -N1 * C2 / 3.0)):
                    step(v.tensor_scalar(to, frm, coef, None, ALU.mult))
                for to in (along, across):
                    step(v.scalar_tensor_tensor(out=to, in0=r11[:, :, :, 0], scalar=N1 * C0 / sqrt(3.0), in1=to, op0=ALU.mult, op1=ALU.add))
                vec.sem_inc(wrad_ready, 1)

                def components(step, b, c, n):
                    if n < 3:
                        if n == 0:
                            vec.wait_ge(feat_here[b], (c - b) * (8 * T) + 16 * T)
                            vec.wait_ge(frame_here[b], (c - b) * 8 + 16)
                        step(v.tensor_tensor(parts[:, :, n, :].rearrange("p t (i v) -> p t i v", i=3),
                                             feat[b][:, :, VU:D].rearrange("p t (v i) -> p t i v", i=3),
                                             frame[b][:, :, 3 * n:3 * n + 3].rearrange("p t (i o) -> p t i o", o=1).to_broadcast([P, T, 3, VU]), ALU.mult), hold=False)
                        return
                    step.settle()
                    if n == 3:
                        vec.wait_ge(ops_copied, c + 1)
                        vec.sem_inc(feat_free, 1)
                    term = lambda i: parts[:, :, :, i * VU:(i + 1) * VU]
                    to = ops[b][:, :, :].rearrange("p t (x j) -> p t x j", x=3)[:, :, :, VU:JC]
                    if n == 3:
                        step(v.tensor_tensor(term(0), term(0), term(1), ALU.add), hold=False)
                    else:
                        v.tensor_tensor(to, term(0), term(2), ALU.add).then_inc(turned_ready, 1)

                def products(b, c, s):
                    r, q = (b * SPC + s) % 2, c * SPC + s
                    vec.wait_ge(sum_free, q + 1)
                    if s == 0:
                        vec.wait_ge(turned_ready, c + 1)
                    for half in range(2):
                        g = 2 * s + half
                        ts = slice(g * TRI, (g + 1) * TRI)
                        vec.wait_ge(radial_ready, c * GPC + g + 1)
                        to = prod[r][:, :, :].rearrange("p j (t c) -> p t c j", c=COLS)[:, half * TRI:(half + 1) * TRI, :, :]
                        for lo, n, frm in ((0, 2 * VU, 0), (2 * VU, VU, 256), (3 * VU, VU, 256)):
                            x = max(0, lo // VU - 1)
                            if s == 0 and half == 0 and x == 1:
                                vec.wait_ge(turned_copied, c * 2 + 2)
                            v.tensor_tensor(to[:, :, lo:lo + n, :], psR[:, g % 2, :, frm:frm + n * JC].rearrange("p t (u j) -> p t u j", j=JC),
                                            ops[b][:, ts, x * JC:(x + 1) * JC].rearrange("p t (o j) -> p t o j", o=1).to_broadcast([P, TRI, n, JC]),
                                            ALU.mult).then_inc(prod_done, 1)

                def fold(b, c, s):
                    r, q = (b * SPC + s) % 2, c * SPC + s
                    vec.wait_ge(prod_done, q * 6 + 12)
                    v.tensor_tensor(prod[r][:, 0:FOLD, :], prod[r][:, 0:FOLD, :], prod[r][:, JC // 2:JC // 2 + FOLD, :], ALU.add).then_inc(prod_ready, 1)

                def finish(step, b, c, n):
                    flat = lambda x, lo, hi: x[:, lo:hi, :].rearrange("p c t -> p (c t)")
                    if n < 3:
                        if n == 0:
                            vec.wait_ge(sum_free, c * SPC + SPC + 2)
                        step(v.tensor_tensor(parts[:, :, n, :].rearrange("p t (o u) -> p t o u", o=3),
                                             red[b][:, :, (n + 1) * VU:(n + 2) * VU].rearrange("p t (o u) -> p t o u", o=1).to_broadcast([P, T, 3, VU]),
                                             frame[b][:, :, 3 * n:3 * n + 3].rearrange("p t (i o) -> p t i o", o=1).to_broadcast([P, T, 3, VU]), ALU.mult), hold=False)
                        return
                    step.settle()
                    if n == 3:
                        vec.sem_inc(frame_free, 1)
                        vec.sem_inc(red_free, 1)
                        step(v.tensor_tensor(parts[:, :, 0, :], parts[:, :, 0, :], parts[:, :, 1, :], ALU.add), hold=False)
                    elif n == 4:
                        vec.wait_ge(scanned, c * 2 + 1)
                        step(v.tensor_copy(seed[:, :, 0], run[:, :, T]), hold=False)
                        step(v.tensor_tensor(seed[:, VU:D, 1:T1].rearrange("p (u o) t -> p t o u", o=3),
                                             parts[:, :, 0, :].rearrange("p t (o u) -> p t o u", o=3),
                                             parts[:, :, 2, :].rearrange("p t (o u) -> p t o u", o=3), ALU.add), hold=False)
                    else:
                        if n == 5:
                            vec.wait_ge(seeded, c + 1)
                            vec.wait_ge(flags_ready, c + 1)
                            vec.wait_ge(run_copied, c + 1)
                        lo = (n - 5) * (D // 2)
                        v.tensor_tensor_scan(flat(run, lo, lo + D // 2), flat(same_c, lo, lo + D // 2),
                                             flat(seed, lo, lo + D // 2), 0.0, ALU.mult, ALU.add).then_inc(scanned, 1)

                for n in range(5):
                    components(step, 0, 0, n)
                base, per_chunk = step.count[0], 10
                of_finish = 6
                before = {1: (0,), 2: (1, 2), 3: (3, 4), 4: (5,), 5: (6,)}
                ahead = {5: (0,), 6: (1,), 7: (2, 3), 8: (4,)}

                def body(i, first, last):
                    step = chain(vec, vec_done, base + i * (2 * per_chunk) - (0 if first else of_finish))
                    for b in range(2):
                        c = i * 2 + b
                        for s in range(SPC):
                            products(b, c, s)
                            if not (first and b == 0):
                                for n in before.get(s, ()):
                                    finish(step, 1 - b, c - 1, n)
                            if not (last and b == 1):
                                for n in ahead.get(s, ()):
                                    components(step, 1 - b, c + 1, n)
                            fold(b, c, s)
                        vec.sem_inc(ops_free, 1)
                pairs_apart(vec, body)
                step = chain(vec, vec_done, base + (CHUNKS - 1) * per_chunk)
                for n in range(7):
                    finish(step, 1, CHUNKS - 1, n)
                vec.wait_ge(run_copied, CHUNKS + 1)


def node_sums(nc, a, k):
    with ExitStack() as ctx:
        sb = lambda name, shape, dt=FP32: ctx.enter_context(nc.sbuf_tensor(name, shape, dt))
        pb = lambda name, shape, dt=FP32: ctx.enter_context(nc.psum_tensor(name, shape, dt))
        sem = lambda name: ctx.enter_context(nc.semaphore(name))
        per_turn = BATCH * GROUP
        blocks_of = lambda i: min(per_turn, BLOCKS - i * per_turn)
        tail, rows = sb("tail5", [P, 2, D]), sb("rows5", [D, 2, P])
        totals = sb("totals5", [D, P + 1])
        patch = sb("patch5", [P, D])
        state = sb("state5", [P, BLOCKS, D])
        psA, psB = pb("psA5", [P, 2, P]), pb("psB5", [P, D])
        tail_ready, turned, carry_ready, carry_back, patch_here, patch_ready, patched, x_ready, x_stored, vec_done = (
            sem(n) for n in ("tail_ready5", "turned5", "carry_ready5", "carry_back5", "patch_here5", "patch_ready5",
                             "patched5", "x_ready", "x_stored", "vec_done5"))
        sums_here = [sem(f"sums_here{i}") for i in range(TURNS)]

        with nc.Block() as block:

            @block.sync
            def _(sp):
                for i in range(TURNS):
                    sp.wait_ge(x_ready, i + 1)
                    b0 = i * per_turn
                    sp.dma_start(a["out"].rearrange("(p b) c -> p b c", b=BLOCKS)[:, b0:b0 + blocks_of(i), :],
                                 state[:, b0:b0 + blocks_of(i), :]).then_inc(x_stored, 16)
                sp.wait_ge(x_stored, 16 * TURNS)

            @block.gpsimd
            def _(pool):
                nc.gpsimd.indirect_dma_start(patch[:, :], None, a["state2"], bass.IndirectOffsetOnAxis(
                    ap=k["end_i"][:, :].bitcast(U32), axis=0)).then_inc(patch_here, 16)
                pool.wait_ge(patch_ready, 1)
                nc.gpsimd.indirect_dma_start(a["state2"], bass.IndirectOffsetOnAxis(
                    ap=k["patch_i"][:, :].bitcast(U32), axis=0), patch[:, :], None,
                    bounds_check=EDGES_PAD - 1, oob_is_err=False).then_inc(patched, 16)
                pool.wait_ge(patched, 16)
                for b in range(BLOCKS):
                    nc.gpsimd.indirect_dma_start(state[:, b, :], None, a["state2"], bass.IndirectOffsetOnAxis(
                        ap=k["last_i"][:, b:b + 1].bitcast(U32), axis=0)).then_inc(sums_here[b // per_turn], 16)

            @block.tensor
            def _(pe):
                pe.wait_ge(tail_ready, 1)
                nc.tensor.transpose(psA[0:D, 0, :], tail[:, 0, :], k["ident"][:, :])
                nc.tensor.transpose(psA[0:D, 1, :], tail[:, 1, :], k["ident"][:, :]).then_inc(turned, 1)
                pe.wait_ge(carry_ready, 1)
                nc.tensor.transpose(psB[:, :], totals[:, 0:P], k["ident"][0:D, 0:D]).then_inc(carry_back, 1)

            @block.vector
            def _(vec):
                v = nc.vector
                step = chain(vec, vec_done)
                step(v.tensor_copy(tail[:, 0, :], k["run"][:, :, T]))
                step(v.tensor_copy(tail[:, 1, :], k["whole"][:, :].to_broadcast([P, D])))
                vec.sem_inc(tail_ready, 1)
                vec.wait_ge(turned, 1)
                step(v.tensor_copy(rows[:, :, :], psA[0:D, :, :]))
                step(v.memset(totals[:, 0:1], 0.0))
                step(v.tensor_tensor_scan(totals[:, 1:P + 1], rows[:, 1, :], rows[:, 0, :], 0.0, ALU.mult, ALU.add))
                vec.sem_inc(carry_ready, 1)
                vec.wait_ge(carry_back, 1)
                vec.wait_ge(patch_here, 16)
                step(v.tensor_tensor(patch[:, :], patch[:, :], psB[:, :], ALU.add))
                vec.sem_inc(patch_ready, 1)
                for i in range(TURNS):
                    b0, nb = i * per_turn, blocks_of(i)
                    at = slice(b0, b0 + nb)
                    vec.wait_ge(sums_here[i], 16 * nb)
                    step(v.tensor_tensor(state[:, at, :], state[:, at, :], k["res"][:, at, :], ALU.add))
                    vec.sem_inc(x_ready, 1)


def gnn_kernel(nc, a):
    with ExitStack() as ctx:
        sb = lambda name, shape, dt=FP32: ctx.enter_context(nc.sbuf_tensor(name, shape, dt))
        k = {
            "ident": sb("ident", [P, P]),
            "res": sb("res", [P, BLOCKS, D]),
            "q_first": sb("q_first", [P, D]),
            "last_i": sb("last_i", [P, BLOCKS], I32),
            "whole": sb("whole", [P, 1]),
            "end_i": sb("end_i", [P, 1], I32),
            "patch_i": sb("patch_i", [P, 1], I32),
        }
        prologue(nc, a, k)
        k["same"] = sb("same_all", [P, SLOTS])
        with ExitStack() as states:
            k["peak"] = states.enter_context(nc.sbuf_tensor("peak", [P, HEADS, T + 1], FP32))
            k["sums"] = states.enter_context(nc.sbuf_tensor("sums", [P, SUMS, T + 1], FP32))
            attention(nc, a, k)
            node_attention(nc, a, k)
        k["run"] = sb("run", [P, D, T + 1])
        tensor_product(nc, a, k)
        node_sums(nc, a, k)


def kernel(x, src, dst, edge_attr_3, edge_weight, L0_gnn_Wq, L0_gnn_Wk, L0_gnn_Wv, L0_gnn_Wo,
           L1_gnn_w1, L1_gnn_b1, L1_gnn_w2, L1_gnn_b2):
    import numpy as np
    import concourse.bacc as bacc
    from concourse.bass_utils import run_bass_kernel_spmd

    def padded(array, rows, value=0):
        array = np.asarray(array)
        fill = np.full((rows - array.shape[0],) + array.shape[1:], value, array.dtype)
        return np.ascontiguousarray(np.concatenate([array, fill]))

    dst_pad = padded(dst, EDGES_PAD, NODES)
    weights = padded(edge_weight, EDGES_PAD).reshape(P, SLOTS)
    arrays = {
        "x": padded(x, NODES_PAD),
        "src": padded(src, EDGES_PAD),
        "dst": dst_pad,
        "dst_ext": np.concatenate([np.full(1, -1, dst_pad.dtype), dst_pad]),
        "dst_rows": dst_pad.reshape(-1, ROWW),
        "samples": np.ascontiguousarray(dst_pad[::ROWW].reshape(SP_, SC_)),
        "attr": padded(edge_attr_3, EDGES_PAD, 1),
        "wT": np.ascontiguousarray(weights.T).reshape(-1),
        "wq": np.asarray(L0_gnn_Wq), "wk": np.asarray(L0_gnn_Wk), "wv": np.asarray(L0_gnn_Wv), "wo": np.asarray(L0_gnn_Wo),
        "w1": np.asarray(L1_gnn_w1).reshape(HID, 1), "b1": np.asarray(L1_gnn_b1).reshape(HID, 1),
        "w2": np.asarray(L1_gnn_w2), "b2": np.asarray(L1_gnn_b2).reshape(1, -1),
    }
    nc = bacc.Bacc("TRN2", target_bir_lowering=False, num_devices=1)
    a = {n: nc.dram_tensor(f"in_{n}", v.shape, mybir.dt.from_np(v.dtype), kind="ExternalInput").ap() for n, v in arrays.items()}
    for name, shape in (("kv", (NODES_PAD, 2 * D)), ("q", (NODES_PAD, D)), ("qexp", (EDGES_PAD, D)), ("ptr", (NODES_PAD, 2)),
                        ("state", (EDGES_PAD + 2, STATE)), ("h2", (NODES_PAD, D)), ("frame", (EDGES_PAD, 9)), ("state2", (EDGES_PAD + 1, D))):
        a[name] = nc.dram_tensor(f"scratch_{name}", shape, FP32, kind="Internal").ap()
    a["out"] = nc.dram_tensor("out_x", (NODES_PAD, D), FP32, kind="ExternalOutput").ap()
    gnn_kernel(nc, a)
    result = run_bass_kernel_spmd(nc, [{f"in_{n}": v for n, v in arrays.items()}], core_ids=[0])
    return result.results[0]["out_x"][:NODES]
```

```python
from contextlib import ExitStack
from math import pi, sqrt

import concourse.bass as bass
from concourse import mybir

FP32 = mybir.dt.float32
BF16 = mybir.dt.bfloat16
FP16 = mybir.dt.float16
I32 = mybir.dt.int32
U32 = mybir.dt.uint32
ALU = mybir.AluOpType
ACT = mybir.ActivationFunctionType
AX = mybir.AxisListType

P = 128
NODES, EDGES, D = 12500, 400000, 32
HEADS, DH = 4, 8
BLOCKS = 98
NODES_PAD = P * BLOCKS
GROUP = 4
BLOCKS_UP = 100
BATCH = 5
TURNS = BLOCKS_UP // (GROUP * BATCH)

T = 54
SLOTS = 3132
CHUNKS = SLOTS // T
PAIRS = CHUNKS // 2
EDGES_PAD = P * SLOTS
TRI = 3
SIX = 2 * TRI
PACKS = 3
PACK = T // PACKS
HALF = PACK // 2 * P
TOP = float(1 << 14)
GPC = T // TRI
SPC = T // SIX

ROWW = 128
SP_, SC_ = 116, 27
BB = BLOCKS + 1
PARTS = 9
PART = BB // PARTS

STATE = 40
HC = DH + 1
SUMS = HEADS * HC
HID = 64
VU = 8
JC = 16
COLS = 32
FOLDS = (3, 2, 3, 2, 3, 3, 2, 3, 2)
BIG = 1.0e30
FAR = float(1 << 22)

C0 = 0.5 / sqrt(pi)
C1 = sqrt(3.0 / (4.0 * pi))
C2 = sqrt(3.0 / (8.0 * pi))
N0 = sqrt(4.0 * pi) / sqrt(16.0)
N1 = sqrt(4.0 * pi) * sqrt(3.0) / sqrt(32.0)

assert CHUNKS * T == SLOTS and 2 * PAIRS == CHUNKS and GPC * TRI == T and SP_ * SC_ * ROWW == EDGES_PAD


def spread(ap, n):
    return ap.rearrange("p (a o) -> p a o", o=1).to_broadcast([ap.shape[0], ap.shape[1], n])


def spread_front(ap, n):
    return ap.rearrange("p (o a) -> p o a", o=1).to_broadcast([ap.shape[0], n, ap.shape[1]])


def chain(engine, done, base=0):
    count = [0]

    def settle():
        engine.wait_ge(done, base + count[0])

    def step(instruction, hold=True):
        count[0] += 1
        instruction.then_inc(done, 1)
        if hold:
            settle()
    step.count, step.settle = count, settle
    return step


def pairs(engine, body):
    with engine.Fori(0, PAIRS - 1) as i:
        body(i, False)
    body(PAIRS - 1, True)


def pairs_apart(engine, body):
    body(0, True, False)
    with engine.Fori(1, PAIRS - 1) as i:
        body(i, False, False)
    body(PAIRS - 1, False, True)


def build_identity(pool, step, ident):
    step(pool.memset(ident[:, :], 0.0))
    step(pool.affine_select(out=ident[:, :], in_=ident[:, :], compare_op=ALU.not_equal, fill=1.0,
                            base=0, pattern=[[-1, P]], channel_multiplier=1))


def normalise(nc, vec, step, squares, x, h, mean, var, root_asked, root_done, asked):
    step(nc.vector.tensor_reduce(mean[:, :], x, axis=AX.X, op=ALU.add))
    step(nc.vector.tensor_scalar(mean[:, :], mean[:, :], 1.0 / D, None, ALU.mult))
    step(nc.vector.tensor_tensor(h, x, spread(mean[:, :], D), ALU.subtract))
    step(nc.vector.tensor_tensor(squares, h, h, ALU.mult))
    step(nc.vector.tensor_reduce(var[:, :], squares, axis=AX.X, op=ALU.add))
    step(nc.vector.tensor_scalar(var[:, :], var[:, :], 1.0 / D, 1e-5, ALU.mult, ALU.add))
    vec.sem_inc(root_asked, 1)
    vec.wait_ge(root_done, asked)
    step(nc.vector.reciprocal(var[:, :], var[:, :]))
    step(nc.vector.scalar_tensor_tensor(out=h, in0=h, scalar=0.0, in1=spread(var[:, :], D),
                                        op0=ALU.max, op1=ALU.mult))


def prologue(nc, a, k):
    with ExitStack() as ctx:
        sb = lambda name, shape, dt=FP32: ctx.enter_context(nc.sbuf_tensor(name, shape, dt))
        pb = lambda name, shape, dt=FP32: ctx.enter_context(nc.psum_tensor(name, shape, dt))
        sem = lambda name: ctx.enter_context(nc.semaphore(name))
        xs = sb("xs", [P, BLOCKS, D])
        hs = sb("hs", [P, BLOCKS_UP, D])
        scratch = sb("scratch", [P, BLOCKS, D])
        zeros = sb("zeros", [P, SLOTS])
        mean, var = sb("mean", [P, BLOCKS]), sb("var", [P, BLOCKS])
        wqkv = sb("wqkv", [P, GROUP, 3 * D])
        stage = sb("stage", [P, BATCH, P])
        hT = sb("hT", [P, BATCH, P])
        kv = sb("kv", [P, BLOCKS_UP, 2 * D])
        q = sb("q", [P, BLOCKS_UP, D])
        samp_i, samp = sb("samp_i", [SP_, SC_], I32), sb("samp", [SP_, SC_])
        starts_i, starts = sb("starts_i", [SP_, P + 1], I32), sb("starts", [SP_, P + 1])
        lows_i, lows = sb("lows_i", [SP_, BB], I32), sb("lows", [SP_, BB])
        above = sb("above", [SP_, SC_, P + 1], BF16)
        here = sb("here", [SP_, SC_, P], BF16)
        less = sb("less", [SP_, SC_, BB], BF16)
        ones = sb("ones", [SP_, BB], BF16)
        part = sb("part", [SP_, SC_])
        nid_i, nid = sb("nid_i", [P, BB], I32), sb("nid", [P, BB])
        row, row_i = sb("row", [P, BB]), sb("row_i", [P, BB], I32)
        drow = sb("drow", [P, BB, ROWW], I32)
        below = sb("below", [P, BB // PARTS, ROWW], BF16)
        ptr = sb("ptr", [P, BB])
        some = sb("some", [P, BLOCKS])
        first_at, first_i = sb("first_at", [P, BLOCKS]), sb("first_i", [P, BLOCKS], I32)
        last_at = sb("last_at", [P, BLOCKS])
        pair = sb("pair", [P, BLOCKS, 2])
        mine_i, mine = sb("mine_i", [P, 1], I32), sb("mine", [P, 1])
        edge_i, last_dst, prev_dst = sb("edge_i", [P, 1], I32), sb("last_dst", [P, 1], I32), sb("prev_dst", [P, 1], I32)
        own = sb("own", [P, 2])
        cross = sb("cross", [P, 3])
        ident = k["ident"]
        psT = pb("psT", [P, 2, 512])
        psM = pb("psM", [P, BATCH, 512])
        psC = pb("psC", [P, 512])

        x_loaded, w_loaded, samp_loaded = sem("x_loaded"), sem("w_loaded"), sem("samp_loaded")
        wblk_cleared, zeros_set, q_filled = sem("wblk_cleared"), sem("zeros_set"), sem("q_filled")
        pool_done, vec_done, act_done = sem("pool_done"), sem("vec_done"), sem("act_done")
        consts_ready, root_asked, root_done = sem("consts_ready"), sem("root_asked"), sem("root_done")
        staged, turned, hT_ready, projected, q_out, kv_out = (sem(n) for n in (
            "staged", "turned", "hT_ready", "projected", "q_out", "kv_out"))
        onehots, counted, rows_asked, ends_loaded = (sem(n) for n in ("onehots", "counted", "rows_asked", "ends_loaded"))
        rows_here = [sem(f"rows_here{i}") for i in range(PARTS)]
        first_asked, q_spread, tables, ptr_out, table_asked = (sem(n) for n in (
            "first_asked", "q_spread", "tables", "ptr_out", "table_asked"))
        own_here, qfirst_here, lns = sem("own_here"), sem("qfirst_here"), sem("lns")
        hT_free = sem("hT_free")

        with nc.Block() as block:

            @block.sync
            def _(sp):
                sp.dma_start(samp_i[:, :], a["samples"]).then_inc(samp_loaded, 16)
                sp.dma_start(xs[:, :, :], a["x"].rearrange("(p b) c -> p b c", b=BLOCKS)).then_inc(x_loaded, 16)
                sp.wait_ge(wblk_cleared, 1)
                for j in range(GROUP):
                    for n, w in enumerate(("wq", "wk", "wv")):
                        sp.dma_start(wqkv[j * D:(j + 1) * D, j, n * D:(n + 1) * D], a[w]).then_inc(w_loaded, 16)
                dst = a["dst"].rearrange("(p s) -> p s", s=SLOTS)
                with nc.allow_non_contiguous_dma(reason="one word per partition"):
                    sp.dma_start(mine_i[:, :], dst[:, 0:1]).then_inc(ends_loaded, 16)
                    sp.dma_start(last_dst[:, :], dst[:, SLOTS - 1:SLOTS]).then_inc(ends_loaded, 16)
                    sp.dma_start(prev_dst[:, :], a["dst_ext"][0:EDGES_PAD].rearrange("(p s) -> p s", s=SLOTS)[:, 0:1]).then_inc(ends_loaded, 16)
                sp.wait_ge(q_out, TURNS)
                sp.wait_ge(kv_out, TURNS)
                sp.dma_start(a["kv"].rearrange("(p b) c -> p b c", b=BLOCKS), kv[:, 0:BLOCKS, :]).then_inc(tables, 16)
                sp.dma_start(a["q"].rearrange("(p b) c -> p b c", b=BLOCKS), q[:, 0:BLOCKS, :]).then_inc(tables, 16)
                sp.wait_ge(table_asked, 1)
                sp.dma_start(a["ptr"].rearrange("(p b) c -> p b c", b=BLOCKS), pair[:, :, :]).then_inc(ptr_out, 16)
                sp.wait_ge(tables, 32)
                sp.wait_ge(ptr_out, 16)

            @block.gpsimd
            def _(pool):
                step = chain(pool, pool_done)
                nc.gpsimd.iota(starts_i[:, :], pattern=[[BLOCKS, P + 1]], base=0, channel_multiplier=0).then_inc(consts_ready, 1)
                nc.gpsimd.iota(lows_i[:, :], pattern=[[1, BB]], base=0, channel_multiplier=0).then_inc(consts_ready, 1)
                nc.gpsimd.iota(nid_i[:, :], pattern=[[1, BB]], base=0, channel_multiplier=BLOCKS).then_inc(consts_ready, 1)
                nc.gpsimd.iota(edge_i[:, :], pattern=[[0, 1]], base=0, channel_multiplier=SLOTS).then_inc(consts_ready, 1)
                nc.gpsimd.memset(ones[:, :], 1.0).then_inc(consts_ready, 1)
                step(nc.gpsimd.memset(zeros[:, :], 0.0))
                pool.sem_inc(zeros_set, 1)
                step(nc.gpsimd.memset(wqkv[:, :, :], 0.0))
                pool.sem_inc(wblk_cleared, 1)
                build_identity(nc.gpsimd, step, ident)
                pool.wait_ge(rows_asked, 1)
                for b in range(BB):
                    nc.gpsimd.indirect_dma_start(
                        drow[:, b, :], None, a["dst_rows"],
                        bass.IndirectOffsetOnAxis(ap=row_i[:, b:b + 1].bitcast(U32), axis=0),
                    ).then_inc(rows_here[b // PART], 16)
                pool.wait_ge(q_filled, 16 * D)
                pool.wait_ge(q_out, TURNS)
                for b in range(BLOCKS):
                    if b == BLOCKS - 10:
                        pool.wait_ge(ends_loaded, 48)
                        pool.wait_ge(ptr_out, 16)
                        pool.wait_ge(tables, 32)
                        mine_at = bass.IndirectOffsetOnAxis(ap=mine_i[:, :].bitcast(U32), axis=0)
                        nc.gpsimd.indirect_dma_start(own[:, :], None, a["ptr"], mine_at).then_inc(own_here, 16)
                        nc.gpsimd.indirect_dma_start(k["q_first"][:, :], None, a["q"], mine_at).then_inc(qfirst_here, 16)
                    if (b + 1) % PART == 0 or b == 0:
                        pool.wait_ge(first_asked, (b + 1) // PART + 1)
                    nc.gpsimd.indirect_dma_start(
                        a["qexp"], bass.IndirectOffsetOnAxis(ap=first_i[:, b:b + 1].bitcast(U32), axis=0),
                        q[:, b, :], None, bounds_check=EDGES_PAD - 1, oob_is_err=False).then_inc(q_spread, 16)
                pool.wait_ge(q_spread, 16 * BLOCKS)
                pool.wait_ge(qfirst_here, 16)

            @block.scalar
            def _(act):
                step = chain(act, act_done)
                act.wait_ge(zeros_set, 1)
                rows = a["qexp"][0:EDGES_PAD, :].rearrange("(p s) c -> p (s c)", s=SLOTS)
                for j in range(D):
                    act.dma_start(rows[:, j * SLOTS:(j + 1) * SLOTS], zeros[:, :]).then_inc(q_filled, 16)
                act.wait_ge(root_asked, 1)
                nc.scalar.activation(var[:, :], var[:, :], ACT.Sqrt).then_inc(root_done, 1)
                with act.Fori(0, TURNS) as i:
                    act.wait_ge(turned, i + 1)
                    nc.scalar.activation(hT[:, :, :].rearrange("p g n -> p (g n)"),
                                         psT[:, :, :].rearrange("p a n -> p (a n)")[:, 0:BATCH * P],
                                         ACT.Copy).then_inc(hT_ready, 1)
                    act.wait_ge(projected, i + 1)
                    nc.scalar.activation(
                        q[:, bass.ds(i * (BATCH * GROUP), BATCH * GROUP), :].rearrange("p (g j) c -> p g j c", j=GROUP),
                        psM[:, :, 0:GROUP * 3 * D].rearrange("p g (j c) -> p g j c", j=GROUP)[:, :, :, 0:D],
                        ACT.Copy, scale=1.0 / sqrt(DH)).then_inc(q_out, 1)

            @block.tensor
            def _(pe):
                pe.wait_ge(onehots, 1)
                for s in range(SC_):
                    nc.tensor.matmul(psC[:, 0:BB], above[:, s, 0:P], ones[:, :], start=(s == 0), stop=False)
                    last = nc.tensor.matmul(psC[:, 0:BB], here[:, s, :], less[:, s, :], start=False, stop=(s == SC_ - 1))
                last.then_inc(counted, 1)
                pe.wait_ge(w_loaded, 16 * GROUP * 3)
                pe.wait_ge(pool_done, 4)
                with pe.Fori(0, TURNS) as i:
                    pe.wait_ge(staged, i + 1)
                    for g in range(BATCH):
                        last = nc.tensor.transpose(psT[:, (g * P) // 512, (g * P) % 512:(g * P) % 512 + P],
                                                   stage[:, g, :], ident[:, :])
                    last.then_inc(turned, 1)
                    pe.wait_ge(hT_ready, i + 1)
                    for g in range(BATCH):
                        last = nc.tensor.matmul(psM[:, g, 0:GROUP * 3 * D], hT[:, g, :],
                                                wqkv[:, :, :].rearrange("p j c -> p (j c)"), start=True, stop=True)
                    last.then_inc(projected, 1)

            @block.vector
            def _(vec):
                step = chain(vec, vec_done)
                v = nc.vector
                step(v.memset(hs[:, BLOCKS:BLOCKS_UP, :], 0.0))
                vec.wait_ge(samp_loaded, 16)
                vec.wait_ge(consts_ready, 5)
                step(v.tensor_copy(samp[:, :], samp_i[:, :]))
                step(v.tensor_copy(starts[:, :], starts_i[:, :]))
                step(v.tensor_copy(lows[:, :], lows_i[:, :]))
                step(v.tensor_copy(nid[:, :], nid_i[:, :]))
                step(v.tensor_tensor(above[:, :, :], spread_front(starts[:, :], SC_), spread(samp[:, :], P + 1), ALU.is_gt))
                step(v.tensor_reduce(part[:, :], above[:, :, :], axis=AX.X, op=ALU.add))
                step(v.tensor_tensor(here[:, :, :], above[:, :, 1:P + 1], above[:, :, 0:P], ALU.subtract))
                step(v.tensor_scalar(part[:, :], part[:, :], float(BLOCKS), -float(BLOCKS * P), ALU.mult, ALU.add))
                step(v.tensor_tensor(part[:, :], samp[:, :], part[:, :], ALU.add))
                step(v.tensor_tensor(less[:, :, :], spread_front(lows[:, :], SC_), spread(part[:, :], BB), ALU.is_gt))
                vec.sem_inc(onehots, 1)
                vec.wait_ge(counted, 1)
                step(v.tensor_scalar(row[:, :], psC[:, 0:BB], -1.0, 0.0, ALU.add, ALU.max))
                step(v.tensor_copy(row_i[:, :], row[:, :]))
                vec.sem_inc(rows_asked, 1)
                vec.wait_ge(x_loaded, 16)
                normalise(nc, vec, step, scratch[:, :, :], xs[:, :, :], hs[:, 0:BLOCKS, :], mean, var, root_asked, root_done, 1)
                step(v.tensor_tensor(k["res"][:, :, :], xs[:, :, :], hs[:, 0:BLOCKS, :], ALU.add))
                with vec.Fori(0, TURNS) as i:
                    v.tensor_copy(stage[:, :, :].rearrange("p g n -> p (g n)"),
                                  hs[:, bass.ds(i * (BATCH * GROUP), BATCH * GROUP), :].rearrange("p b c -> p (b c)")
                                  ).then_inc(staged, 1)
                    vec.wait_ge(q_out, i + 1)
                    v.tensor_copy(
                        kv[:, bass.ds(i * (BATCH * GROUP), BATCH * GROUP), :].rearrange("p (g j) c -> p g j c", j=GROUP),
                        psM[:, :, 0:GROUP * 3 * D].rearrange("p g (j c) -> p g j c", j=GROUP)[:, :, :, D:3 * D]
                    ).then_inc(kv_out, 1)
                    vec.wait_ge(kv_out, i + 1)
                for g in range(PARTS):
                    vec.wait_ge(rows_here[g], 16 * PART)
                    at = slice(g * PART, (g + 1) * PART)
                    step(v.tensor_tensor(below[:, :, :], drow[:, at, :], spread(nid[:, at], ROWW), ALU.is_lt))
                    step(v.tensor_reduce(ptr[:, at], below[:, :, :], axis=AX.X, op=ALU.add))
                    step(v.scalar_tensor_tensor(out=ptr[:, at], in0=row[:, at], scalar=float(ROWW), in1=ptr[:, at], op0=ALU.mult, op1=ALU.add))
                    part_lo, part_hi = max(0, g * PART - 1), (g + 1) * PART - 1
                    lo, hi, at = ptr[:, part_lo:part_hi], ptr[:, part_lo + 1:part_hi + 1], slice(part_lo, part_hi)
                    step(v.tensor_tensor(some[:, at], hi, lo, ALU.is_gt))
                    step(v.tensor_scalar(first_at[:, at], some[:, at], -FAR, FAR, ALU.mult, ALU.add))
                    step(v.tensor_tensor(first_at[:, at], first_at[:, at], lo, ALU.add))
                    step(v.tensor_copy(first_i[:, at], first_at[:, at]))
                    vec.sem_inc(first_asked, 1)
                lo, hi = ptr[:, 0:BLOCKS], ptr[:, 1:BB]
                step(v.tensor_scalar(last_at[:, :], hi, -1.0 - EDGES_PAD, None, ALU.add))
                step(v.tensor_tensor(last_at[:, :], last_at[:, :], some[:, :], ALU.mult))
                step(v.tensor_scalar(last_at[:, :], last_at[:, :], float(EDGES_PAD), None, ALU.add))
                step(v.tensor_copy(k["last_i"][:, :], last_at[:, :]))
                step(v.tensor_copy(pair[:, :, 0], lo))
                step(v.tensor_copy(pair[:, :, 1], hi))
                vec.sem_inc(table_asked, 1)
                vec.wait_ge(ends_loaded, 48)
                step(v.tensor_tensor(k["whole"][:, :], last_dst[:, :], prev_dst[:, :], ALU.is_equal))
                vec.wait_ge(own_here, 16)
                step(v.tensor_copy(mine[:, :], edge_i[:, :]))
                step(v.tensor_scalar(cross[:, 2:3], own[:, 1:2], -1.0, None, ALU.add))
                step(v.tensor_copy(k["end_i"][:, :], cross[:, 2:3]))
                step(v.tensor_tensor(cross[:, 0:1], own[:, 0:1], mine[:, :], ALU.is_lt))
                step(v.tensor_scalar(mine[:, :], mine[:, :], float(SLOTS), None, ALU.add))
                step(v.tensor_tensor(cross[:, 1:2], cross[:, 2:3], mine[:, :], ALU.is_lt))
                step(v.tensor_tensor(cross[:, 0:1], cross[:, 0:1], cross[:, 1:2], ALU.mult))
                step(v.tensor_scalar(cross[:, 0:1], cross[:, 0:1], -FAR, FAR, ALU.mult, ALU.add))
                step(v.tensor_tensor(cross[:, 0:1], cross[:, 0:1], cross[:, 2:3], ALU.add))
                step(v.tensor_copy(k["patch_i"][:, :], cross[:, 0:1]))


def attention(nc, a, k):
    with ExitStack() as ctx:
        sb = lambda name, shape, dt=FP32: ctx.enter_context(nc.sbuf_tensor(name, shape, dt))
        sem = lambda name: ctx.enter_context(nc.semaphore(name))
        T1 = T + 1
        src_i = [sb(f"src_i{b}", [P, T], I32) for b in range(2)]
        kv = [sb(f"kv{b}", [P, T, 2 * D]) for b in range(2)]
        dst_i = [sb(f"dst_i{b}", [P, T1], I32) for b in range(2)]
        attr = [sb(f"attr{b}", [P, T, 3]) for b in range(2)]
        qin = [sb(f"qin{b}", [P, T, D]) for b in range(2)]
        same = sb("same", [P, T1])
        pen = sb("pen", [P, T1])
        same_c, pen_c = sb("same_c", [P, D, T1]), sb("pen_c", [P, HEADS, T1])
        qseed, qrun = sb("qseed", [P, D, T1]), sb("qrun", [P, D, T1])
        qk = sb("qk", [P, HEADS, T, DH])
        score = sb("score", [P, HEADS, T1])
        decay = sb("decay", [P, HEADS, T1])
        rel = sb("rel", [P, HEADS, T])
        decay_c = sb("decay_c", [P, SUMS, T1])
        ev, sums = sb("ev", [P, HEADS, HC, T1]), k["sums"]
        peak = k["peak"]
        out = [sb(f"out{b}", [P, T, STATE]) for b in range(2)]
        sq, rn = sb("sq", [P, T, 3]), sb("rn", [P, T])
        frame = [sb(f"frame_out{b}", [P, T, 9]) for b in range(2)]
        sgn, inv, xy = sb("sgn", [P, T]), sb("inv", [P, T]), sb("xy", [P, T])
        zrow = sb("zrow", [2, STATE])

        src_loaded, dst_loaded, attr_loaded, q_loaded, kv_here, stored = (
            [sem(f"{n}{b}") for b in range(2)] for n in ("src_loaded", "dst_loaded", "attr_loaded", "q_loaded", "kv_here", "stored"))
        kv_free, dst_free, attr_free, q_free = (sem(n) for n in ("kv_free", "dst_free", "attr_free", "q_free"))
        flags_ready, spread_ready, q_scanned, exps_asked, exps_ready = (sem(n) for n in (
            "flags_ready", "spread_ready", "q_scanned", "exps_asked", "exps_ready"))
        sums_ready, sums_copied, rn_asked, rn_ready = (sem(n) for n in ("sums_ready", "sums_copied", "rn_asked", "rn_ready"))
        frame_ready, frame_free = sem("frame_ready"), sem("frame_free")
        frame_stored = [sem(f"frame_stored{b}") for b in range(2)]
        vec_done, zrow_set, chunk_begun = sem("vec_done2"), sem("zrow_set"), sem("chunk_begun")
        edges = lambda name: a[name].rearrange("(p s) -> p s", s=SLOTS)

        with nc.Block() as block:

            @block.sync
            def _(sp):
                base = a["dst_ext"]
                before = base[0:EDGES_PAD].rearrange("(p s) -> p s", s=SLOTS)
                def load_src(b, at):
                    sp.dma_start(src_i[b][:, :], edges("src")[:, bass.ds(at, T)]).then_inc(src_loaded[b], 16)

                load_src(0, 0)
                load_src(1, T)

                def body(i, last):
                    for b in range(2):
                        at = i * (2 * T) + b * T
                        sp.wait_ge(dst_free, i * 2 + b + 1)
                        sp.dma_start(dst_i[b][:, 0:T], before[:, bass.ds(at, T)]).then_inc(dst_loaded[b], 16)
                        sp.dma_start(dst_i[b][:, T:T1], edges("dst")[:, bass.ds(at + (T - 1), 1)], allow_slow_non_contiguous=True).then_inc(dst_loaded[b], 16)
                        sp.wait_ge(attr_free, i * 2 + b + 1)
                        sp.dma_start(attr[b][:, :, :].rearrange("p t c -> p (t c)"),
                                     a["attr"].rearrange("(p s) c -> p (s c)", s=SLOTS)[:, bass.ds(at * 3, 3 * T)]).then_inc(attr_loaded[b], 16)
                        sp.wait_ge(q_free, i * 2 + b + 1)
                        sp.dma_start(qin[b][:, :, :].rearrange("p t c -> p (t c)"),
                                     a["qexp"].rearrange("(p s) c -> p (s c)", s=SLOTS)[:, bass.ds(at * D, D * T)]).then_inc(q_loaded[b], 16)
                        sp.wait_ge(frame_ready, i * 2 + b + 1)
                        sp.dma_start(a["frame"].rearrange("(p s) c -> p (s c)", s=SLOTS)[:, bass.ds(at * 9, 9 * T)],
                                     frame[b][:, :, :].rearrange("p t c -> p (t c)")).then_inc(frame_stored[b], 16)
                        sp.wait_ge(frame_stored[b], i * 16 + 16)
                        sp.sem_inc(frame_free, 1)
                        if not last:
                            sp.wait_ge(kv_here[b], i * (16 * T) + 16 * T)
                            load_src(b, i * (2 * T) + (b + 2) * T)
                pairs(sp, body)

            @block.gpsimd
            def _(pool):
                with pool.Fori(0, PAIRS) as i:
                    for b in range(2):
                        pool.wait_ge(src_loaded[b], i * 16 + 16)
                        pool.wait_ge(kv_free, i * 2 + b + 1)
                        pool.sem_inc(chunk_begun, 1)
                        for t in range(T):
                            nc.gpsimd.indirect_dma_start(
                                kv[b][:, t, :], None, a["kv"],
                                bass.IndirectOffsetOnAxis(ap=src_i[b][:, t:t + 1].bitcast(U32), axis=0)).then_inc(kv_here[b], 16)

            @block.scalar
            def _(act):
                act.wait_ge(zrow_set, 1)
                for b in range(2):
                    act.dma_start(a["state"][EDGES_PAD + b:EDGES_PAD + b + 1, :], zrow[b:b + 1, :]).then_inc(stored[b], 16)
                act.sem_inc(q_free, 2)
                with act.Fori(0, PAIRS) as i:
                    for b in range(2):
                        c1 = i * 2 + b + 1
                        act.wait_ge(rn_asked, c1)
                        nc.scalar.activation(rn[:, :], rn[:, :], ACT.Sqrt).then_inc(rn_ready, 1)
                        act.wait_ge(flags_ready, c1)
                        act.wait_ge(q_scanned, c1)
                        nc.scalar.activation(same_c[:, :, :], spread_front(same[:, :], D), ACT.Copy).then_inc(spread_ready, 1)
                        nc.scalar.activation(pen_c[:, :, :], spread_front(pen[:, :], HEADS), ACT.Copy).then_inc(spread_ready, 1)
                        act.wait_ge(q_loaded[b], i * 16 + 16)
                        nc.scalar.activation(qseed[:, :, 1:T1], qin[b][:, :, :].rearrange("p t c -> p c t"), ACT.Copy).then_inc(spread_ready, 1)
                        act.wait_ge(spread_ready, c1 * 3)
                        act.sem_inc(q_free, 1)
                        act.wait_ge(exps_asked, c1)
                        nc.scalar.activation(decay_c[:, :, :].rearrange("p (h c) t -> p h c t", c=HC),
                                             decay[:, :, :].rearrange("p h (o t) -> p h o t", o=1).to_broadcast([P, HEADS, HC, T1]),
                                             ACT.Exp).then_inc(exps_ready, 1)
                        nc.scalar.activation(ev[:, :, DH, 1:T1], rel[:, :, :], ACT.Exp).then_inc(exps_ready, 1)
                        act.wait_ge(sums_ready, c1)
                        act.wait_ge(stored[b], i * 16 + 16)
                        nc.scalar.activation(out[b][:, :, 0:SUMS], sums[:, :, 1:T1].rearrange("p c t -> p t c"), ACT.Copy).then_inc(sums_copied, 1)
                        nc.scalar.activation(out[b][:, :, SUMS:STATE], peak[:, :, 1:T1].rearrange("p c t -> p t c"), ACT.Copy).then_inc(sums_copied, 1)
                        act.wait_ge(sums_copied, c1 * 2 + 2)
                        act.dma_start(a["state"][0:EDGES_PAD, :].rearrange("(p s) c -> p (s c)", s=SLOTS)[:, bass.ds(i * (2 * T * STATE) + b * (T * STATE), T * STATE)],
                                      out[b][:, :, :].rearrange("p t c -> p (t c)")).then_inc(stored[b], 16)
                for b in range(2):
                    act.wait_ge(stored[b], 16 * (PAIRS + 1))

            @block.vector
            def _(vec):
                v = nc.vector
                step = chain(vec, vec_done)
                step(v.memset(zrow[:, :], 0.0))
                vec.sem_inc(zrow_set, 1)
                step(v.tensor_copy(qrun[:, :, T], k["q_first"][:, :]))
                step(v.memset(peak[:, :, T:T1], -BIG))
                step(v.memset(sums[:, :, T:T1], 0.0))
                step(v.memset(same[:, :], 0.0))
                step(v.memset(decay[:, :, :], -BIG))
                for primed, n in ((kv_free, 2), (dst_free, 2), (attr_free, 2), (frame_free, 2), (q_scanned, 1), (sums_copied, 2)):
                    vec.sem_inc(primed, n)
                steps = 34
                base = step.count[0]
                with vec.Fori(0, PAIRS) as i:
                    step = chain(vec, vec_done, base + i * (2 * steps))
                    for b in range(2):
                        c1 = i * 2 + b + 1
                        at = i * (2 * T) + b * T
                        vec.wait_ge(attr_loaded[b], i * 16 + 16)
                        step(v.tensor_tensor(sq[:, :, :], attr[b][:, :, :], attr[b][:, :, :], ALU.mult))
                        step(v.tensor_reduce(rn[:, :], sq[:, :, :], axis=AX.X, op=ALU.add))
                        vec.sem_inc(rn_asked, 1)
                        vec.wait_ge(dst_loaded[b], i * 32 + 32)
                        step(v.tensor_tensor(same[:, 1:T1], dst_i[b][:, 1:T1], dst_i[b][:, 0:T], ALU.is_equal))
                        vec.sem_inc(dst_free, 1)
                        step(v.tensor_scalar(pen[:, :], same[:, :], BIG, -BIG, ALU.mult, ALU.add))
                        vec.sem_inc(flags_ready, 1)
                        step(v.tensor_copy(k["same"][:, bass.ds(at, T)], same[:, 1:T1]))
                        vec.wait_ge(rn_ready, c1)
                        step(v.reciprocal(rn[:, :], rn[:, :]))
                        vec.wait_ge(frame_free, c1)
                        fr = frame[b]
                        nx, ny, nz = fr[:, :, 0], fr[:, :, 1], fr[:, :, 2]
                        step(v.tensor_tensor(fr[:, :, 0:2], attr[b][:, :, 1:3], spread(rn[:, :], 2), ALU.mult))
                        step(v.tensor_tensor(nz, attr[b][:, :, 0], rn[:, :], ALU.mult))
                        vec.sem_inc(attr_free, 1)
                        step(v.tensor_scalar(sgn[:, :], nz, 0.0, 2.0, ALU.is_ge, ALU.mult))
                        step(v.tensor_scalar(sgn[:, :], sgn[:, :], -1.0, None, ALU.add))
                        step(v.tensor_tensor(inv[:, :], sgn[:, :], nz, ALU.add))
                        step(v.reciprocal(inv[:, :], inv[:, :]))
                        step(v.scalar_tensor_tensor(out=xy[:, :], in0=ny, scalar=-1.0, in1=inv[:, :], op0=ALU.mult, op1=ALU.mult))
                        step(v.tensor_tensor(fr[:, :, 6], xy[:, :], nx, ALU.mult))
                        step(v.tensor_tensor(xy[:, :], xy[:, :], ny, ALU.mult))
                        step(v.tensor_tensor(fr[:, :, 7], xy[:, :], sgn[:, :], ALU.add))
                        step(v.tensor_scalar(fr[:, :, 8], ny, -1.0, None, ALU.mult))
                        step(v.scalar_tensor_tensor(out=fr[:, :, 5], in0=nx, scalar=-1.0, in1=sgn[:, :], op0=ALU.mult, op1=ALU.mult))
                        step(v.tensor_tensor(fr[:, :, 4], fr[:, :, 6], sgn[:, :], ALU.mult))
                        step(v.tensor_tensor(xy[:, :], nx, inv[:, :], ALU.mult))
                        step(v.tensor_tensor(xy[:, :], xy[:, :], fr[:, :, 5], ALU.mult))
                        step(v.tensor_scalar(fr[:, :, 3], xy[:, :], 1.0, None, ALU.add))
                        vec.sem_inc(frame_ready, 1)
                        step(v.tensor_copy(qseed[:, :, 0], qrun[:, :, T]))
                        vec.wait_ge(spread_ready, c1 * 3)
                        flat = lambda x: x[:, :, :].rearrange("p c t -> p (c t)")
                        step(v.tensor_tensor_scan(flat(qrun), flat(same_c), flat(qseed), 0.0, ALU.mult, ALU.add))
                        vec.wait_ge(kv_here[b], i * (16 * T) + 16 * T)
                        step(v.tensor_tensor(qk[:, :, :, :], qrun[:, :, 1:T1].rearrange("p (h d) t -> p h t d", d=DH),
                                             kv[b][:, :, 0:D].rearrange("p t (h d) -> p h t d", d=DH), ALU.mult))
                        step(v.tensor_reduce(score[:, :, 1:T1], qk[:, :, :, :], axis=AX.X, op=ALU.add))
                        step(v.tensor_copy(score[:, :, 0], peak[:, :, T]))
                        vec.wait_ge(sums_copied, c1 * 2)
                        step(v.tensor_tensor_scan(flat(peak), flat(pen_c), flat(score), -BIG, ALU.add, ALU.max))
                        step(v.tensor_tensor(decay[:, :, 1:T1], peak[:, :, 0:T], pen_c[:, :, 1:T1], ALU.add))
                        step(v.tensor_tensor(decay[:, :, 1:T1], decay[:, :, 1:T1], peak[:, :, 1:T1], ALU.subtract))
                        step(v.tensor_tensor(rel[:, :, :], score[:, :, 1:T1], peak[:, :, 1:T1], ALU.subtract))
                        vec.sem_inc(q_scanned, 1)
                        vec.sem_inc(exps_asked, 1)
                        vec.wait_ge(exps_ready, c1 * 2)
                        step(v.tensor_tensor(ev[:, :, 0:DH, 1:T1], kv[b][:, :, D:2 * D].rearrange("p t (h d) -> p h d t", d=DH),
                                             ev[:, :, DH:HC, 1:T1].to_broadcast([P, HEADS, DH, T]), ALU.mult))
                        vec.sem_inc(kv_free, 1)
                        step(v.tensor_copy(ev[:, :, :, 0], sums[:, :, T].rearrange("p (h c) -> p h c", c=HC)))
                        step(v.tensor_tensor_scan(flat(sums), flat(decay_c), ev[:, :, :, :].rearrange("p h c t -> p (h c t)"), 0.0, ALU.mult, ALU.add))
                        vec.sem_inc(sums_ready, 1)
                    assert step.count[0] == 2 * steps, step.count[0]
                vec.wait_ge(sums_copied, CHUNKS * 2 + 2)


def node_attention(nc, a, k):
    with ExitStack() as ctx:
        sb = lambda name, shape, dt=FP32: ctx.enter_context(nc.sbuf_tensor(name, shape, dt))
        pb = lambda name, shape, dt=FP32: ctx.enter_context(nc.psum_tensor(name, shape, dt))
        sem = lambda name: ctx.enter_context(nc.semaphore(name))
        per_turn = BATCH * GROUP
        blocks_of = lambda i: min(per_turn, BLOCKS - i * per_turn)
        tail = sb("tail", [P, 3, SUMS])
        rows = sb("rows", [SUMS, 3, P])
        peaks, totals = sb("peaks", [SUMS, P + 1]), sb("totals", [SUMS, P + 1])
        shrink, gain = sb("shrink", [SUMS, P]), sb("gain", [SUMS, P])
        carry = sb("carry", [P, 2, SUMS])
        patch = sb("patch", [P, STATE])
        top, ex = sb("top", [P, SUMS]), sb("ex", [P, 2, SUMS])
        mix = sb("mix", [P, 2, SUMS])
        state = sb("state", [P, BLOCKS, STATE])
        rden = sb("rden", [P, per_turn, HEADS])
        stage, hT = sb("stage3", [P, BATCH, P]), sb("hT3", [P, BATCH, P])
        wo = sb("wo", [P, GROUP, D])
        hs = sb("hs3", [P, BLOCKS, D])
        squares = sb("squares3", [P, per_turn, D])
        mean, var = sb("mean3", [P, per_turn]), sb("var3", [P, per_turn])
        ident = k["ident"]
        psA, psB = pb("psA", [P, 3, P]), pb("psB", [P, 2, SUMS])
        psT = pb("psT3", [P, 2, 512])
        psM = pb("psM3", [P, 2, 512])

        wo_loaded, wo_cleared, tail_ready, turned, rows_ready, ex_asked, ex_done, carry_ready, carry_back = (sem(n) for n in (
            "wo_loaded", "wo_cleared", "tail_ready", "turned3", "rows_ready", "ex_asked", "ex_done", "carry_ready", "carry_back"))
        patch_here, patch_ready, patched = sem("patch_here"), sem("patch_ready"), sem("patched")
        states_here = [sem(f"states_here{i}") for i in range(TURNS)]
        staged, stage_turned, hT_ready, projected, root_asked, root_done, h_ready, h_stored = (sem(n) for n in (
            "staged3", "stage_turned3", "hT_ready3", "projected3", "root_asked3", "root_done3", "h_ready3", "h_stored"))
        vec_done, pool_done = sem("vec_done3"), sem("pool_done3")

        with nc.Block() as block:

            @block.sync
            def _(sp):
                sp.wait_ge(wo_cleared, 1)
                for j in range(GROUP):
                    sp.dma_start(wo[j * D:(j + 1) * D, j, :], a["wo"]).then_inc(wo_loaded, 16)
                for i in range(TURNS):
                    sp.wait_ge(h_ready, i + 1)
                    b0 = i * per_turn
                    sp.dma_start(a["h2"].rearrange("(p b) c -> p b c", b=BLOCKS)[:, b0:b0 + blocks_of(i), :],
                                 hs[:, b0:b0 + blocks_of(i), :]).then_inc(h_stored, 16)
                sp.wait_ge(h_stored, 16 * TURNS)

            @block.gpsimd
            def _(pool):
                step = chain(pool, pool_done)
                step(nc.gpsimd.memset(wo[:, :, :], 0.0))
                pool.sem_inc(wo_cleared, 1)
                nc.gpsimd.indirect_dma_start(patch[:, :], None, a["state"], bass.IndirectOffsetOnAxis(
                    ap=k["end_i"][:, :].bitcast(U32), axis=0)).then_inc(patch_here, 16)
                pool.wait_ge(patch_ready, 1)
                nc.gpsimd.indirect_dma_start(a["state"], bass.IndirectOffsetOnAxis(
                    ap=k["patch_i"][:, :].bitcast(U32), axis=0), patch[:, :], None,
                    bounds_check=EDGES_PAD - 1, oob_is_err=False).then_inc(patched, 16)
                pool.wait_ge(patched, 16)
                for b in range(BLOCKS):
                    nc.gpsimd.indirect_dma_start(state[:, b, :], None, a["state"], bass.IndirectOffsetOnAxis(
                        ap=k["last_i"][:, b:b + 1].bitcast(U32), axis=0)).then_inc(states_here[b // per_turn], 16)

            @block.scalar
            def _(act):
                act.wait_ge(ex_asked, 1)
                nc.scalar.activation(shrink[:, :], shrink[:, :], ACT.Exp).then_inc(ex_done, 1)
                nc.scalar.activation(gain[:, :], gain[:, :], ACT.Exp).then_inc(ex_done, 1)
                act.wait_ge(ex_asked, 2)
                nc.scalar.activation(ex[:, :, :], ex[:, :, :], ACT.Exp).then_inc(ex_done, 1)
                for i in range(TURNS):
                    act.wait_ge(stage_turned, i + 1)
                    nc.scalar.activation(hT[:, :, :].rearrange("p g n -> p (g n)"),
                                         psT[:, :, :].rearrange("p a n -> p (a n)")[:, 0:BATCH * P],
                                         ACT.Copy).then_inc(hT_ready, 1)
                    act.wait_ge(root_asked, i + 1)
                    nc.scalar.activation(var[:, :], var[:, :], ACT.Sqrt).then_inc(root_done, 1)

            @block.tensor
            def _(pe):
                pe.wait_ge(tail_ready, 1)
                for n in range(3):
                    last = nc.tensor.transpose(psA[0:SUMS, n, :], tail[:, n, :], ident[:, :])
                last.then_inc(turned, 1)
                pe.wait_ge(carry_ready, 1)
                nc.tensor.transpose(psB[:, 0, :], peaks[:, 0:P], ident[0:SUMS, 0:SUMS])
                nc.tensor.transpose(psB[:, 1, :], totals[:, 0:P], ident[0:SUMS, 0:SUMS]).then_inc(carry_back, 1)
                pe.wait_ge(wo_loaded, 16 * GROUP)
                for i in range(TURNS):
                    pe.wait_ge(staged, i + 1)
                    for g in range(BATCH):
                        last = nc.tensor.transpose(psT[:, g // 4, (g % 4) * P:(g % 4 + 1) * P], stage[:, g, :], ident[:, :])
                    last.then_inc(stage_turned, 1)
                    pe.wait_ge(hT_ready, i + 1)
                    for g in range(BATCH):
                        last = nc.tensor.matmul(psM[:, g // 4, (g % 4) * P:(g % 4 + 1) * P], hT[:, g, :],
                                                wo[:, :, :].rearrange("p j c -> p (j c)"), start=True, stop=True)
                    last.then_inc(projected, 1)

            @block.vector
            def _(vec):
                v = nc.vector
                step = chain(vec, vec_done)
                step(v.tensor_copy(tail[:, 0, :].rearrange("p (h c) -> p h c", c=HC), spread(k["peak"][:, :, T], HC)))
                step(v.tensor_copy(tail[:, 1, :], k["sums"][:, :, T]))
                step(v.tensor_copy(tail[:, 2, :], k["whole"][:, :].to_broadcast([P, SUMS])))
                vec.sem_inc(tail_ready, 1)
                vec.wait_ge(turned, 1)
                step(v.tensor_copy(rows[:, :, :], psA[0:SUMS, :, :]))
                step(v.tensor_scalar(rows[:, 2, :], rows[:, 2, :], BIG, -BIG, ALU.mult, ALU.add))
                step(v.memset(peaks[:, 0:1], -BIG))
                step(v.memset(totals[:, 0:1], 0.0))
                step(v.tensor_tensor_scan(peaks[:, 1:P + 1], rows[:, 2, :], rows[:, 0, :], -BIG, ALU.add, ALU.max))
                step(v.tensor_tensor(shrink[:, :], peaks[:, 0:P], rows[:, 2, :], ALU.add))
                step(v.tensor_tensor(shrink[:, :], shrink[:, :], peaks[:, 1:P + 1], ALU.subtract))
                step(v.tensor_tensor(gain[:, :], rows[:, 0, :], peaks[:, 1:P + 1], ALU.subtract))
                vec.sem_inc(ex_asked, 1)
                vec.wait_ge(ex_done, 2)
                step(v.tensor_tensor(gain[:, :], gain[:, :], rows[:, 1, :], ALU.mult))
                step(v.tensor_tensor_scan(totals[:, 1:P + 1], shrink[:, :], gain[:, :], 0.0, ALU.mult, ALU.add))
                vec.sem_inc(carry_ready, 1)
                vec.wait_ge(carry_back, 1)
                step(v.tensor_copy(carry[:, :, :], psB[:, :, :]))
                vec.wait_ge(patch_here, 16)
                pk = spread(patch[:, SUMS:STATE], HC)
                byhead = lambda x: x.rearrange("p (h c) -> p h c", c=HC)
                step(v.tensor_tensor(byhead(top[:, :]), byhead(carry[:, 0, :]), pk, ALU.max))
                step(v.tensor_tensor(byhead(ex[:, 0, :]), pk, byhead(top[:, :]), ALU.subtract))
                step(v.tensor_tensor(ex[:, 1, :], carry[:, 0, :], top[:, :], ALU.subtract))
                vec.sem_inc(ex_asked, 1)
                vec.wait_ge(ex_done, 3)
                step(v.tensor_tensor(mix[:, 0, :], patch[:, 0:SUMS], ex[:, 0, :], ALU.mult))
                step(v.tensor_tensor(mix[:, 1, :], carry[:, 1, :], ex[:, 1, :], ALU.mult))
                step(v.tensor_tensor(patch[:, 0:SUMS], mix[:, 0, :], mix[:, 1, :], ALU.add))
                vec.sem_inc(patch_ready, 1)
                step(v.memset(stage[:, :, :], 0.0))
                step(v.memset(var[:, :], 1.0))
                for i in range(TURNS):
                    b0, nb = i * per_turn, blocks_of(i)
                    at = slice(b0, b0 + nb)
                    vec.wait_ge(states_here[i], 16 * nb)
                    st = state[:, at, 0:SUMS].rearrange("p b (h c) -> p b h c", c=HC)
                    step(v.tensor_scalar(rden[:, 0:nb, :], st[:, :, :, DH], 1e-16, None, ALU.max))
                    step(v.reciprocal(rden[:, 0:nb, :], rden[:, 0:nb, :]))
                    step(v.tensor_tensor(
                        stage[:, :, :].rearrange("p g (j c) -> p (g j) c", j=GROUP)[:, 0:nb, :].rearrange("p b (h c) -> p b h c", c=DH),
                        st[:, :, :, 0:DH],
                        rden[:, 0:nb, :].rearrange("p b (h o) -> p b h o", o=1).to_broadcast([P, nb, HEADS, DH]), ALU.mult))
                    vec.sem_inc(staged, 1)
                    vec.wait_ge(projected, i + 1)
                    step(v.tensor_tensor(k["res"][:, at, :], k["res"][:, at, :],
                                         psM[:, :, :].rearrange("p a (j c) -> p (a j) c", c=D)[:, 0:nb, :], ALU.add))
                    normalise(nc, vec, step, squares[:, 0:nb, :], k["res"][:, at, :], hs[:, at, :], mean[:, 0:nb], var[:, 0:nb],
                              root_asked, root_done, i + 1)
                    vec.sem_inc(h_ready, 1)


def tensor_product(nc, a, k):
    with ExitStack() as ctx:
        sb = lambda name, shape, dt=FP32: ctx.enter_context(nc.sbuf_tensor(name, shape, dt))
        pb = lambda name, shape, dt=FP32: ctx.enter_context(nc.psum_tensor(name, shape, dt))
        sem = lambda name: ctx.enter_context(nc.semaphore(name))
        T1 = T + 1
        GC = SIX * COLS
        w1, b1 = sb("w1", [P, 1]), sb("b1", [P, 1])
        units = [sb(f"units{r}", [P, HALF]) for r in range(2)]
        high = [sb(f"high{r}", [P, HALF], FP16) for r in range(2)]
        low = [sb(f"low{r}", [P, HALF], FP16) for r in range(2)]
        stack = sb("stack", [P, PACKS, 2 * HALF], FP16)
        capped = sb("capped", [P, PACKS, 2 * HALF], FP16)
        whigh, wlow = sb("whigh", [P, 384], FP16), sb("wlow", [P, 384], FP16)
        tops, tops0, scales0, scales = sb("tops", [P, 4]), sb("tops0", [1, 8]), sb("scales0", [1, 4]), sb("scales", [P, 4])
        ones_row = sb("ones_row", [1, P])
        src_i = [sb(f"src4_{b}", [P, T], I32) for b in range(2)]
        feat = [sb(f"feat{b}", [P, T, D]) for b in range(2)]
        frame = [sb(f"frame{b}", [P, T, 9]) for b in range(2)]
        ops = [sb(f"ops{b}", [P, T, 3 * JC]) for b in range(2)]
        parts = sb("parts", [P, T, 3, 3 * VU])
        prod = [sb(f"prod{r}", [P, JC, GC]) for r in range(2)]
        red = [sb(f"red{b}", [P, T, COLS]) for b in range(2)]
        seed, same_c, run = sb("seed", [P, D, T1]), sb("same_c4", [P, D, T1]), k["run"]
        out = sb("out4", [P, T, D])
        raw, new = (out[:, :, :].rearrange("p t c -> p (t c)")[:, n * 768:(n + 1) * 768].rearrange("p (x c) -> p x c", x=2) for n in range(2))
        zrow = sb("zrow4", [1, D])
        ident = k["ident"]
        psR = pb("psR", [P, 2, TRI, 512])
        psS = pb("psS", [P, 2, 512])

        w_loaded, wrad_ready, zrow_set, rows_set = sem("w_loaded4"), sem("wrad_ready"), sem("zrow_set4"), sem("rows_set")
        tops_ready, tops_turned, scales_ready, scales_spread, units_scaled = (sem(n) for n in (
            "tops_ready", "tops_turned", "scales_ready", "scales_spread", "units_scaled"))
        src_loaded, feat_here, w_here, frame_here, stacked = ([sem(f"{n}{b}") for b in range(2)] for n in (
            "src_loaded4", "feat_here", "w_here", "frame_here", "stacked"))
        feat_free, frame_free, stored = sem("feat_free"), sem("frame_free4"), sem("stored4")
        stack_free = [sem(f"stack_free{h}") for h in range(PACKS)]
        units_ready, high_ready, split_done, parts_seen = sem("units_ready"), sem("high_ready"), sem("split_done"), sem("parts_seen")
        radial_ready, prod_done, prod_ready, sum_ready, sum_free = (sem(n) for n in (
            "radial_ready", "prod_done", "prod_ready", "sum_ready", "sum_free"))
        ops_copied, turned_ready, turned_copied, ops_free, flags_ready, red_free, scanned, run_copied = (sem(n) for n in (
            "ops_copied", "turned_ready", "turned_copied", "ops_free", "flags_ready4", "red_free", "scanned", "run_copied"))
        seeded, vec_done, chunk_begun = sem("seeded"), sem("vec_done4"), sem("chunk_begun4")

        with nc.Block() as block:

            @block.sync
            def _(sp):
                sources = a["src"].rearrange("(p s) -> p s", s=SLOTS)
                frames = a["frame"].rearrange("(p s) c -> p (s c)", s=SLOTS)

                def load_src(b, at):
                    sp.dma_start(src_i[b][:, :], sources[:, bass.ds(at, T)]).then_inc(src_loaded[b], 16)

                def load_frame(b, at):
                    sp.dma_start(frame[b][:, :, :].rearrange("p t c -> p (t c)"), frames[:, bass.ds(at * 9, 9 * T)]).then_inc(frame_here[b], 16)

                def load_w(r, at):
                    for h in range(2):
                        sp.dma_start(units[r][h * HID:(h + 1) * HID, :], a["wT"][bass.ds(at + h * HALF, HALF)].rearrange("(o n) -> o n", o=1).to_broadcast([HID, HALF])
                                     ).then_inc(w_here[r], 16)

                def stack_up(r, h, q, c):
                    sp.wait_ge(split_done, q + 3)
                    sp.sem_inc(parts_seen, 1)
                    sp.wait_ge(stack_free[h], c + 1)
                    for half in range(2):
                        frm, to = slice(half * HID, (half + 1) * HID), slice(half * HALF, (half + 1) * HALF)
                        sp.dma_start(stack[0:HID, h, to], high[r][frm, :]).then_inc(stacked[r], 16)
                        sp.dma_start(stack[HID:P, h, to], low[r][frm, :]).then_inc(stacked[r], 16)
                        sp.dma_start(capped[0:HID, h, to], high[r][frm, :]).then_inc(stacked[r], 16)

                load_src(0, 0)
                load_src(1, T)
                for half in (slice(0, HID), slice(HID, P)):
                    sp.dma_start(w1[half, :], a["w1"]).then_inc(w_loaded, 16)
                    sp.dma_start(b1[half, :], a["b1"]).then_inc(w_loaded, 16)
                    sp.dma_start(raw[half, 0, :], a["w2"]).then_inc(w_loaded, 16)
                sp.dma_start(raw[0:HID, 1, :], a["w2"]).then_inc(w_loaded, 16)
                sp.dma_start(raw[HID:P, 1, :], a["b2"].to_broadcast([HID, 384])).then_inc(w_loaded, 16)
                for j in range(2):
                    sp.dma_start(prod[j][:, :, :].rearrange("p j c -> p (j c)")[:, 0:SLOTS // 2],
                                 a["wT"].rearrange("(j p s) -> j p s", j=2, p=P)[j]).then_inc(w_loaded, 16)
                load_w(0, 0)
                load_w(1, PACK * P)
                load_frame(0, 0)
                load_frame(1, T)
                for h in range(PACKS):
                    stack_up(h % 2, h, h, 0)
                    load_w(h % 2, (h + 2) * PACK * P)

                def body(i, last):
                    for b in range(2):
                        c1 = i * 2 + b + 1
                        if not last:
                            sp.wait_ge(feat_here[b], i * (16 * T) + 16 * T)
                            load_src(b, i * (2 * T) + (b + 2) * T)
                        if not (last and b == 1):
                            for h in range(PACKS):
                                pack = (b + 1) * PACKS + h
                                stack_up(pack % 2, h, i * (2 * PACKS) + pack, c1)
                                if not last or h == 0:
                                    load_w(pack % 2, i * (2 * T * P) + (pack + 2) * (PACK * P))
                        if not last:
                            sp.wait_ge(frame_free, c1)
                            load_frame(b, i * (2 * T) + (b + 2) * T)
                pairs(sp, body)

            @block.gpsimd
            def _(pool):
                with pool.Fori(0, PAIRS) as i:
                    for b in range(2):
                        pool.wait_ge(src_loaded[b], i * 16 + 16)
                        pool.wait_ge(feat_free, i * 2 + b + 1)
                        pool.sem_inc(chunk_begun, 1)
                        for t in range(T):
                            nc.gpsimd.indirect_dma_start(
                                feat[b][:, t, :], None, a["h2"],
                                bass.IndirectOffsetOnAxis(ap=src_i[b][:, t:t + 1].bitcast(U32), axis=0)).then_inc(feat_here[b], 16)

            @block.tensor
            def _(pe):
                def radial(i, b, g):
                    c = i * 2 + b
                    h, g0 = g // (GPC // PACKS), g // (GPC // PACKS) * (GPC // PACKS)
                    if g == g0:
                        pack = b * PACKS + h
                        pe.wait_ge(stacked[pack % 2], (i * PACKS + pack // 2) * 96 + 192)
                    pe.wait_ge(prod_done, 3 * (c * GPC + g) + 3)
                    for t in range(TRI):
                        at = ((g - g0) * TRI + t) * P
                        nc.tensor.matmul(psR[:, g % 2, t, 0:384], stack[:, h, at:at + P], whigh[:, :], start=True, stop=False)
                        last_mm = nc.tensor.matmul(psR[:, g % 2, t, 0:384], capped[:, h, at:at + P], wlow[:, :], start=False, stop=True)
                    last_mm.then_inc(radial_ready, 1)
                    if g == g0 + GPC // PACKS - 1:
                        pe.wait_ge(radial_ready, c * GPC + g + 1)
                        pe.sem_inc(stack_free[h], 1)

                def sums(c, b, s):
                    r, q = (b * SPC + s) % 2, c * SPC + s
                    pe.wait_ge(sum_free, q + 1)
                    pe.wait_ge(prod_done, q * 6 + 12)
                    order = [j for j in range(FOLDS[s], JC) if not JC // 2 <= j < JC // 2 + FOLDS[s]]
                    for n, j in enumerate(order):
                        nc.tensor.matmul(psS[:, r, 0:GC], ident[:, :], prod[r][:, j, :], start=(n == 0), stop=False)
                    pe.wait_ge(prod_ready, q + 1)
                    for j in range(FOLDS[s]):
                        last_mm = nc.tensor.matmul(psS[:, r, 0:GC], ident[:, :], prod[r][:, j, :], start=False, stop=(j == FOLDS[s] - 1))
                    last_mm.then_inc(sum_ready, 1)

                pe.wait_ge(tops_ready, 1)
                for j in range(4):
                    turn = nc.tensor.matmul(psS[0:1, 0, j * P:(j + 1) * P], tops[:, j:j + 1], ident[:, :], start=True, stop=True)
                turn.then_inc(tops_turned, 1)
                pe.wait_ge(scales_ready, 1)
                nc.tensor.matmul(psS[:, 1, 0:4], ones_row[:, :], scales0[:, :], start=True, stop=True).then_inc(scales_spread, 1)
                pe.wait_ge(wrad_ready, 1)
                radial(0, 0, 0)
                radial(0, 0, 1)

                def body(i, last):
                    for b in range(2):
                        for s in range(SPC):
                            for g in (2 * s + 2, 2 * s + 3):
                                if g < GPC:
                                    radial(i, b, g)
                                elif not (last and b == 1):
                                    radial(i, b + 1, g - GPC)
                            sums(i * 2 + b, b, s)
                pairs(pe, body)

            @block.scalar
            def _(act):
                act.wait_ge(zrow_set, 1)
                act.dma_start(a["state2"][EDGES_PAD:EDGES_PAD + 1, :], zrow[:, :]).then_inc(stored, 16)

                def hidden(i, pack):
                    r, q, use = pack % 2, i * (2 * PACKS) + pack, i * PACKS + pack // 2
                    act.wait_ge(w_here[r], use * 32 + 32)
                    nc.scalar.activation(units[r][:, :], units[r][:, :], ACT.Relu, bias=b1[:, :], scale=w1[:, :]).then_inc(units_ready, 1)
                    act.wait_ge(units_ready, q + 1)
                    act.wait_ge(stacked[r], use * 96 + 96)
                    nc.scalar.activation(high[r][:, :], units[r][:, :], ACT.Copy).then_inc(high_ready, 1)

                def scalars(b, c):
                    act.wait_ge(feat_here[b], (c - b) * (8 * T) + 16 * T)
                    act.wait_ge(ops_free, c + 1)
                    nc.scalar.activation(ops[b][:, :, 0:VU], feat[b][:, :, 0:VU], ACT.Copy).then_inc(ops_copied, 1)

                def turned(b, c):
                    act.wait_ge(turned_ready, c + 1)
                    nc.scalar.activation(ops[b][:, :, JC:JC + VU], ops[b][:, :, 2 * JC + VU:3 * JC], ACT.Copy, scale=-1.0).then_inc(turned_copied, 1)
                    nc.scalar.activation(ops[b][:, :, 2 * JC:2 * JC + VU], ops[b][:, :, JC + VU:2 * JC], ACT.Copy).then_inc(turned_copied, 1)

                def seed_scalars(b, c):
                    act.wait_ge(sum_free, c * SPC + SPC + 2)
                    act.wait_ge(scanned, c * 2 + 1)
                    nc.scalar.activation(seed[:, 0:VU, 1:T1], red[b][:, :, 0:VU].rearrange("p t u -> p u t"), ACT.Copy).then_inc(seeded, 1)

                def flags(c, at):
                    act.wait_ge(scanned, c * 2 + 1)
                    nc.scalar.activation(same_c[:, :, 1:T1], spread_front(k["same"][:, bass.ds(at, T)], D), ACT.Copy).then_inc(flags_ready, 1)

                def store(c, at):
                    act.wait_ge(scanned, c * 2 + 3)
                    act.wait_ge(stored, c * 16 + 16)
                    nc.scalar.activation(out[:, :, :], run[:, :, 1:T1].rearrange("p c t -> p t c"), ACT.Copy).then_inc(run_copied, 1)
                    act.wait_ge(run_copied, c + 2)
                    act.dma_start(a["state2"][0:EDGES_PAD, :].rearrange("(p s) c -> p (s c)", s=SLOTS)[:, bass.ds(at * D, T * D)],
                                  out[:, :, :].rearrange("p t c -> p (t c)")).then_inc(stored, 16)

                act.wait_ge(rows_set, 1)
                act.wait_ge(units_scaled, 1)
                for pack in range(PACKS):
                    hidden(0, pack)
                scalars(0, 0)
                turned(0, 0)

                def body(i, first, last):
                    for b in range(2):
                        c = i * 2 + b
                        at = i * (2 * T) + b * T
                        more = not (last and b == 1)
                        for s in range(SPC):
                            if s == 0:
                                act.wait_ge(red_free, c + 1)
                            act.wait_ge(sum_ready, c * SPC + s + 1)
                            nc.scalar.activation(red[b][:, s * SIX:(s + 1) * SIX, :].rearrange("p t c -> p (t c)"),
                                                 psS[:, (b * SPC + s) % 2, 0:GC], ACT.Copy, scale=scales[:, 2:3]).then_inc(sum_free, 1)
                            if s == 0 and not (first and b == 0):
                                seed_scalars(1 - b, c - 1)
                            if s == 1 and more:
                                scalars(1 - b, c + 1)
                            if s == 5 and not (first and b == 0):
                                store(c - 1, at - T)
                            if s == 5:
                                flags(c, at)
                            if s % 3 == 0 and more:
                                hidden(i, (b + 1) * PACKS + s // 3)
                            if s == 7 and more:
                                turned(1 - b, c + 1)
                pairs_apart(act, body)
                seed_scalars(1, CHUNKS - 1)
                store(CHUNKS - 1, SLOTS - T)
                act.wait_ge(stored, 16 * (CHUNKS + 1))

            @block.vector
            def _(vec):
                v = nc.vector
                for primed, n in ((feat_free, 2), (prod_done, 6), (sum_free, 2), (ops_free, 2),
                                  (red_free, 2), (scanned, 1), (run_copied, 1), (split_done, 2),
                                  (stacked[0], 96), (stacked[1], 96), *((free, 1) for free in stack_free)):
                    vec.sem_inc(primed, n)
                step = chain(vec, vec_done)
                step(v.memset(zrow[:, :], 0.0))
                vec.sem_inc(zrow_set, 1)
                step(v.memset(capped[HID:P, :, :], TOP))
                step(v.memset(ones_row[:, :], 1.0))
                step(v.memset(tops[:, :], 0.0))
                step(v.memset(same_c[:, :, 0:1], 0.0))
                step(v.memset(run[:, :, T:T1], 0.0))
                vec.sem_inc(rows_set, 1)
                vec.wait_ge(w_loaded, 160)
                for x in range(2):
                    block_of = lambda lo, n: raw[:, x, lo:lo + n].rearrange("p (u v) -> p u v", u=VU)
                    r11 = raw[:, x, 192:384].rearrange("p (u v f) -> p u v f", u=VU, f=3)
                    to = new[:, x, :].rearrange("p (u j) -> p u j", j=JC)
                    along, across = to[:, VU:2 * VU, VU:JC], to[:, 2 * VU:3 * VU, VU:JC]
                    for out_, frm, coef in (
                            (to[:, 0:VU, 0:VU], block_of(0, 64), N0 * C0),
                            (to[:, 0:VU, VU:JC], block_of(64, 64), N0 * C1 / sqrt(3.0)),
                            (to[:, VU:2 * VU, 0:VU], block_of(128, 64), N1 * C1 / sqrt(3.0)),
                            (to[:, 2 * VU:3 * VU, 0:VU], r11[:, :, :, 1], N1 * C1 / sqrt(6.0)),
                            (along, r11[:, :, :, 2], N1 * C2 * 2.0 / 3.0),
                            (across, r11[:, :, :, 2], -N1 * C2 / 3.0)):
                        step(v.tensor_scalar(out_, frm, coef, None, ALU.mult), hold=False)
                    step.settle()
                    for out_ in (along, across):
                        step(v.scalar_tensor_tensor(out=out_, in0=r11[:, :, :, 0], scalar=N1 * C0 / sqrt(3.0), in1=out_, op0=ALU.mult, op1=ALU.add))
                def magnitude(to, x):
                    step(v.tensor_reduce(to, x, axis=AX.X, op=ALU.max, apply_absolute_value=True))
                flat_prod = [prod[j][:, :, :].rearrange("p j c -> p (j c)")[:, 0:SLOTS // 2] for j in range(2)]
                magnitude(tops[:, 0:1], flat_prod[0])
                magnitude(tops[:, 1:2], flat_prod[1])
                step(v.tensor_tensor(tops[:, 0:1], tops[:, 0:1], tops[:, 1:2], ALU.max))
                magnitude(tops[:, 1:2], w1[:, :])
                magnitude(tops[:, 2:3], b1[:, :])
                magnitude(tops[:, 3:4], new[:, 1, :])
                vec.sem_inc(tops_ready, 1)
                vec.wait_ge(tops_turned, 1)
                at0 = lambda n: tops0[:, n:n + 1]
                step(v.tensor_reduce(tops0[:, 0:3], psS[0:1, 0, 0:3 * P].rearrange("p (j n) -> p j n", j=3), axis=AX.X, op=ALU.max))
                step(v.tensor_reduce(at0(3), psS[0:1, 0, 3 * P:3 * P + HID], axis=AX.X, op=ALU.max))
                step(v.tensor_copy(at0(4), psS[0:1, 0, 3 * P + HID:3 * P + HID + 1]))

                def power_of_two(x):
                    step(v.tensor_scalar(x, x, 1.0e-12, None, ALU.max))
                    step(v.tensor_scalar(x.bitcast(I32), x.bitcast(I32), 0x7F800000, None, ALU.bitwise_and))
                step(v.tensor_tensor(at0(0), at0(0), at0(1), ALU.mult))
                step(v.tensor_tensor(at0(0), at0(0), at0(2), ALU.add))
                power_of_two(at0(0))
                step(v.reciprocal(at0(5), at0(0)))
                step(v.tensor_tensor(at0(4), at0(4), at0(5), ALU.mult))
                step(v.tensor_tensor(at0(3), at0(3), at0(4), ALU.max))
                power_of_two(at0(3))
                step(v.reciprocal(at0(6), at0(3)))
                step(v.tensor_scalar(scales0[:, 0:1], at0(5), TOP, None, ALU.mult))
                step(v.tensor_scalar(scales0[:, 1:2], at0(6), TOP, None, ALU.mult))
                step(v.tensor_tensor(scales0[:, 2:3], at0(0), at0(3), ALU.mult))
                step(v.tensor_scalar(scales0[:, 2:3], scales0[:, 2:3], 1.0 / (TOP * TOP), None, ALU.mult))
                step(v.tensor_tensor(scales0[:, 3:4], scales0[:, 1:2], at0(5), ALU.mult))
                vec.sem_inc(scales_ready, 1)
                vec.wait_ge(scales_spread, 1)
                step(v.tensor_copy(scales[:, :], psS[:, 1, 0:4]))
                step(v.tensor_scalar(w1[:, :], w1[:, :], scales[:, 0:1], None, ALU.mult))
                step(v.tensor_scalar(b1[:, :], b1[:, :], scales[:, 0:1], None, ALU.mult))
                vec.sem_inc(units_scaled, 1)
                step(v.tensor_scalar(new[:, 0, :], new[:, 0, :], scales[:, 1:2], None, ALU.mult))
                step(v.tensor_copy(whigh[:, :], new[:, 0, :]))
                step(v.tensor_tensor(wlow[0:HID, :], new[0:HID, 0, :], whigh[0:HID, :], ALU.subtract))
                bias, piece = new[HID:P, 1, :], new[HID:P, 0, :]
                step(v.tensor_scalar(bias, bias, scales[HID:P, 3:4], None, ALU.mult))
                step(v.memset(piece, 0.0))
                for j in range(3):
                    step(v.tensor_copy(wlow[HID:P, :], bias))
                    step(v.scalar_tensor_tensor(out=piece, in0=wlow[HID:P, :], scalar=ident[HID:P, HID + j:HID + j + 1], in1=piece, op0=ALU.mult, op1=ALU.add))
                    step(v.tensor_tensor(bias, bias, wlow[HID:P, :], ALU.subtract))
                step(v.tensor_copy(wlow[HID:P, :], piece))
                vec.sem_inc(wrad_ready, 1)

                def split(i, pack):
                    r, q = pack % 2, i * (2 * PACKS) + pack
                    vec.wait_ge(high_ready, q + 1)
                    v.tensor_tensor(low[r][:, :], units[r][:, :], high[r][:, :], ALU.subtract).then_inc(split_done, 1)

                for pack in range(PACKS):
                    split(0, pack)

                def components(step, b, c, n):
                    if n < 3:
                        if n == 0:
                            vec.wait_ge(feat_here[b], (c - b) * (8 * T) + 16 * T)
                            vec.wait_ge(frame_here[b], (c - b) * 8 + 16)
                        step(v.tensor_tensor(parts[:, :, n, :].rearrange("p t (i v) -> p t i v", i=3),
                                             feat[b][:, :, VU:D].rearrange("p t (v i) -> p t i v", i=3),
                                             frame[b][:, :, 3 * n:3 * n + 3].rearrange("p t (i o) -> p t i o", o=1).to_broadcast([P, T, 3, VU]), ALU.mult), hold=False)
                        return
                    step.settle()
                    if n == 3:
                        vec.wait_ge(ops_copied, c + 1)
                        vec.sem_inc(feat_free, 1)
                    term = lambda i: parts[:, :, :, i * VU:(i + 1) * VU]
                    to = ops[b][:, :, :].rearrange("p t (x j) -> p t x j", x=3)[:, :, :, VU:JC]
                    if n == 3:
                        step(v.tensor_tensor(term(0), term(0), term(1), ALU.add), hold=False)
                    else:
                        v.tensor_tensor(to, term(0), term(2), ALU.add).then_inc(turned_ready, 1)

                def products(b, c, s):
                    r, q = (b * SPC + s) % 2, c * SPC + s
                    vec.wait_ge(sum_free, q + 1)
                    if s == 0:
                        vec.wait_ge(turned_ready, c + 1)
                    for half in range(2):
                        g = 2 * s + half
                        ts = slice(g * TRI, (g + 1) * TRI)
                        vec.wait_ge(radial_ready, c * GPC + g + 1)
                        to = prod[r][:, :, :].rearrange("p j (t c) -> p t c j", c=COLS)[:, half * TRI:(half + 1) * TRI, :, :]
                        for lo, n, frm in ((0, 2 * VU, 0), (2 * VU, VU, 256), (3 * VU, VU, 256)):
                            x = max(0, lo // VU - 1)
                            if s == 0 and half == 0 and x == 1:
                                vec.wait_ge(turned_copied, c * 2 + 2)
                            v.tensor_tensor(to[:, :, lo:lo + n, :], psR[:, g % 2, :, frm:frm + n * JC].rearrange("p t (u j) -> p t u j", j=JC),
                                            ops[b][:, ts, x * JC:(x + 1) * JC].rearrange("p t (o j) -> p t o j", o=1).to_broadcast([P, TRI, n, JC]),
                                            ALU.mult).then_inc(prod_done, 1)

                def fold(b, c, s):
                    r, q = (b * SPC + s) % 2, c * SPC + s
                    vec.wait_ge(prod_done, q * 6 + 12)
                    v.tensor_tensor(prod[r][:, 0:FOLDS[s], :], prod[r][:, 0:FOLDS[s], :], prod[r][:, JC // 2:JC // 2 + FOLDS[s], :], ALU.add).then_inc(prod_ready, 1)

                def finish(step, b, c, n):
                    flat = lambda x, lo, hi: x[:, lo:hi, :].rearrange("p c t -> p (c t)")
                    if n < 3:
                        if n == 0:
                            vec.wait_ge(sum_free, c * SPC + SPC + 2)
                        step(v.tensor_tensor(parts[:, :, n, :].rearrange("p t (o u) -> p t o u", o=3),
                                             red[b][:, :, (n + 1) * VU:(n + 2) * VU].rearrange("p t (o u) -> p t o u", o=1).to_broadcast([P, T, 3, VU]),
                                             frame[b][:, :, 3 * n:3 * n + 3].rearrange("p t (i o) -> p t i o", o=1).to_broadcast([P, T, 3, VU]), ALU.mult), hold=False)
                        return
                    step.settle()
                    if n == 3:
                        vec.sem_inc(frame_free, 1)
                        vec.sem_inc(red_free, 1)
                        step(v.tensor_tensor(parts[:, :, 0, :], parts[:, :, 0, :], parts[:, :, 1, :], ALU.add), hold=False)
                    elif n == 4:
                        vec.wait_ge(scanned, c * 2 + 1)
                        step(v.tensor_copy(seed[:, :, 0], run[:, :, T]), hold=False)
                        step(v.tensor_tensor(seed[:, VU:D, 1:T1].rearrange("p (u o) t -> p t o u", o=3),
                                             parts[:, :, 0, :].rearrange("p t (o u) -> p t o u", o=3),
                                             parts[:, :, 2, :].rearrange("p t (o u) -> p t o u", o=3), ALU.add), hold=False)
                    else:
                        if n == 5:
                            vec.wait_ge(seeded, c + 1)
                            vec.wait_ge(flags_ready, c + 1)
                            vec.wait_ge(run_copied, c + 1)
                        lo = (n - 5) * (D // 2)
                        v.tensor_tensor_scan(flat(run, lo, lo + D // 2), flat(same_c, lo, lo + D // 2),
                                             flat(seed, lo, lo + D // 2), 0.0, ALU.mult, ALU.add).then_inc(scanned, 1)

                for n in range(5):
                    components(step, 0, 0, n)
                base, per_chunk = step.count[0], 10
                of_finish = 6
                before = {1: (0, 1), 2: (2,), 3: (3, 4), 4: (5, 6)}
                ahead = {5: (0,), 6: (1, 2), 7: (3,), 8: (4,)}

                def body(i, first, last):
                    step = chain(vec, vec_done, base + i * (2 * per_chunk) - (0 if first else of_finish))
                    for b in range(2):
                        c = i * 2 + b
                        for s in range(SPC):
                            products(b, c, s)
                            if not (first and b == 0):
                                for n in before.get(s, ()):
                                    finish(step, 1 - b, c - 1, n)
                            if not (last and b == 1):
                                for n in ahead.get(s, ()):
                                    components(step, 1 - b, c + 1, n)
                            if s % 3 == 2 and not (last and b == 1):
                                split(i, (b + 1) * PACKS + s // 3)
                            fold(b, c, s)
                        vec.sem_inc(ops_free, 1)
                pairs_apart(vec, body)
                step = chain(vec, vec_done, base + (CHUNKS - 1) * per_chunk)
                for n in range(7):
                    finish(step, 1, CHUNKS - 1, n)
                vec.wait_ge(run_copied, CHUNKS + 1)


def node_sums(nc, a, k):
    with ExitStack() as ctx:
        sb = lambda name, shape, dt=FP32: ctx.enter_context(nc.sbuf_tensor(name, shape, dt))
        pb = lambda name, shape, dt=FP32: ctx.enter_context(nc.psum_tensor(name, shape, dt))
        sem = lambda name: ctx.enter_context(nc.semaphore(name))
        per_turn = BATCH * GROUP
        blocks_of = lambda i: min(per_turn, BLOCKS - i * per_turn)
        tail, rows = sb("tail5", [P, 2, D]), sb("rows5", [D, 2, P])
        totals = sb("totals5", [D, P + 1])
        patch = sb("patch5", [P, D])
        state = sb("state5", [P, BLOCKS, D])
        psA, psB = pb("psA5", [P, 2, P]), pb("psB5", [P, D])
        tail_ready, turned, carry_ready, carry_back, patch_here, patch_ready, patched, x_ready, x_stored, vec_done = (
            sem(n) for n in ("tail_ready5", "turned5", "carry_ready5", "carry_back5", "patch_here5", "patch_ready5",
                             "patched5", "x_ready", "x_stored", "vec_done5"))
        sums_here = [sem(f"sums_here{i}") for i in range(TURNS)]

        with nc.Block() as block:

            @block.sync
            def _(sp):
                for i in range(TURNS):
                    sp.wait_ge(x_ready, i + 1)
                    b0 = i * per_turn
                    sp.dma_start(a["out"].rearrange("(p b) c -> p b c", b=BLOCKS)[:, b0:b0 + blocks_of(i), :],
                                 state[:, b0:b0 + blocks_of(i), :]).then_inc(x_stored, 16)
                sp.wait_ge(x_stored, 16 * TURNS)

            @block.gpsimd
            def _(pool):
                nc.gpsimd.indirect_dma_start(patch[:, :], None, a["state2"], bass.IndirectOffsetOnAxis(
                    ap=k["end_i"][:, :].bitcast(U32), axis=0)).then_inc(patch_here, 16)
                pool.wait_ge(patch_ready, 1)
                nc.gpsimd.indirect_dma_start(a["state2"], bass.IndirectOffsetOnAxis(
                    ap=k["patch_i"][:, :].bitcast(U32), axis=0), patch[:, :], None,
                    bounds_check=EDGES_PAD - 1, oob_is_err=False).then_inc(patched, 16)
                pool.wait_ge(patched, 16)
                for b in range(BLOCKS):
                    nc.gpsimd.indirect_dma_start(state[:, b, :], None, a["state2"], bass.IndirectOffsetOnAxis(
                        ap=k["last_i"][:, b:b + 1].bitcast(U32), axis=0)).then_inc(sums_here[b // per_turn], 16)

            @block.tensor
            def _(pe):
                pe.wait_ge(tail_ready, 1)
                nc.tensor.transpose(psA[0:D, 0, :], tail[:, 0, :], k["ident"][:, :])
                nc.tensor.transpose(psA[0:D, 1, :], tail[:, 1, :], k["ident"][:, :]).then_inc(turned, 1)
                pe.wait_ge(carry_ready, 1)
                nc.tensor.transpose(psB[:, :], totals[:, 0:P], k["ident"][0:D, 0:D]).then_inc(carry_back, 1)

            @block.vector
            def _(vec):
                v = nc.vector
                step = chain(vec, vec_done)
                step(v.tensor_copy(tail[:, 0, :], k["run"][:, :, T]))
                step(v.tensor_copy(tail[:, 1, :], k["whole"][:, :].to_broadcast([P, D])))
                vec.sem_inc(tail_ready, 1)
                vec.wait_ge(turned, 1)
                step(v.tensor_copy(rows[:, :, :], psA[0:D, :, :]))
                step(v.memset(totals[:, 0:1], 0.0))
                step(v.tensor_tensor_scan(totals[:, 1:P + 1], rows[:, 1, :], rows[:, 0, :], 0.0, ALU.mult, ALU.add))
                vec.sem_inc(carry_ready, 1)
                vec.wait_ge(carry_back, 1)
                vec.wait_ge(patch_here, 16)
                step(v.tensor_tensor(patch[:, :], patch[:, :], psB[:, :], ALU.add))
                vec.sem_inc(patch_ready, 1)
                for i in range(TURNS):
                    b0, nb = i * per_turn, blocks_of(i)
                    at = slice(b0, b0 + nb)
                    vec.wait_ge(sums_here[i], 16 * nb)
                    step(v.tensor_tensor(state[:, at, :], state[:, at, :], k["res"][:, at, :], ALU.add))
                    vec.sem_inc(x_ready, 1)


def gnn_kernel(nc, a):
    with ExitStack() as ctx:
        sb = lambda name, shape, dt=FP32: ctx.enter_context(nc.sbuf_tensor(name, shape, dt))
        k = {
            "ident": sb("ident", [P, P]),
            "res": sb("res", [P, BLOCKS, D]),
            "q_first": sb("q_first", [P, D]),
            "last_i": sb("last_i", [P, BLOCKS], I32),
            "whole": sb("whole", [P, 1]),
            "end_i": sb("end_i", [P, 1], I32),
            "patch_i": sb("patch_i", [P, 1], I32),
        }
        prologue(nc, a, k)
        k["same"] = sb("same_all", [P, SLOTS])
        with ExitStack() as states:
            k["peak"] = states.enter_context(nc.sbuf_tensor("peak", [P, HEADS, T + 1], FP32))
            k["sums"] = states.enter_context(nc.sbuf_tensor("sums", [P, SUMS, T + 1], FP32))
            attention(nc, a, k)
            node_attention(nc, a, k)
        k["run"] = sb("run", [P, D, T + 1])
        tensor_product(nc, a, k)
        node_sums(nc, a, k)


def kernel(x, src, dst, edge_attr_3, edge_weight, L0_gnn_Wq, L0_gnn_Wk, L0_gnn_Wv, L0_gnn_Wo,
           L1_gnn_w1, L1_gnn_b1, L1_gnn_w2, L1_gnn_b2):
    import numpy as np
    import concourse.bacc as bacc
    from concourse.bass_utils import run_bass_kernel_spmd

    def padded(array, rows, value=0):
        array = np.asarray(array)
        fill = np.full((rows - array.shape[0],) + array.shape[1:], value, array.dtype)
        return np.ascontiguousarray(np.concatenate([array, fill]))

    dst_pad = padded(dst, EDGES_PAD, NODES)
    weights = padded(edge_weight, EDGES_PAD).reshape(P, SLOTS)
    arrays = {
        "x": padded(x, NODES_PAD),
        "src": padded(src, EDGES_PAD),
        "dst": dst_pad,
        "dst_ext": np.concatenate([np.full(1, -1, dst_pad.dtype), dst_pad]),
        "dst_rows": dst_pad.reshape(-1, ROWW),
        "samples": np.ascontiguousarray(dst_pad[::ROWW].reshape(SP_, SC_)),
        "attr": padded(edge_attr_3, EDGES_PAD, 1),
        "wT": np.ascontiguousarray(weights.T).reshape(-1),
        "wq": np.asarray(L0_gnn_Wq), "wk": np.asarray(L0_gnn_Wk), "wv": np.asarray(L0_gnn_Wv), "wo": np.asarray(L0_gnn_Wo),
        "w1": np.asarray(L1_gnn_w1).reshape(HID, 1), "b1": np.asarray(L1_gnn_b1).reshape(HID, 1),
        "w2": np.asarray(L1_gnn_w2), "b2": np.asarray(L1_gnn_b2).reshape(1, -1),
    }
    nc = bacc.Bacc("TRN2", target_bir_lowering=False, num_devices=1)
    a = {n: nc.dram_tensor(f"in_{n}", v.shape, mybir.dt.from_np(v.dtype), kind="ExternalInput").ap() for n, v in arrays.items()}
    for name, shape in (("kv", (NODES_PAD, 2 * D)), ("q", (NODES_PAD, D)), ("qexp", (EDGES_PAD, D)), ("ptr", (NODES_PAD, 2)),
                        ("state", (EDGES_PAD + 2, STATE)), ("h2", (NODES_PAD, D)), ("frame", (EDGES_PAD, 9)), ("state2", (EDGES_PAD + 1, D))):
        a[name] = nc.dram_tensor(f"scratch_{name}", shape, FP32, kind="Internal").ap()
    a["out"] = nc.dram_tensor("out_x", (NODES_PAD, D), FP32, kind="ExternalOutput").ap()
    gnn_kernel(nc, a)
    result = run_bass_kernel_spmd(nc, [{f"in_{n}": v for n, v in arrays.items()}], core_ids=[0])
    return result.results[0]["out_x"][:NODES]
```
